# Optimizing a Trainium2 kernel written in Bass

```python
import numpy as np
import jax
import jax.numpy as jnp

def _softmax(x, axis=-1):
    return jax.nn.softmax(x, axis=axis)

def _gelu(x):
    return jax.nn.gelu(x, approximate=True)

def _silu(x):
    return jax.nn.silu(x)

def _sigmoid(x):
    return jax.nn.sigmoid(x)

def _layernorm(x, axis=-1, eps=1e-05):
    m = jnp.mean(x, axis=axis, keepdims=True)
    v = jnp.var(x, axis=axis, keepdims=True)
    return (x - m) / jnp.sqrt(v + eps)

def _scatter_add(tgt, idx, src, axis=0):
    return tgt.at[idx].add(src)

def _segment_sum(src, seg, n):
    return jax.ops.segment_sum(src, seg, n)
kernel_name = 'mk_flamingo_gated_d2_seqx_r4_f7f0a2'

def setup_inputs(seed: int=0):
    np.random.seed(seed)
    _w = jnp.asarray

    def _rec_inputs():
        import jax
        import jax.numpy as jnp
        _rk = jax.random.key(seed)
        x = 7.22e-05 + 1 * jax.random.normal(jax.random.fold_in(_rk, 1), (8, 256, 256), jnp.float32)
        _lenS = 256 - jax.random.randint(jax.random.fold_in(_rk, 7), (8,), 0, max(1, 256 // 4) + 1, jnp.int32)
        _lenS2 = 120 - jax.random.randint(jax.random.fold_in(_rk, 8), (8,), 0, max(1, 120 // 4) + 1, jnp.int32)
        _ctx_1024P = jax.random.normal(jax.random.fold_in(_rk, 11), (8, 16, 256), jnp.float32)
        _ctx_1024c = jax.random.dirichlet(jax.random.fold_in(_rk, 511), 0.3 * jnp.ones((16,), jnp.float32), (8, 120))
        _ctx_1024t = jnp.einsum('bsk,bkd->bsd', _ctx_1024c, _ctx_1024P)
        _ctx_1024t = _ctx_1024t * jax.lax.rsqrt(jnp.mean(jnp.square(_ctx_1024t)) + 1e-12) * 0.953939
        ctx_1024 = 4.13588e-05 + 0.999923 * (_ctx_1024t + 0.3 * jax.random.normal(jax.random.fold_in(_rk, 611), (8, 120, 256), jnp.float32))
        _validS = jnp.arange(256)[None, :] < _lenS[:, None]
        _validS2 = jnp.arange(120)[None, :] < _lenS2[:, None]
        _causal = jnp.tril(jnp.ones((256, 256), dtype=bool))
        mask_Bx1x1xS2_ff0 = jnp.where(jnp.ones((8, 1, 1, 120), dtype=bool), 0.0, -1000000000.0).astype(jnp.float32)
        _g = jax.random.normal(jax.random.fold_in(_rk, 9001), (2, 2), jnp.float32)
        _g = jnp.sign(_g) * jnp.maximum(jnp.abs(_g), 1.0) + (_g == 0) * 1.0
        g_xattn = _g[0]
        g_ffn = _g[1]
        return (x, ctx_1024, mask_Bx1x1xS2_ff0, g_xattn, g_ffn)
    x, ctx_1024, mask_Bx1x1xS2_ff0, g_xattn, g_ffn = _rec_inputs()

    def _L0_xattn_setup():
        import jax, jax.numpy as jnp
        import numpy as np
        D_MODEL = 256
        NUM_HEADS = 16
        DEPTH = D_MODEL // NUM_HEADS

        def _split_heads(x):
            B, S, _ = x.shape
            return x.reshape(B, S, NUM_HEADS, DEPTH).transpose(0, 2, 1, 3)
        key = jax.random.key(seed)
        ks = jax.random.split(key, 12)
        B, S = (4, 512)
        scale = 1.0 / np.sqrt(D_MODEL)
        inp = {'query': jax.random.normal(ks[0], (B, S, D_MODEL), dtype=jnp.float32), 'key': jax.random.normal(ks[1], (B, S, D_MODEL), dtype=jnp.float32), 'value': jax.random.normal(ks[2], (B, S, D_MODEL), dtype=jnp.float32), 'mask': jnp.zeros((B, 1, 1, S), dtype=jnp.float32), 'Wq': jax.random.normal(ks[3], (D_MODEL, D_MODEL), dtype=jnp.float32) * scale, 'bq': jnp.zeros((D_MODEL,), dtype=jnp.float32), 'Wk': jax.random.normal(ks[4], (D_MODEL, D_MODEL), dtype=jnp.float32) * scale, 'bk': jnp.zeros((D_MODEL,), dtype=jnp.float32), 'Wv': jax.random.normal(ks[5], (D_MODEL, D_MODEL), dtype=jnp.float32) * scale, 'bv': jnp.zeros((D_MODEL,), dtype=jnp.float32), 'Wo': jax.random.normal(ks[6], (D_MODEL, D_MODEL), dtype=jnp.float32) * scale, 'bo': jnp.zeros((D_MODEL,), dtype=jnp.float32)}
        return inp
    _L0_xattn_all = _L0_xattn_setup()
    _L0_xattn_in = {k: v for k, v in _L0_xattn_all.items() if k in ('Wq', 'bq', 'Wk', 'bk', 'Wv', 'bv', 'Wo', 'bo')}
    del _L0_xattn_all

    def _L0_ffn_setup():
        import jax, jax.numpy as jnp
        import numpy as np
        B, S, D = (4, 512, 256)
        E, K, I = (8, 2, 688)
        key = jax.random.key(seed)
        k0, k1, k2, k3, k4 = jax.random.split(key, 5)
        return {'x': jax.random.normal(k0, (B, S, D), jnp.float32), 'router_w': jax.random.normal(k1, (D, E), jnp.float32) * 0.02, 'w_gate': jax.random.normal(k2, (E, D, I), jnp.float32) * 0.02, 'w_up': jax.random.normal(k3, (E, D, I), jnp.float32) * 0.02, 'w_down': jax.random.normal(k4, (E, I, D), jnp.float32) * 0.02}
    _L0_ffn_all = _L0_ffn_setup()
    _L0_ffn_in = {k: v for k, v in _L0_ffn_all.items() if k in ('router_w', 'w_gate', 'w_up', 'w_down')}
    del _L0_ffn_all

    def _L1_xattn_setup():
        import jax, jax.numpy as jnp
        import numpy as np
        EMBED_DIM = 256
        NUM_HEADS = 16
        HEAD_DIM = EMBED_DIM // NUM_HEADS
        B, NQ, K = (2, 512, 512)
        key = jax.random.key(seed)
        ks = jax.random.split(key, 11)
        s = 1.0 / np.sqrt(EMBED_DIM)
        return {'Q_input': jax.random.normal(ks[0], (B, NQ, EMBED_DIM), jnp.float32), 'K_input': jax.random.normal(ks[1], (B, K, EMBED_DIM), jnp.float32), 'V_input': jax.random.normal(ks[2], (B, K, EMBED_DIM), jnp.float32), 'Wq': jax.random.normal(ks[3], (EMBED_DIM, EMBED_DIM), jnp.float32) * s, 'bq': jnp.zeros((EMBED_DIM,), jnp.float32), 'Wk': jax.random.normal(ks[4], (EMBED_DIM, EMBED_DIM), jnp.float32) * s, 'bk': jnp.zeros((EMBED_DIM,), jnp.float32), 'Wv': jax.random.normal(ks[5], (EMBED_DIM, EMBED_DIM), jnp.float32) * s, 'bv': jnp.zeros((EMBED_DIM,), jnp.float32), 'Wo': jax.random.normal(ks[6], (EMBED_DIM, EMBED_DIM), jnp.float32) * s, 'bo': jnp.zeros((EMBED_DIM,), jnp.float32)}
    _L1_xattn_all = _L1_xattn_setup()
    _L1_xattn_in = {k: v for k, v in _L1_xattn_all.items() if k in ('Wq', 'bq', 'Wk', 'bk', 'Wv', 'bv', 'Wo', 'bo')}
    del _L1_xattn_all

    def _L1_ffn_setup():
        import jax, jax.numpy as jnp
        import numpy as np
        B, T, C = (4, 512, 256)
        NUM_EXPERTS = 8
        TOP_K = 2
        D_EXPERT = 4 * C * TOP_K // NUM_EXPERTS
        key = jax.random.key(seed)
        k0, k1, k2, k3 = jax.random.split(key, 4)
        x = jax.random.normal(k0, (B, T, C), dtype=jnp.float32)
        router_w = jax.random.normal(k1, (NUM_EXPERTS, C), dtype=jnp.float32) * 0.02
        w1_all = jax.random.normal(k2, (NUM_EXPERTS, C, D_EXPERT), dtype=jnp.float32) * 0.02
        w2_all = jax.random.normal(k3, (NUM_EXPERTS, D_EXPERT, C), dtype=jnp.float32) * 0.02
        return {'x': x, 'router_w': router_w, 'w1_all': w1_all, 'w2_all': w2_all}
    _L1_ffn_all = _L1_ffn_setup()
    _L1_ffn_in = {k: v for k, v in _L1_ffn_all.items() if k in ('router_w', 'w1_all', 'w2_all')}
    del _L1_ffn_all
    return {'x': x, 'ctx_1024': ctx_1024, 'mask_Bx1x1xS2_ff0': mask_Bx1x1xS2_ff0, 'g_xattn': g_xattn, 'g_ffn': g_ffn, 'L0_xattn_Wq': _L0_xattn_in['Wq'], 'L0_xattn_bq': _L0_xattn_in['bq'], 'L0_xattn_Wk': _L0_xattn_in['Wk'], 'L0_xattn_bk': _L0_xattn_in['bk'], 'L0_xattn_Wv': _L0_xattn_in['Wv'], 'L0_xattn_bv': _L0_xattn_in['bv'], 'L0_xattn_Wo': _L0_xattn_in['Wo'], 'L0_xattn_bo': _L0_xattn_in['bo'], 'L0_ffn_router_w': _L0_ffn_in['router_w'], 'L0_ffn_w_gate': _L0_ffn_in['w_gate'], 'L0_ffn_w_up': _L0_ffn_in['w_up'], 'L0_ffn_w_down': _L0_ffn_in['w_down'], 'L1_xattn_Wq': _L1_xattn_in['Wq'], 'L1_xattn_bq': _L1_xattn_in['bq'], 'L1_xattn_Wk': _L1_xattn_in['Wk'], 'L1_xattn_bk': _L1_xattn_in['bk'], 'L1_xattn_Wv': _L1_xattn_in['Wv'], 'L1_xattn_bv': _L1_xattn_in['bv'], 'L1_xattn_Wo': _L1_xattn_in['Wo'], 'L1_xattn_bo': _L1_xattn_in['bo'], 'L1_ffn_router_w': _L1_ffn_in['router_w'], 'L1_ffn_w1_all': _L1_ffn_in['w1_all'], 'L1_ffn_w2_all': _L1_ffn_in['w2_all']}

def reference(x, ctx_1024, mask_Bx1x1xS2_ff0, g_xattn, g_ffn, L0_xattn_Wq, L0_xattn_bq, L0_xattn_Wk, L0_xattn_bk, L0_xattn_Wv, L0_xattn_bv, L0_xattn_Wo, L0_xattn_bo, L0_ffn_router_w, L0_ffn_w_gate, L0_ffn_w_up, L0_ffn_w_down, L1_xattn_Wq, L1_xattn_bq, L1_xattn_Wk, L1_xattn_bk, L1_xattn_Wv, L1_xattn_bv, L1_xattn_Wo, L1_xattn_bo, L1_ffn_router_w, L1_ffn_w1_all, L1_ffn_w2_all):
    import jax
    import jax.numpy as jnp

    def _L0_xattn_ref(query, key, value, mask, Wq, bq, Wk, bk, Wv, bv, Wo, bo):
        import jax, jax.numpy as jnp
        import numpy as np
        D_MODEL = 256
        NUM_HEADS = 16
        DEPTH = D_MODEL // NUM_HEADS

        def _split_heads(x):
            B, S, _ = x.shape
            return x.reshape(B, S, NUM_HEADS, DEPTH).transpose(0, 2, 1, 3)
        B, Sq, _ = query.shape
        q = _split_heads(query @ Wq + bq)
        k = _split_heads(key @ Wk + bk)
        v = _split_heads(value @ Wv + bv)
        logits = jnp.einsum('bhqd,bhkd->bhqk', q, k) / jnp.sqrt(jnp.float32(DEPTH))
        logits = logits + mask * -1000000000.0
        attn = jax.nn.softmax(logits, axis=-1)
        ctx = jnp.einsum('bhqk,bhkd->bhqd', attn, v)
        ctx = ctx.transpose(0, 2, 1, 3).reshape(B, Sq, D_MODEL)
        return ctx @ Wo + bo

    def _L0_ffn_ref(x, router_w, w_gate, w_up, w_down):
        import jax, jax.numpy as jnp
        import numpy as np
        B, S, D = (4, 512, 256)
        E, K, I = (8, 2, 688)
        orig_shape = x.shape
        d = orig_shape[-1]
        xf = x.reshape(-1, d)
        T = xf.shape[0]
        n_experts = router_w.shape[1]
        probs = jax.nn.softmax(xf @ router_w, axis=-1)
        w, idx = jax.lax.top_k(probs, K)
        w = w / (jnp.sum(w, axis=-1, keepdims=True) + 1e-06)
        combine = jnp.zeros((T, n_experts), xf.dtype).at[jnp.arange(T)[:, None], idx].add(w)
        out = jnp.zeros_like(xf)
        for e in range(n_experts):
            h = jax.nn.silu(xf @ w_gate[e]) * (xf @ w_up[e])
            out = out + combine[:, e:e + 1] * (h @ w_down[e])
        return out.reshape(orig_shape)

    def _L1_xattn_ref(Q_input, K_input, V_input, Wq, bq, Wk, bk, Wv, bv, Wo, bo):
        import jax, jax.numpy as jnp
        import numpy as np
        EMBED_DIM = 256
        NUM_HEADS = 16
        HEAD_DIM = EMBED_DIM // NUM_HEADS
        B, NQ, K = (2, 512, 512)
        b, n_q, _ = Q_input.shape
        k = K_input.shape[1]
        Q = Q_input @ Wq.T + bq
        Kp = K_input @ Wk.T + bk
        V = V_input @ Wv.T + bv
        Q = Q.reshape(b, n_q, NUM_HEADS, HEAD_DIM).transpose(0, 2, 1, 3)
        Kp = Kp.reshape(b, k, NUM_HEADS, HEAD_DIM).transpose(0, 2, 1, 3)
        V = V.reshape(b, k, NUM_HEADS, HEAD_DIM).transpose(0, 2, 1, 3)
        scores = jnp.einsum('bhqd,bhkd->bhqk', Q, Kp) / jnp.sqrt(jnp.float32(HEAD_DIM))
        weights = jax.nn.softmax(scores, axis=-1)
        attn = jnp.einsum('bhqk,bhkd->bhqd', weights, V)
        attn = attn.transpose(0, 2, 1, 3).reshape(b, n_q, EMBED_DIM)
        return attn @ Wo.T + bo

    def _L1_ffn_ref(x, router_w, w1_all, w2_all):
        import jax, jax.numpy as jnp
        import numpy as np
        B, T, C = (4, 512, 256)
        NUM_EXPERTS = 8
        TOP_K = 2
        D_EXPERT = 4 * C * TOP_K // NUM_EXPERTS
        b, t, c = x.shape
        x_flat = x.reshape(-1, c)
        router_logits = x_flat @ router_w.T
        top_k_logits, top_k_idx = jax.lax.top_k(router_logits, TOP_K)
        router_probs = jax.nn.softmax(top_k_logits, axis=-1)
        hidden = jnp.einsum('nc,ecd->ned', x_flat, w1_all)
        hidden = jnp.square(jax.nn.relu(hidden))
        out_all = jnp.einsum('ned,edc->nec', hidden, w2_all)
        sel = jnp.take_along_axis(out_all, top_k_idx[:, :, None], axis=1)
        out = jnp.sum(sel * router_probs[:, :, None], axis=1)
        return out.reshape(b, t, c)
    x = x + jnp.tanh(g_xattn[0]) * _L0_xattn_ref(_layernorm(x, axis=-1), ctx_1024, ctx_1024, mask_Bx1x1xS2_ff0, L0_xattn_Wq, L0_xattn_bq, L0_xattn_Wk, L0_xattn_bk, L0_xattn_Wv, L0_xattn_bv, L0_xattn_Wo, L0_xattn_bo)
    x = x + jnp.tanh(g_ffn[0]) * _L0_ffn_ref(_layernorm(x, axis=-1), L0_ffn_router_w, L0_ffn_w_gate, L0_ffn_w_up, L0_ffn_w_down)
    x = x + jnp.tanh(g_xattn[1]) * _L1_xattn_ref(_layernorm(x, axis=-1), ctx_1024, ctx_1024, L1_xattn_Wq, L1_xattn_bq, L1_xattn_Wk, L1_xattn_bk, L1_xattn_Wv, L1_xattn_bv, L1_xattn_Wo, L1_xattn_bo)
    x = x + jnp.tanh(g_ffn[1]) * _L1_ffn_ref(_layernorm(x, axis=-1), L1_ffn_router_w, L1_ffn_w1_all, L1_ffn_w2_all)
    return x

_drawn_inputs = setup_inputs


def setup_inputs(seed=0):
    import zlib

    import numpy as np

    out = dict(_drawn_inputs(seed))
    spreads = {'g_ffn': (-1.0, 0.6),
     'L0_xattn_bq': (0.0, 0.1),
     'L0_xattn_bk': (0.0, 0.1),
     'L0_xattn_bv': (0.0, 0.1),
     'L0_xattn_bo': (0.0, 0.1),
     'L1_xattn_bq': (0.0, 0.503),
     'L1_xattn_bk': (0.0, 0.8),
     'L1_xattn_bv': (0.0, 0.1),
     'L1_xattn_bo': (0.0, 0.1)}
    factors = {'L0_ffn_router_w': 6.125,
     'L0_ffn_w_gate': 5.259,
     'L0_ffn_w_up': 5.198,
     'L0_ffn_w_down': 5.203,
     'L1_ffn_router_w': 3.837,
     'L1_ffn_w1_all': 3.745,
     'L1_ffn_w2_all': 3.395}
    for name, (base, spread) in spreads.items():
        noise = np.random.default_rng([zlib.crc32(name.encode()), seed]).standard_normal(out[name].shape)
        drawn = base * np.exp(spread * noise) if base else spread * noise
        out[name] = jnp.asarray(drawn.astype(out[name].dtype))
    for name, factor in factors.items():
        out[name] = (out[name] * factor).astype(out[name].dtype)
    return out
```

```python
from contextlib import ExitStack

import concourse.bass as bass
from concourse import mybir

F32 = mybir.dt.float32
BF16 = mybir.dt.bfloat16
I32 = mybir.dt.int32
U32 = mybir.dt.uint32
ALU = mybir.AluOpType
ACT = mybir.ActivationFunctionType
X = mybir.AxisListType.X

P = 128
NEG = -1000000000.0


def need(eng, sem, value):
    if not isinstance(value, int) or value > 0:
        eng.wait_ge(sem, value)


def apart(eng, passed, *waits):
    for sem, v in waits:
        need(eng, sem, v)
    if any(not isinstance(v, int) for _, v in waits):
        eng.sem_inc(passed, 1)


def flamingo_kernel(nc, x, ctx_rows, mask, g_xattn, g_ffn, attn_w, attn_b, router_w, experts, out):
    NB, S, D = x.shape
    K = ctx_rows.shape[1]
    H = 16
    DH = D // H
    HP = P // DH
    KT = D // P
    NT = NB * S // P
    QT = S // P
    NE = router_w[0].shape[1]
    TOPK = 2
    CH = 4 * K
    HID = [experts[0][0].shape[2], experts[1][0].shape[2]]
    KD = [-(-h // P) for h in HID]
    MAX_BLOCKS = (NT * P * TOPK + NE * (P - 1)) // P
    REGION = NT * P + P
    UPW = [2 * HID[0], HID[1]]
    EW = [KT * UPW[l] + KD[l] * D for l in range(2)]
    U3 = 3
    assert MAX_BLOCKS % U3 == 0 and QT == 2 and KT == 2

    xs_dram = nc.dram_tensor("xs_dram", [NE * REGION, D], F32, kind="Internal").ap()
    ys_dram = nc.dram_tensor("ys_dram", [MAX_BLOCKS * P, D], F32, kind="Internal").ap()

    es = ExitStack()
    with es:
        def sb(name, shape, dt=F32):
            return es.enter_context(nc.sbuf_tensor(name, shape, dt))

        def sem(name):
            return es.enter_context(nc.semaphore(name))

        x_sb = sb("x_sb", [P, NT, D])
        w_all = sb("w_all", [P, NE * EW[0]])
        w_att = sb("w_att", [P, 4, KT, D])
        wr = sb("wr", [P, 2, KT, NE])
        bq = sb("bq", [P, 2, KT])
        bq4 = sb("bq4", [P, 2, KT])
        bk = sb("bk", [P, 2, KT])
        bv = sb("bv", [P, 2, D])
        bo = sb("bo", [P, 2, D])
        gates = sb("gates", [P, 4])
        tg = sb("tg", [P, 4])
        maskgath = sb("maskgath", [P, 1024])
        mask_bc = maskgath[:, 0:NB * K].rearrange("p (b k) -> p b k", b=NB)
        yg = maskgath[:, :].rearrange("p (t k d) -> p t k d", t=2, k=2)
        ctx_sb = sb("ctx_sb", [P, D])
        ctxT = sb("ctxT", [P, KT, K])
        kT = sb("kT", [P, KT, K])
        v_tmp = sb("v_tmp", [P, D])
        v_pad = sb("v_pad", [P, H, 2 * DH])
        xn1 = sb("xn1", [P, QT, D])
        xn1T = sb("xn1T", [P, KT, S])
        qT = sb("qT", [P, KT, S])
        pT = sb("pT", [P, 2, 4 * P])
        cT = sb("cT", [P, KT, P])
        xn2 = sb("xn2", [P, QT, D])
        share = sb("share", [P, 3968])
        s_sb = share[:, 0:2 * HP * K].rearrange("p (h n) -> p h n", h=2)
        kbd = share[:, 2 * HP * K:4 * HP * K].rearrange("p (m h k) -> p m h k", m=2, h=HP)
        xg = share[:, 0:768].rearrange("p (u d) -> p u d", u=U3)
        xgT = share[:, 768:1024].rearrange("p (k n) -> p k n", k=KT)
        act_sb = share[:, 1024:1712]
        h_sb = share[:, 1712:2400]
        hT = share[:, 2400:3168].rearrange("p (c n) -> p c n", c=6)
        y_sb = share[:, 3168:3936].rearrange("p (u d) -> p u d", u=U3)
        p_buf = w_all[:, (NE - 1) * EW[0]:(NE - 1) * EW[0] + 2 * H * K].rearrange("p (q n) -> p q n", q=2)
        spare = (NE - 1) * EW[0] + 2 * H * K
        xn2T = w_all[:, spare:spare + D].rearrange("p (k n) -> p k n", k=KT)
        assert 2 * H * K + D <= EW[0]
        mx = sb("mx", [P, 2, HP])
        rsum = sb("rsum", [P, QT, H])
        rinv = sb("rinv", [P, QT, H])
        st1 = sb("st1", [P, QT, 6])
        mv1 = sb("mv1", [P, QT, 2])
        ve1 = sb("ve1", [P, QT])
        rstd1 = sb("rstd1", [P, QT])
        st2 = sb("st2", [P, QT, 6])
        mv2 = sb("mv2", [P, QT, 2])
        ve2 = sb("ve2", [P, QT])
        rstd2 = sb("rstd2", [P, QT])
        top8 = sb("top8", [P, NT, 8])
        logits = sb("logits", [P, 2, NE])
        topnow = sb("topnow", [P, 2, 8])
        idx8 = sb("idx8", [P, 2, 8], U32)
        idxf = sb("idxf", [P, 2, TOPK])
        onehot = sb("onehot", [P, NT, TOPK, NE])
        maskb = sb("maskb", [P, 2, NE], BF16)
        cumb = sb("cumb", [P, NE], BF16)
        rk = sb("rk", [P, 2, NE])
        prod = sb("prod", [P, 2, TOPK, NE])
        slotf = sb("slotf", [P, NT, TOPK])
        slot_now = sb("slot_now", [P, 2, TOPK], I32)
        cnt = sb("cnt", [P, NE])
        pad_i = sb("pad_i", [P, NE], I32)
        cmpb = pT[:, :, :].rearrange("p a b -> p (a b)")[:, 0:MAX_BLOCKS * NE]
        nb = sb("nb", [P, NE])
        sbk = sb("sbk", [P, NE])
        tot1 = sb("tot1", [P, 1])
        jc = sb("jc", [P, MAX_BLOCKS])
        be = sb("be", [P, MAX_BLOCKS])
        sbx = sb("sbx", [P, MAX_BLOCKS])
        xrow_i = sb("xrow_i", [P, MAX_BLOCKS], I32)
        woff_i = sb("woff_i", [P, MAX_BLOCKS], I32)
        yoff = sb("yoff", [P, NE])
        yslot = sb("yslot", [P, NT, TOPK])
        ynow = sb("ynow", [P, 2, TOPK], I32)
        zsum = sb("zsum", [P, NT])
        wcomb = sb("wcomb", [P, NT, TOPK])
        ident = sb("ident", [P, P])
        hmask = sb("hmask", [P, HP])
        tri = sb("tri", [P, P], BF16)
        ones = sb("ones", [P, P], BF16)
        iota8 = sb("iota8", [P, NE])
        eR = sb("eR", [P, NE])
        padbase = sb("padbase", [P, NE])
        thr = sb("thr", [P, NT])
        jrow = sb("jrow", [P, MAX_BLOCKS])
        lower = sb("lower", [P, NE, NE])
        mhalf = sb("mhalf", [P, QT])
        zrow = sb("zrow", [P, D])
        ps = es.enter_context(nc.psum_tensor("ps", [P, 8, 512], F32))

        L_x = [sem(f"x_loaded{i}") for i in range(4)]
        L_w = sem("attn_w_loaded")
        L_small = sem("small_loaded")
        L_ctx = sem("ctx_loaded")
        L_exp = sem("experts_loaded")
        L_xg = [sem(f"block_loaded{u}") for u in range(U3)]
        D_y = [sem(f"block_stored{u}") for u in range(U3)]
        D_sc = sem("tokens_scattered")
        D_pad = sem("pads_scattered")
        D_ga = sem("results_gathered")
        D_out = [sem(f"out_stored{i}") for i in range(2)]
        C_g = sem("consts_pool")
        C_v = sem("consts_vector")
        C_a = sem("gates_ready")
        p_k, p_xnT, p_q, p_v, p_ctx = (sem(n) for n in ("k_psum", "xn1T_psum", "q_psum", "v_psum", "ctxT_psum"))
        p_s, p_t, p_pv, p_o = (sem(n) for n in ("scores_psum", "probsT_psum", "ctx_chunk_psum", "o_psum"))
        p_x2, p_lg, p_rk = (sem(n) for n in ("xn2T_psum", "logits_psum", "rank_psum"))
        a_k, a_xnT, a_q, a_ctx = (sem(n) for n in ("k_sb_ready", "xn1T_ready", "q_ready", "ctxT_ready"))
        a_t, a_exp, a_c, a_x2, a_lg = (sem(n) for n in ("probsT_ready", "exp_ready", "cT_ready", "xn2T_ready", "logits_ready"))
        d_v, d_add, d_max, d_sub, d_sum, d_ri = (sem(n) for n in ("v_ready", "masked_ready", "max_ready", "shifted_ready", "sum_ready", "rinv_ready"))
        d_o, d_res, d_st2, d_mv2, d_xn2 = (sem(n) for n in ("o_read", "residual_ready", "stats2_ready", "meanvar2_ready", "xn2_ready"))
        d_st1, d_mv1, d_xn1 = (sem(n) for n in ("stats1_ready", "meanvar1_ready", "xn1_ready"))
        d_r1, d_mask, d_rk, d_slot, d_cum = (sem(n) for n in ("route_step", "mask_ready", "rank_read", "slots_ready", "cum_ready"))
        d_r2 = sem("route2_step")
        d_keep = sem("batch_kept")
        d_f = sem("final_route_step")
        d_tm = sem("top_max_ready")
        d_comb, d_c1, d_yn = (sem(n) for n in ("combined", "combine_step", "gather_index_ready"))
        g_kbd, g_norm, g_ve2, g_rs2, g_ve1, g_rs1, g_vp = (sem(n) for n in (
            "kbd_ready", "probs_ready", "vareps2", "rstd2_ready", "vareps1", "rstd1_ready", "vpad_ready"))
        f_cnt = sem("count_psum")
        f_exp = sem("top_exp_ready")
        b_x, b_up, b_h, b_hT, b_y = (sem(n) for n in ("blkT_psum", "up_psum", "h_used", "hT_psum", "y_psum"))
        e_x, e_act, e_hT, e_hTv, e_y, e_h = (sem(n) for n in ("blkT_ready", "act_ready", "hT_ready_a", "hT_ready_v", "y_ready", "h_ready"))
        g_passed, d_passed = sem("pool_passed"), sem("vector_passed")

        block = es.enter_context(nc.Block())

        NSMALL = 2 * 5 + 3

        def run_steps(eng, l, step):
            step(-1, False, True, True, False)
            step(0, True, True, True, False)
            step(1, True, True, True, True)
            with eng.Fori(2, NB - 2) as b:
                step(b, True, True, True, True)
            step(NB - 2, True, True, False, True)
            step(NB - 1, True, False, False, True)
            step(NB, False, False, False, True)

        def run_blocks(eng, l, step):
            for j in range(U3 + 1):
                step(j, j % U3, (j - 1) // U3, j == 0, False)
            with eng.Fori(1, (MAX_BLOCKS - U3) // U3) as i:
                for u in range(U3):
                    step(U3 * i + (1 + u), (1 + u) % U3, i, False, False)
            for j in (MAX_BLOCKS - 2, MAX_BLOCKS - 1):
                step(j, j % U3, (j - 1) // U3, False, j == MAX_BLOCKS - 1)

        UP = [[(0, 0, 344), (1, HID[0], 344), (2, 344, 344), (3, HID[0] + 344, 344)], [(0, 0, HID[1])]]
        DOWN = [[(c, min(P, HID[l] - c * P)) for c in range(KD[l])] for l in range(2)]

        @block.sync
        def _(sp):
            xv = x.rearrange("b (t p) d -> p (b t) d", p=P)

            def load_ctx(l, b):
                sp.dma_start(ctx_sb[0:K, :], ctx_rows[b % NB if isinstance(b, int) else b, :, :]).then_inc(L_ctx, 16)

            def load_att(l):
                for i in (1, 0, 2, 3):
                    sp.dma_start(w_att[:, i, :, :], attn_w[l][i].rearrange("(k p) n -> p k n", p=P)).then_inc(L_w, 16)

            sp.dma_start(x_sb[:, 0:2, :], xv[:, 0:2, :]).then_inc(L_x[0], 16)
            sp.dma_start(ctx_sb[0:K, :], ctx_rows[0, :, :]).then_inc(L_ctx, 16)
            load_att(0)
            for l in range(2):
                q_b, k_b, v_b, o_b = attn_b[l]
                sp.dma_start(bq[:, l, :], q_b).then_inc(L_small, 16)
                sp.dma_start(bk[:, l, :], k_b).then_inc(L_small, 16)
                sp.dma_start(bv[:, l, :], v_b.unsqueeze(0).to_broadcast([P, D])).then_inc(L_small, 16)
                sp.dma_start(bo[:, l, :], o_b.unsqueeze(0).to_broadcast([P, D])).then_inc(L_small, 16)
                sp.dma_start(wr[:, l, :, :], router_w[l].rearrange("(k p) n -> p k n", p=P)).then_inc(L_small, 16)
            sp.dma_start(mask_bc, mask.unsqueeze(0).to_broadcast([P, NB, K])).then_inc(L_small, 16)
            sp.dma_start(gates[:, 0:2], g_xattn.unsqueeze(0).to_broadcast([P, 2])).then_inc(L_small, 16)
            sp.dma_start(gates[:, 2:4], g_ffn.unsqueeze(0).to_broadcast([P, 2])).then_inc(L_small, 16)
            for i, (a, z) in enumerate(((2, 4), (4, 8), (8, 16))):
                sp.dma_start(x_sb[:, a:z, :], xv[:, a:z, :]).then_inc(L_x[i + 1], 16)

            for l in range(2):
                with sp.Fori(1, NB) as b:
                    sp.wait_ge(p_ctx, NB * l + b)
                    sp.dma_start(ctx_sb[0:K, :], ctx_rows[bass.ds(b, 1), :, :].rearrange("b k d -> (b k) d")).then_inc(L_ctx, 16)
                sp.wait_ge(p_ctx, NB * (l + 1))
                if l == 0:
                    sp.dma_start(ctx_sb[0:K, :], ctx_rows[0, :, :]).then_inc(L_ctx, 16)
                    sp.wait_ge(p_o, NT)
                    load_att(1)
                sp.wait_ge(D_sc, 16 * TOPK * NT * (l + 1))
                sp.wait_ge(D_pad, 16 * NE * (l + 1))
                sp.wait_ge(d_f, 16 + 22 * l)

                def load_block(j, u):
                    J = MAX_BLOCKS * l + j
                    if not (isinstance(j, int) and j < U3):
                        sp.wait_ge(b_x, J - U3 + 1)
                    row = sp.value_load(xrow_i[0:1, bass.ds(j, 1)], min_val=0, max_val=NE * REGION - P)
                    sp.dma_start(xg[:, u, :], xs_dram[bass.ds(row, P), :]).then_inc(L_xg[u], 16)

                def store_block(j, u):
                    J = MAX_BLOCKS * l + j
                    sp.wait_ge(e_y, J + 1)
                    sp.dma_start(ys_dram[bass.ds(j * P, P), :], y_sb[:, u, :]).then_inc(D_y[u], 16)

                for j in range(U3):
                    load_block(j, j)
                with sp.Fori(1, MAX_BLOCKS // U3) as i:
                    for u in range(U3):
                        load_block(U3 * i + u, u)
                        store_block(U3 * i + (u - U3), u)
                for j in range(MAX_BLOCKS - U3, MAX_BLOCKS):
                    store_block(j, j % U3)
            ov = out.rearrange("b (t p) d -> p b t d", p=P)
            for b in range(NB):
                sp.wait_ge(d_comb, NT + 2 * (b + 1))
                sp.dma_start(ov[:, b, :, :], x_sb[:, 2 * b:2 * b + 2, :]).then_inc(D_out[b % 2], 16)
            sp.wait_ge(D_out[0], 16 * NB // 2)
            sp.wait_ge(D_out[1], 16 * NB // 2)

        @block.gpsimd
        def _(g):
            g.memset(ident[:], 0.0).then_inc(C_g, 1)
            g.memset(hmask[:], 1.0).then_inc(C_g, 1)
            g.memset(tri[:], 1.0).then_inc(C_g, 1)
            g.memset(ones[:], 1.0).then_inc(C_g, 1)
            g.memset(lower[:], 1.0).then_inc(C_g, 1)
            g.memset(mhalf[:], -0.5).then_inc(C_g, 1)
            g.wait_ge(C_g, 6)
            g.affine_select(out=ident[:], in_=ident[:], compare_op=ALU.not_equal, fill=1.0, base=0,
                            pattern=[[-1, P]], channel_multiplier=1).then_inc(C_g, 1)
            g.affine_select(out=hmask[:], in_=hmask[:], compare_op=ALU.is_ge, fill=0.0, base=0,
                            pattern=[[-DH, HP]], channel_multiplier=1).then_inc(C_g, 1)
            g.wait_ge(C_g, 8)
            g.affine_select(out=hmask[:], in_=hmask[:], compare_op=ALU.is_ge, fill=0.0, base=DH - 1,
                            pattern=[[DH, HP]], channel_multiplier=-1).then_inc(C_g, 1)
            g.affine_select(out=tri[:], in_=tri[:], compare_op=ALU.is_ge, fill=0.0, base=-1,
                            pattern=[[1, P]], channel_multiplier=-1).then_inc(C_g, 1)
            g.affine_select(out=lower[:], in_=lower[:], compare_op=ALU.is_ge, fill=0.0, base=-1,
                            pattern=[[1, NE], [-1, NE]], channel_multiplier=0).then_inc(C_g, 1)

            def ramp(t, n, step, base, per):
                return g.iota(t, pattern=[[step, n]], base=base, channel_multiplier=per,
                              allow_small_or_imprecise_dtypes=True)
            ramp(iota8[:], NE, 1, 0, 0)
            ramp(eR[:], NE, REGION, 0, 0)
            ramp(padbase[:], NE, REGION, 0, 1)
            ramp(thr[:], NT, P, 0, 0).then_inc(C_g, 1)
            ramp(jrow[:], MAX_BLOCKS, 1, 0, 0).then_inc(C_g, 1)
            g.memset(zrow[:], 0.0).then_inc(C_g, 1)
            g.memset(v_pad[:], 0.0).then_inc(C_g, 1)

            def rstd(mv, ve, out_, ready, s_ve, v_ve, s_out):
                g.tensor_scalar(ve, mv, 1e-5, None, ALU.add).then_inc(s_ve, 1)
                g.wait_ge(s_ve, v_ve)
                g.tensor_tensor(out_, ve, ready, ALU.pow).then_inc(s_out, 1)

            for l in range(2):
                def ln1_rstd(B):
                    apart(g, g_passed, (d_mv1, 2 * B + 2))
                    rstd(mv1[:, :, 1], ve1[:], rstd1[:], mhalf[:], g_ve1, B + 1, g_rs1)

                def gather(B):
                    apart(g, g_passed, (d_yn, B + 1))
                    for t in range(2):
                        for k in range(TOPK):
                            g.indirect_dma_start(yg[:, t, k, :], None, ys_dram,
                                                 bass.IndirectOffsetOnAxis(ap=ynow[:, t, k:k + 1], axis=0)
                                                 ).then_inc(D_ga, 16)

                def norm(U, qt, h):
                    g.wait_ge(d_ri, 2 * U + h + 1)
                    pv = p_buf[:, qt, h * HP * K:(h + 1) * HP * K].rearrange("p (h k) -> p h k", h=HP)
                    g.tensor_tensor(pv, pv, rinv[:, qt, h * HP:(h + 1) * HP].unsqueeze(2).to_broadcast([P, HP, K]),
                                    ALU.mult).then_inc(g_norm, 1)

                def ln2_rstd(U, qt):
                    apart(g, g_passed, (d_mv2, U + 1))
                    rstd(mv2[:, qt, 1:2], ve2[:, qt:qt + 1], rstd2[:, qt:qt + 1], mhalf[:, 0:1], g_ve2, U + 1, g_rs2)

                if l == 1:
                    for u in range(U3):
                        g.wait_ge(D_y[u], 16 * MAX_BLOCKS // U3)
                    gather(0)
                ln1_rstd(NB * l)

                def step(b, cur, nxt, nn, prev):
                    B = NB * l + b
                    if nxt:
                        g.wait_ge(a_k, B + 2)
                        if cur:
                            g.wait_ge(p_s, 4 * B + 4)
                        g.tensor_tensor(kbd, kT[:, :, :].unsqueeze(2).to_broadcast([P, KT, HP, K]),
                                        hmask[:, :].unsqueeze(1).unsqueeze(3).to_broadcast([P, KT, HP, K]),
                                        ALU.mult).then_inc(g_kbd, 1)
                    if cur:
                        norm(2 * B + 1, 1, 1)
                        ln2_rstd(2 * B, 0)
                    if nn and l == 1:
                        gather(b + 2)
                    if nxt:
                        norm(2 * B + 2, 0, 0)
                    if prev:
                        apart(g, g_passed, (d_slot, B))
                        for t in range(2):
                            for k in range(TOPK):
                                g.indirect_dma_start(xs_dram, bass.IndirectOffsetOnAxis(ap=slot_now[:, t, k:k + 1], axis=0),
                                                     xn1[:, t, :], None).then_inc(D_sc, 16)
                    if nxt:
                        norm(2 * B + 2, 0, 1)
                    if cur:
                        ln2_rstd(2 * B + 1, 1)
                    if nxt:
                        apart(g, g_passed, (d_v, B + 2), (p_pv, 8 * B + 8 if cur else 0))
                        for s in range(2):
                            i = g.tensor_copy(v_pad[0:K, s::2, s * DH:(s + 1) * DH],
                                              v_tmp[0:K, :].rearrange("p (g s d) -> p s g d", s=2, d=DH)[:, s, :, :])
                        i.then_inc(g_vp, 1)
                        norm(2 * B + 3, 1, 0)
                    if nn:
                        ln1_rstd(B + 2)
                run_steps(g, l, step)
                g.wait_ge(d_f, 2 + 22 * l)
                for e in range(NE):
                    g.indirect_dma_start(xs_dram, bass.IndirectOffsetOnAxis(ap=pad_i[:, e:e + 1], axis=0),
                                         zrow[:, :], None).then_inc(D_pad, 16)

            for u in range(U3):
                g.wait_ge(D_y[u], 2 * 16 * MAX_BLOCKS // U3)
            with g.Fori(0, NB) as b:
                apart(g, g_passed, (d_yn, b + (NB + 1)))
                for t in range(2):
                    for k in range(TOPK):
                        g.indirect_dma_start(yg[:, t, k, :], None, ys_dram,
                                             bass.IndirectOffsetOnAxis(ap=ynow[:, t, k:k + 1], axis=0)
                                             ).then_inc(D_ga, 16)

        @block.scalar
        def _(a):
            def load_experts(l, es_):
                base = [w_all[:, e * EW[l]:(e + 1) * EW[l]] for e in range(NE)]
                for e in es_:
                    ups, down = experts[l][:-1], experts[l][-1]
                    for i, w in enumerate(ups):
                        dst = base[e][:, 0:KT * UPW[l]].rearrange("p (k n) -> p k n", k=KT)
                        a.dma_start(dst[:, :, i * HID[l]:(i + 1) * HID[l]],
                                    w[e, :, :].rearrange("(k p) n -> p k n", p=P)).then_inc(L_exp, 16)
                    full = HID[l] // P
                    dst = base[e][:, KT * UPW[l]:].rearrange("p (c n) -> p c n", c=KD[l])
                    a.dma_start(dst[:, 0:full, :],
                                down[e, 0:full * P, :].rearrange("(c p) n -> p c n", p=P)).then_inc(L_exp, 16)
                    if HID[l] % P:
                        a.dma_start(dst[0:HID[l] % P, full, :], down[e, full * P:, :]).then_inc(L_exp, 16)

            load_experts(0, range(NE - 1))
            a.wait_ge(L_small, 16 * NSMALL)
            a.activation(tg[:, :], gates[:, :], ACT.Tanh).then_inc(C_a, 1)
            a.mul(bq4[:, :, :], bq[:, :, :], 0.25).then_inc(C_a, 1)
            a.wait_ge(C_a, 2)

            for l in range(2):
                def ctx_evac(B):
                    a.wait_ge(p_ctx, B + 1)
                    if not (isinstance(B, int) and B == 0):
                        a.wait_ge(p_v, B)
                    a.copy(ctxT[:, :, :], ps[:, 7, 0:KT * K].rearrange("p (k n) -> p k n", k=KT)).then_inc(a_ctx, 1)

                def t_evac(U, c):
                    a.wait_ge(p_t, 4 * U + c + 1)
                    need(a, p_pv, 4 * U + c - 1)
                    a.copy(pT[0:K, c % 2, :], ps[0:K, 4 + c % 2, :]).then_inc(a_t, 1)

                def exp(U, qt, h):
                    a.wait_ge(d_sub, 2 * U + h + 1)
                    need(a, p_t, 4 * U - 4)
                    a.activation(p_buf[:, qt, h * HP * K:(h + 1) * HP * K], s_sb[:, h, :], ACT.Exp).then_inc(a_exp, 1)

                def x2_evac(U):
                    a.wait_ge(p_x2, U + 1)
                    need(a, p_lg, U)
                    a.copy(xn2T[:, :, :], ps[:, 7, 0:KT * P].rearrange("p (k n) -> p k n", k=KT)).then_inc(a_x2, 1)

                def lg_evac(U, B, qt):
                    a.wait_ge(p_lg, U + 1)
                    need(a, d_mask, B)
                    a.copy(logits[:, qt, :], ps[:, 7, 0:NE]).then_inc(a_lg, 1)

                def c_evac(U):
                    a.wait_ge(p_pv, 4 * U + 4)
                    need(a, p_o, U)
                    a.copy(cT[:, :, :], ps[:, 6, 0:KT * P].rearrange("p (k n) -> p k n", k=KT)).then_inc(a_c, 1)

                ctx_evac(NB * l)

                def step(b, cur, nxt, nn, prev):
                    B = NB * l + b
                    U = 2 * B
                    if cur:
                        t_evac(U, 0)
                        t_evac(U, 1)
                    if nxt:
                        a.wait_ge(p_k, B + 2)
                        need(a, g_kbd, B + 1)
                        for m in range(KT):
                            i = a.activation(kT[:, m, :], ps[:, 7, m * K:(m + 1) * K], ACT.Identity, bias=bk[:, l, m:m + 1])
                        i.then_inc(a_k, 1)
                    if cur:
                        t_evac(U, 2)
                    if nxt:
                        a.wait_ge(p_xnT, B + 2)
                        need(a, p_q, B + 1)
                        a.copy(xn1T[:, :, :], ps[:, 7, :].rearrange("p (k n) -> p k n", k=KT)).then_inc(a_xnT, 1)
                    if cur:
                        t_evac(U, 3)
                    if nxt:
                        a.wait_ge(p_q, B + 2)
                        need(a, p_s, 4 * B + 4)
                        for m in range(KT):
                            i = a.activation(qT[:, m, :], ps[:, 7, m * S:(m + 1) * S], ACT.Identity,
                                             bias=bq4[:, l, m:m + 1], scale=0.25)
                        i.then_inc(a_q, 1)
                    if cur:
                        exp(U + 1, 1, 1)
                        c_evac(U)
                    if prev:
                        x2_evac(U - 1)
                        lg_evac(U - 1, B - 1, 1)
                    if nxt:
                        exp(U + 2, 0, 0)
                    if cur:
                        t_evac(U + 1, 0)
                        t_evac(U + 1, 1)
                    if nxt:
                        exp(U + 2, 0, 1)
                    if cur:
                        t_evac(U + 1, 2)
                        x2_evac(U)
                        t_evac(U + 1, 3)
                        lg_evac(U, B, 0)
                        c_evac(U + 1)
                    if nxt:
                        exp(U + 3, 1, 0)
                    if nn:
                        ctx_evac(B + 2)
                run_steps(a, l, step)

                if l == 0:
                    load_experts(0, [NE - 1])
                a.wait_ge(d_f, 17 + 22 * l)
                a.activation(top8[:, :, :], top8[:, :, :], ACT.Exp).then_inc(f_exp, 1)

                def blk(j, u, i, first, last):
                    J = MAX_BLOCKS * l + j
                    nq = len(UP[l]) // 2 or 1
                    if l == 0:
                        for q in range(2):
                            a.wait_ge(b_up, 4 * j + 2 * q + 1)
                            need(a, e_h, 2 * j - 1 + q)
                            a.activation(act_sb[:, 344 * q:344 * q + 344], ps[:, 2 * q, 0:344], ACT.Silu).then_inc(e_act, 1)
                    else:
                        a.wait_ge(b_up, 4 * MAX_BLOCKS + j + 1)
                        a.wait_ge(e_h, 2 * MAX_BLOCKS + j)
                        a.activation(act_sb[:, 0:HID[1]], ps[:, 0, 0:HID[1]], ACT.Relu).then_inc(e_act, 1)
                    a.wait_ge(b_hT, 2 * j + 1 if l == 0 else 2 * MAX_BLOCKS + j + 1)
                    need(a, b_y, J)
                    n = min(4, KD[l])
                    a.copy(hT[:, 0:n, :], ps[:, 4, 0:n * P].rearrange("p (c n) -> p c n", c=n)).then_inc(e_hT, 1)
                run_blocks(a, l, blk)
                if l == 0:
                    a.wait_ge(b_y, MAX_BLOCKS)
                    load_experts(1, range(NE))

        @block.vector
        def _(v):
            v.memset(cumb[:], 0.0).then_inc(C_v, 1)
            v.wait_ge(L_small, 16 * NSMALL)
            v.tensor_scalar(mask_bc, mask_bc, NEG, None, ALU.mult).then_inc(C_v, 1)
            v.wait_ge(C_a, 2)
            for l in range(2):
                v.tensor_scalar(bo[:, l, :], bo[:, l, :], tg[:, l:l + 1], None, ALU.mult).then_inc(C_v, 1)
            v.wait_ge(C_v, 4)
            v.wait_ge(C_g, 15)

            for l in range(2):
                F = 22 * l

                def ln1_stats(B, b, loaded=None):
                    if loaded is not None:
                        v.wait_ge(loaded, 16)
                    for t in range(2):
                        v.bn_stats(st1[:, t, :], x_sb[:, 2 * b + t, :] if isinstance(b, int) else
                                   x_sb[:, bass.ds(2 * b + t, 1), :]).then_inc(d_st1, 1)
                    for t in range(2):
                        apart(v, d_passed, (d_st1, 2 * B + t + 1))
                        v.bn_aggr(mv1[:, t, :], st1[:, t, :]).then_inc(d_mv1, 1)

                def ln1_apply(B, b):
                    v.wait_ge(g_rs1, B + 1)
                    v.wait_ge(d_mv1, 2 * B + 2)
                    need(v, p_xnT, B)
                    need(v, D_sc, 64 * (B - 2))
                    for t in range(2):
                        i = v.tensor_scalar(xn1[:, t:t + 1, :], x_sb[:, bass.ds(2 * b + t, 1), :], mv1[:, t, 0:1],
                                            rstd1[:, t:t + 1], ALU.subtract, ALU.mult)
                    i.then_inc(d_xn1, 1)

                def combine(B, b):
                    v.wait_ge(D_ga, 64 * (B + 1))
                    for k in range(TOPK):
                        for t in range(2):
                            if k:
                                v.wait_ge(d_c1, 2 * B + t + 1)
                            xt = x_sb[:, bass.ds(2 * b + t, 1), :]
                            v.scalar_tensor_tensor(
                                out=xt, in0=yg[:, t, k:k + 1, :], scalar=wcomb[:, bass.ds(2 * b + t, 1), k:k + 1].rearrange("p a b -> p (a b)"),
                                in1=xt, op0=ALU.mult, op1=ALU.add).then_inc(d_comb if k else d_c1, 1)

                def next_index(B, b):
                    apart(v, d_passed, (D_ga, 64 * B))
                    v.tensor_copy(ynow[:, :, :], yslot[:, bass.ds(2 * b, 2), :]).then_inc(d_yn, 1)

                def softmax_a(U, b, h):
                    v.wait_ge(p_s, 2 * U + h + 1)
                    sps = ps[:, 2 * h:2 * h + 2, 0:CH].rearrange("p c (h k) -> p c h k", h=4)
                    s4 = s_sb[:, h, :].rearrange("p (c h k) -> p c h k", c=2, h=4)
                    s3 = s_sb[:, h, :].rearrange("p (h k) -> p h k", h=HP)
                    m4 = mx[:, h, :].rearrange("p (c h) -> p c h", c=2)
                    need(v, a_exp, 2 * U + h - 1)
                    if l == 0:
                        mb = mask_bc[:, bass.ds(b, 1), :].unsqueeze(2).to_broadcast([P, 1, 4, K])
                        for c in range(2):
                            i = v.tensor_tensor(s4[:, c:c + 1, :, :], sps[:, c:c + 1, :, :], mb, ALU.add)
                        i.then_inc(d_add, 1)
                        v.wait_ge(d_add, 2 * U + h + 1)
                        v.tensor_reduce(mx[:, h, :], s3, X, ALU.max).then_inc(d_max, 1)
                        v.wait_ge(d_max, 2 * U + h + 1)
                        v.tensor_tensor(s3, s3, mx[:, h, :].unsqueeze(2).to_broadcast([P, HP, K]),
                                        ALU.subtract).then_inc(d_sub, 1)
                    else:
                        v.tensor_reduce(m4, sps, X, ALU.max).then_inc(d_max, 1)
                        v.wait_ge(d_max, 2 * U + h + 1)
                        v.tensor_tensor(s4, sps, m4.unsqueeze(3).to_broadcast([P, 2, 4, K]),
                                        ALU.subtract).then_inc(d_sub, 1)

                def softmax_b(U, qt, h):
                    v.wait_ge(a_exp, 2 * U + h + 1)
                    hs = slice(h * HP, (h + 1) * HP)
                    v.tensor_reduce(rsum[:, qt, hs], p_buf[:, qt, h * HP * K:(h + 1) * HP * K]
                                    .rearrange("p (h k) -> p h k", h=HP), X, ALU.add).then_inc(d_sum, 1)
                    v.wait_ge(d_sum, 2 * U + h + 1)
                    need(v, g_norm, 2 * U + h - 3)
                    v.reciprocal(rinv[:, qt, hs], rsum[:, qt, hs]).then_inc(d_ri, 1)

                def residual(U, T, qt):
                    v.wait_ge(p_o, U + 1)
                    xt = x_sb[:, bass.ds(T, 1), :]
                    v.scalar_tensor_tensor(out=xt, in0=ps[:, 7, 0:D].unsqueeze(1), scalar=tg[:, l:l + 1], in1=xt,
                                           op0=ALU.mult, op1=ALU.add).then_inc(d_o, 1)
                    v.wait_ge(d_o, U + 1)
                    v.tensor_tensor(xt, xt, bo[:, l, :].unsqueeze(1), ALU.add).then_inc(d_res, 1)
                    apart(v, d_passed, (d_res, U + 1))
                    v.bn_stats(st2[:, qt, :], xt).then_inc(d_st2, 1)
                    apart(v, d_passed, (d_st2, U + 1))
                    v.bn_aggr(mv2[:, qt, :], st2[:, qt, :]).then_inc(d_mv2, 1)

                def keep(B, nxt):
                    if nxt:
                        v.wait_ge(p_xnT, B + 3)
                    need(v, D_sc, 64 * B)
                    v.wait_ge(d_xn2, 2 * B + 2)
                    v.tensor_copy(xn1[:, :, :], xn2[:, :, :]).then_inc(d_keep, 1)

                def ln2_apply(U, T, B, qt):
                    v.wait_ge(g_rs2, U + 1)
                    v.wait_ge(d_mv2, U + 1)
                    if qt == 0:
                        need(v, d_keep, B)
                    v.tensor_scalar(xn2[:, qt:qt + 1, :], x_sb[:, bass.ds(T, 1), :], mv2[:, qt, 0:1], rstd2[:, qt:qt + 1],
                                    ALU.subtract, ALU.mult).then_inc(d_xn2, 1)

                def route1(B, b):
                    apart(v, d_passed, (a_lg, 2 * B + 2))
                    for t in range(2):
                        v.max(topnow[:, t, :], logits[:, t, :]).then_inc(d_r1, 1)
                    for t in range(2):
                        apart(v, d_passed, (d_r1, 7 * B + t + 1))
                        v.max_index(idx8[:, t, :], topnow[:, t, :], logits[:, t, :]).then_inc(d_r1, 1)
                    v.tensor_copy(top8[:, bass.ds(2 * b, 2), :], topnow[:, :, :]).then_inc(d_r1, 1)
                    v.wait_ge(d_r1, 7 * B + 5)
                    v.tensor_copy(idxf[:, :, :], idx8[:, :, 0:TOPK]).then_inc(d_r1, 1)
                    v.wait_ge(d_r1, 7 * B + 6)
                    oh = onehot[:, bass.ds(2 * b, 2), :, :]
                    v.tensor_tensor(oh, iota8[:, :].unsqueeze(1).unsqueeze(1).to_broadcast([P, 2, TOPK, NE]),
                                    idxf[:, :, :].unsqueeze(3).to_broadcast([P, 2, TOPK, NE]), ALU.is_equal).then_inc(d_r1, 1)
                    v.wait_ge(d_r1, 7 * B + 7)
                    need(v, p_rk, B)
                    need(v, d_cum, 2 * B)
                    v.tensor_tensor(maskb[:, :, :], oh[:, :, 0, :], oh[:, :, 1, :], ALU.add).then_inc(d_mask, 1)

                def route2(B, b):
                    v.wait_ge(p_rk, B + 1)
                    v.tensor_tensor(rk[:, :, :], ps[:, 7, 0:2 * NE].rearrange("p (t e) -> p t e", t=2),
                                    eR[:, :].unsqueeze(1).to_broadcast([P, 2, NE]), ALU.add).then_inc(d_rk, 1)
                    v.wait_ge(d_rk, B + 1)
                    v.tensor_tensor(prod[:, :, :, :], onehot[:, bass.ds(2 * b, 2), :, :],
                                    rk[:, :, :].unsqueeze(2).to_broadcast([P, 2, TOPK, NE]), ALU.mult).then_inc(d_r2, 1)
                    v.tensor_tensor(cumb[:, :], cumb[:, :], maskb[:, 0, :], ALU.add).then_inc(d_cum, 1)
                    v.wait_ge(d_r2, 2 * B + 1)
                    v.tensor_reduce(slotf[:, bass.ds(2 * b, 2), :], prod[:, :, :, :], X, ALU.add).then_inc(d_r2, 1)
                    v.wait_ge(d_cum, 2 * B + 1)
                    v.tensor_tensor(cumb[:, :], cumb[:, :], maskb[:, 1, :], ALU.add).then_inc(d_cum, 1)
                    apart(v, d_passed, (d_r2, 2 * B + 2), (D_sc, 64 * B))
                    v.tensor_copy(slot_now[:, :, :], slotf[:, bass.ds(2 * b, 2), :]).then_inc(d_slot, 1)

                def value_bias(B):
                    v.wait_ge(p_v, B + 1)
                    need(v, g_vp, B)
                    v.tensor_tensor(v_tmp[0:K, :], ps[0:K, 7, 0:D], bv[0:K, l, :], ALU.add).then_inc(d_v, 1)

                if l == 1:
                    next_index(0, 0)
                    combine(0, 0)
                    v.wait_ge(d_comb, 2)
                ln1_stats(NB * l, 0, L_x[0] if l == 0 else None)
                ln1_apply(NB * l, 0)

                def step(b, cur, nxt, nn, prev):
                    B = NB * l + b
                    U = 2 * B
                    if nxt:
                        value_bias(B + 1)
                    if cur:
                        softmax_b(U + 1, 1, 1)
                    if nxt:
                        softmax_a(U + 2, b + 1, 0)
                    if prev:
                        route1(B - 1, b - 1)
                    if cur:
                        residual(U, 2 * b, 0)
                    if nxt:
                        softmax_a(U + 2, b + 1, 1)
                    if prev:
                        keep(B - 1, nxt)
                    if cur:
                        ln2_apply(U, 2 * b, B, 0)
                    if nxt:
                        softmax_b(U + 2, 0, 0)
                    if prev:
                        route2(B - 1, b - 1)
                    if nn and l == 1:
                        next_index(b + 2, b + 2)
                    if nxt:
                        softmax_b(U + 2, 0, 1)
                        softmax_a(U + 3, b + 1, 0)
                    if cur:
                        residual(U + 1, 2 * b + 1, 1)
                    if nxt:
                        softmax_a(U + 3, b + 1, 1)
                    if cur:
                        ln2_apply(U + 1, 2 * b + 1, B, 1)
                    if nxt:
                        softmax_b(U + 3, 1, 0)
                    if nn:
                        if l == 1:
                            combine(b + 2, b + 2)
                            apart(v, d_passed, (d_comb, 2 * (b + 2) + 2))
                        if l == 0 and not cur:
                            v.wait_ge(L_x[1], 16)
                        if l == 0 and cur and not prev:
                            v.wait_ge(L_x[2], 16)
                            v.wait_ge(L_x[3], 16)
                        ln1_stats(B + 2, b + 2)
                        ln1_apply(B + 2, b + 2)
                run_steps(v, l, step)

                bc = lambda t, n: t.unsqueeze(1).to_broadcast([P, n, NE])
                v.wait_ge(d_r1, 7 * NB * (l + 1))
                v.tensor_copy(zsum[:, :], top8[:, :, 0]).then_inc(d_tm, 1)
                v.wait_ge(f_cnt, l + 1)
                v.tensor_copy(cnt[:, :], ps[:, 7, 0:NE]).then_inc(d_f, 1)
                v.wait_ge(d_f, F + 1)
                v.tensor_tensor(pad_i[:, :], cnt[:, :], padbase[:, :], ALU.add).then_inc(d_f, 1)
                c16 = cmpb[:, 0:NE * NT].rearrange("p (e t) -> p e t", e=NE)
                v.tensor_tensor(c16, cnt[:, :].unsqueeze(2).to_broadcast([P, NE, NT]),
                                thr[:, :].unsqueeze(1).to_broadcast([P, NE, NT]), ALU.is_gt).then_inc(d_f, 1)
                v.wait_ge(d_f, F + 3)
                v.tensor_reduce(nb[:, :], c16, X, ALU.add).then_inc(d_f, 1)
                v.wait_ge(d_f, F + 4)
                c8 = cmpb[:, 0:NE * NE].rearrange("p (e f) -> p e f", e=NE)
                v.tensor_tensor(c8, lower[:, :, :], bc(nb[:, :], NE), ALU.mult).then_inc(d_f, 1)
                v.wait_ge(d_f, F + 5)
                v.tensor_reduce(sbk[:, :], c8, X, ALU.add).then_inc(d_f, 1)
                v.wait_ge(d_f, F + 6)
                v.tensor_scalar(tot1[:, :], nb[:, NE - 1:NE], sbk[:, NE - 1:NE], -1.0, ALU.add, ALU.add).then_inc(d_f, 1)
                v.wait_ge(d_f, F + 7)
                v.tensor_scalar(jc[:, :], jrow[:, :], tot1[:, 0:1], None, ALU.min).then_inc(d_f, 1)
                v.wait_ge(d_f, F + 8)
                cj = cmpb[:, :].rearrange("p (j e) -> p j e", e=NE)
                v.tensor_tensor(cj, jc[:, :].unsqueeze(2).to_broadcast([P, MAX_BLOCKS, NE]),
                                bc(sbk[:, :], MAX_BLOCKS), ALU.is_ge).then_inc(d_f, 1)
                v.wait_ge(d_f, F + 9)
                v.tensor_reduce(be[:, :], cj, X, ALU.add).then_inc(d_f, 1)
                v.wait_ge(d_f, F + 10)
                v.tensor_tensor(cj, cj, bc(sbk[:, :], MAX_BLOCKS), ALU.mult).then_inc(d_f, 1)
                v.wait_ge(d_f, F + 11)
                v.tensor_reduce(sbx[:, :], cj, X, ALU.max).then_inc(d_f, 1)
                v.wait_ge(d_f, F + 12)
                v.tensor_tensor(jc[:, :], jc[:, :], sbx[:, :], ALU.subtract).then_inc(d_f, 1)
                v.wait_ge(d_f, F + 13)
                v.tensor_scalar(jc[:, :], jc[:, :], float(P), -float(REGION), ALU.mult, ALU.add).then_inc(d_f, 1)
                v.wait_ge(d_f, F + 14)
                v.scalar_tensor_tensor(out=xrow_i[:, :], in0=be[:, :], scalar=float(REGION), in1=jc[:, :],
                                       op0=ALU.mult, op1=ALU.add).then_inc(d_f, 1)
                v.tensor_scalar(woff_i[:, :], be[:, :], float(EW[l]), -float(EW[l]), ALU.mult, ALU.add).then_inc(d_f, 1)
                v.wait_ge(d_tm, l + 1)
                v.tensor_tensor(top8[:, :, :], top8[:, :, :], zsum[:, :].unsqueeze(2).to_broadcast([P, NT, 8]),
                                ALU.subtract).then_inc(d_f, 1)
                v.scalar_tensor_tensor(out=yoff[:, :], in0=sbk[:, :], scalar=float(P), in1=eR[:, :],
                                       op0=ALU.mult, op1=ALU.subtract).then_inc(d_f, 1)
                v.wait_ge(d_f, F + 18)
                c32 = cmpb[:, 0:NT * TOPK * NE].rearrange("p (n e) -> p n e", e=NE)
                v.tensor_tensor(c32, onehot[:, :, :, :].rearrange("p t k e -> p (t k) e"), bc(yoff[:, :], NT * TOPK),
                                ALU.mult).then_inc(d_f, 1)
                v.wait_ge(d_f, F + 19)
                v.tensor_reduce(yslot[:, :, :].rearrange("p t k -> p (t k)"), c32, X, ALU.add).then_inc(d_f, 1)
                v.wait_ge(d_f, F + 20)
                v.tensor_tensor(yslot[:, :, :], yslot[:, :, :], slotf[:, :, :], ALU.add).then_inc(d_f, 1)
                v.memset(cumb[:], 0.0).then_inc(d_f, 1)

                def blk(j, u, i, first, last):
                    J = MAX_BLOCKS * l + j
                    if first:
                        x_evac(J, j)
                    if l == 0:
                        for q in range(2):
                            v.wait_ge(e_act, 2 * j + q + 1)
                            v.wait_ge(b_up, 4 * j + 2 * q + 2)
                            need(v, b_hT, 2 * j)
                            v.tensor_tensor(h_sb[:, 344 * q:344 * q + 344], act_sb[:, 344 * q:344 * q + 344],
                                            ps[:, 2 * q + 1, 0:344], ALU.mult).then_inc(e_h, 1)
                    else:
                        v.wait_ge(e_act, 2 * MAX_BLOCKS + j + 1)
                        v.wait_ge(b_hT, 2 * MAX_BLOCKS + j)
                        v.tensor_tensor(h_sb[:, 0:HID[1]], act_sb[:, 0:HID[1]], act_sb[:, 0:HID[1]], ALU.mult).then_inc(e_h, 1)
                    if not last:
                        x_evac(J + 1, j + 1)
                    if not first:
                        y_evac(J - 1, (u - 1) % U3, i)
                    if l == 0:
                        v.wait_ge(b_hT, 2 * j + 2)
                        need(v, b_y, j)
                        v.tensor_copy(hT[:, 4, :], ps[:, 5, 0:P])
                        r = DOWN[0][5][1]
                        v.tensor_copy(hT[0:r, 5, :], ps[0:r, 5, P:2 * P]).then_inc(e_hTv, 1)
                    if last:
                        y_evac(J, u, i)

                def x_evac(J, j):
                    v.wait_ge(b_x, J + 1)
                    need(v, b_up, 4 * j if l == 0 else 4 * MAX_BLOCKS + j)
                    v.tensor_copy(xgT[:, :, :], ps[:, 7, 0:KT * P].rearrange("p (k n) -> p k n", k=KT)).then_inc(e_x, 1)

                def y_evac(J, u, i):
                    v.wait_ge(b_y, J + 1)
                    need(v, D_y[u], 16 * i + 16 * (MAX_BLOCKS // U3) * l)
                    v.tensor_copy(y_sb[:, u, :], ps[:, 6, 0:D]).then_inc(e_y, 1)

                v.wait_ge(f_exp, l + 1)
                e01 = top8[:, :, 0:TOPK]
                v.tensor_reduce(zsum[:, :], top8[:, :, :], X, ALU.add).then_inc(C_v, 1)
                v.tensor_tensor(wcomb[:, :, 0], top8[:, :, 0], top8[:, :, 1], ALU.add).then_inc(C_v, 1)
                v.wait_ge(C_v, 4 + 6 * l + 2)
                v.scalar_tensor_tensor(out=zsum[:, :], in0=zsum[:, :], scalar=1e-6 if l == 0 else 0.0, in1=wcomb[:, :, 0],
                                       op0=ALU.mult, op1=ALU.add).then_inc(C_v, 1)
                v.wait_ge(C_v, 4 + 6 * l + 3)
                v.reciprocal(zsum[:, :], zsum[:, :]).then_inc(C_v, 1)
                v.wait_ge(C_v, 4 + 6 * l + 4)
                v.tensor_scalar(zsum[:, :], zsum[:, :], tg[:, 2 + l:3 + l], None, ALU.mult).then_inc(C_v, 1)
                v.wait_ge(C_v, 4 + 6 * l + 5)
                v.tensor_tensor(wcomb[:, :, :], e01, zsum[:, :].unsqueeze(2).to_broadcast([P, NT, TOPK]), ALU.mult).then_inc(C_v, 1)
                v.wait_ge(C_v, 4 + 6 * l + 6)

                run_blocks(v, l, blk)

            with v.Fori(0, NB) as b:
                apart(v, d_passed, (D_ga, 64 * b + 64 * NB))
                v.tensor_copy(ynow[:, :, :], yslot[:, bass.ds(2 * b, 2), :]).then_inc(d_yn, 1)
                combine(b + NB, b)

        @block.tensor
        def _(t):
            t.wait_ge(C_g, 15)

            for l in range(2):
                def ctx_t(B):
                    t.wait_ge(L_ctx, 16 * (B + 1))
                    for k in range(KT):
                        i = t.transpose(ps[:, 7, k * K:(k + 1) * K], ctx_sb[0:K, k * P:(k + 1) * P], ident[0:K, 0:K])
                    i.then_inc(p_ctx, 1)

                def k_proj(B):
                    t.wait_ge(a_ctx, B + 1)
                    for m in range(KT):
                        for k in range(KT):
                            i = t.matmul(ps[:, 7, m * K:(m + 1) * K], w_att[:, 1, k, m * P:(m + 1) * P], ctxT[:, k, :],
                                         start=(k == 0), stop=(k == KT - 1))
                    i.then_inc(p_k, 1)

                def x_t(B):
                    t.wait_ge(d_xn1, B + 1)
                    t.wait_ge(a_k, B + 1)
                    for k in range(KT):
                        for q in range(QT):
                            i = t.transpose(ps[:, 7, k * S + q * P:k * S + (q + 1) * P], xn1[:, q, k * P:(k + 1) * P], ident[:, :])
                    i.then_inc(p_xnT, 1)

                def q_proj(B):
                    t.wait_ge(a_xnT, B + 1)
                    for m in range(KT):
                        for k in range(KT):
                            i = t.matmul(ps[:, 7, m * S:(m + 1) * S], w_att[:, 0, k, m * P:(m + 1) * P], xn1T[:, k, :],
                                         start=(k == 0), stop=(k == KT - 1))
                    i.then_inc(p_q, 1)

                def v_proj(B):
                    t.wait_ge(a_q, B + 1)
                    for k in range(KT):
                        i = t.matmul(ps[0:K, 7, 0:D], ctxT[:, k, :], w_att[:, 2, k, :], start=(k == 0), stop=(k == KT - 1))
                    i.then_inc(p_v, 1)

                def score(U, qt, c):
                    h = c // 2
                    if c % 2 == 0:
                        if l == 0:
                            need(t, d_add, 2 * U + h - 1)
                        else:
                            t.wait_ge(d_sub, 2 * U + h - 1)
                    i = t.matmul(ps[:, c, 0:CH], qT[:, h, qt * P:(qt + 1) * P],
                                 kbd[:, h, 4 * (c % 2):4 * (c % 2) + 4, :], start=True, stop=True)
                    if c % 2 == 1:
                        i.then_inc(p_s, 1)

                def probs_t(U, qt, c):
                    if c % 2 == 0:
                        t.wait_ge(g_norm, 2 * U + c // 2 + 1)
                    need(t, a_t, 4 * U + c - 1)
                    for h in range(4):
                        i = t.transpose(ps[0:K, 4 + c % 2, h * P:(h + 1) * P],
                                        p_buf[:, qt, (4 * c + h) * K:(4 * c + h + 1) * K], ident[:, :])
                    i.then_inc(p_t, 1)

                def values(U, B, c):
                    t.wait_ge(a_t, 4 * U + c + 1)
                    if c == 0:
                        t.wait_ge(g_vp, B + 1)
                        need(t, a_c, U)
                    for h4 in range(4):
                        h = 4 * c + h4
                        g4 = (h % HP) // 2
                        i = t.matmul(ps[32 * g4:32 * g4 + 32, 6, (h // HP) * P:(h // HP + 1) * P], v_pad[0:K, h, :],
                                     pT[0:K, c % 2, h4 * P:(h4 + 1) * P], start=(h % 2 == 0), stop=(h % 2 == 1))
                    i.then_inc(p_pv, 1)

                def out_proj(U):
                    t.wait_ge(a_c, U + 1)
                    for k in range(KT):
                        i = t.matmul(ps[:, 7, 0:D], cT[:, k, :], w_att[:, 3, k, :], start=(k == 0), stop=(k == KT - 1))
                    i.then_inc(p_o, 1)

                def x2_t(U, qt):
                    t.wait_ge(d_xn2, U + 1)
                    for k in range(KT):
                        i = t.transpose(ps[:, 7, k * P:(k + 1) * P], xn2[:, qt, k * P:(k + 1) * P], ident[:, :])
                    i.then_inc(p_x2, 1)

                def route(U):
                    t.wait_ge(a_x2, U + 1)
                    for k in range(KT):
                        i = t.matmul(ps[:, 7, 0:NE], xn2T[:, k, :], wr[:, l, k, :], start=(k == 0), stop=(k == KT - 1))
                    i.then_inc(p_lg, 1)

                def ranks(B):
                    t.wait_ge(d_mask, B + 1)
                    need(t, d_cum, 2 * B)
                    t.matmul(ps[:, 7, 0:NE], tri[:, :], maskb[:, 0, :], start=True, stop=False)
                    t.matmul(ps[:, 7, 0:NE], ones[:, :], cumb[:, :], start=False, stop=True)
                    t.matmul(ps[:, 7, NE:2 * NE], tri[:, :], maskb[:, 1, :], start=True, stop=False)
                    t.matmul(ps[:, 7, NE:2 * NE], ones[:, :], maskb[:, 0, :], start=False, stop=False)
                    t.matmul(ps[:, 7, NE:2 * NE], ones[:, :], cumb[:, :], start=False, stop=True).then_inc(p_rk, 1)

                if l == 1:
                    t.wait_ge(e_x, MAX_BLOCKS)
                    t.wait_ge(e_y, MAX_BLOCKS)
                t.wait_ge(L_w, 64 * (l + 1))
                t.wait_ge(L_small, 16 * NSMALL)
                ctx_t(NB * l)

                def step(b, cur, nxt, nn, prev):
                    B = NB * l + b
                    U = 2 * B
                    if cur:
                        probs_t(U, 0, 0)
                        probs_t(U, 0, 1)
                    if nxt:
                        k_proj(B + 1)
                    if cur:
                        values(U, B, 0)
                        probs_t(U, 0, 2)
                    if nxt:
                        x_t(B + 1)
                    if cur:
                        values(U, B, 1)
                        probs_t(U, 0, 3)
                    if nxt:
                        q_proj(B + 1)
                    if cur:
                        values(U, B, 2)
                    if nxt:
                        v_proj(B + 1)
                    if cur:
                        values(U, B, 3)
                    if nxt:
                        t.wait_ge(g_kbd, B + 2)
                        t.wait_ge(a_q, B + 2)
                        score(U + 2, 0, 0)
                    if prev:
                        if nxt:
                            t.wait_ge(d_v, B + 2)
                        x2_t(U - 1, 1)
                    if nxt:
                        score(U + 2, 0, 1)
                    if prev:
                        route(U - 1)
                    if nxt:
                        score(U + 2, 0, 2)
                    if cur:
                        if prev:
                            t.wait_ge(a_lg, U)
                        else:
                            t.wait_ge(d_v, B + 2)
                        out_proj(U)
                    if nxt:
                        score(U + 2, 0, 3)
                    if cur:
                        probs_t(U + 1, 1, 0)
                        probs_t(U + 1, 1, 1)
                    if prev:
                        if cur:
                            t.wait_ge(d_o, U + 1)
                        else:
                            t.wait_ge(a_lg, U)
                        ranks(B - 1)
                    if cur:
                        values(U + 1, B, 0)
                        probs_t(U + 1, 1, 2)
                        if prev:
                            t.wait_ge(d_rk, B)
                        x2_t(U, 0)
                        values(U + 1, B, 1)
                        probs_t(U + 1, 1, 3)
                        values(U + 1, B, 2)
                        route(U)
                        values(U + 1, B, 3)
                    if nxt:
                        score(U + 3, 1, 0)
                        score(U + 3, 1, 1)
                    if cur:
                        t.wait_ge(a_lg, U + 1)
                        out_proj(U + 1)
                    if nxt:
                        score(U + 3, 1, 2)
                    if nn:
                        if cur:
                            t.wait_ge(d_o, U + 2)
                        else:
                            t.wait_ge(d_v, B + 2)
                        ctx_t(B + 2)
                    if nxt:
                        score(U + 3, 1, 3)
                run_steps(t, l, step)

                t.wait_ge(d_cum, 2 * NB * (l + 1))
                t.wait_ge(d_rk, NB * (l + 1))
                t.matmul(ps[:, 7, 0:NE], ones[:, :], cumb[:, :], start=True, stop=True).then_inc(f_cnt, 1)
                t.wait_ge(d_f, 16 + 22 * l)
                t.wait_ge(L_exp, 16 * (4 * NE if l == 0 else 4 * NE + 2 * NE))

                def block_t(j, u, i):
                    J = MAX_BLOCKS * l + j
                    t.wait_ge(L_xg[u], 16 * i + (16 + 16 * (MAX_BLOCKS // U3) * l))
                    need(t, e_x, J)
                    for k in range(KT):
                        i = t.transpose(ps[:, 7, k * P:(k + 1) * P], xg[:, u, k * P:(k + 1) * P], ident[:, :])
                    i.then_inc(b_x, 1)

                def up(j):
                    J = MAX_BLOCKS * l + j
                    off = t.value_load(woff_i[0:1, bass.ds(j, 1)], min_val=0, max_val=(NE - 1) * EW[l])
                    t.wait_ge(e_x, J + 1)
                    for n, (bank, col, w) in enumerate(UP[l]):
                        if l == 0:
                            need(t, e_h, 2 * j - 1 + n // 2) if n % 2 else need(t, e_act, 2 * j - 1 + n // 2)
                        else:
                            t.wait_ge(e_act, 2 * MAX_BLOCKS + j)
                        for k in range(KT):
                            i = t.matmul(ps[:, bank, 0:w], xgT[:, k, :], w_all[:, bass.ds(off + (k * UPW[l] + col), w)],
                                         start=(k == 0), stop=(k == KT - 1))
                        i.then_inc(b_up, 1)

                def h_t(j):
                    if l == 0:
                        t.wait_ge(e_h, 2 * j + 2)
                        need(t, e_hT, j)
                    else:
                        t.wait_ge(e_h, 2 * MAX_BLOCKS + j + 1)
                        t.wait_ge(e_hT, MAX_BLOCKS + j)
                    for c, r in DOWN[l]:
                        if c == 4:
                            i.then_inc(b_hT, 1)
                            need(t, e_hTv, j)
                        i = t.transpose(ps[0:r, 4 + c // 4, (c % 4) * P:(c % 4 + 1) * P], h_sb[:, c * P:c * P + r], ident[:, :])
                    i.then_inc(b_hT, 1)

                def down(j):
                    J = MAX_BLOCKS * l + j
                    off = t.value_load(woff_i[0:1, bass.ds(j, 1)], min_val=0, max_val=(NE - 1) * EW[l])
                    t.wait_ge(e_hT, J + 1)
                    if l == 0:
                        t.wait_ge(e_hTv, j + 1)
                    need(t, e_y, J)
                    for c, r in DOWN[l]:
                        i = t.matmul(ps[:, 6, 0:D], hT[0:r, c, :], w_all[0:r, bass.ds(off + (KT * UPW[l] + c * D), D)],
                                     start=(c == 0), stop=(c == KD[l] - 1))
                    i.then_inc(b_y, 1)

                block_t(0, 0, 0)

                def blk(j, u, i, first, last):
                    up(j)
                    if not last:
                        block_t(j + 1, (u + 1) % U3, i if u == 1 else i + 1)
                    if not first:
                        down(j - 1)
                    h_t(j)
                    if last:
                        down(j)
                run_blocks(t, l, blk)


def kernel(**inputs):
    import numpy as np
    import concourse.bacc as bacc
    from concourse.bass_utils import run_bass_kernel_spmd

    nc = bacc.Bacc("TRN2", target_bir_lowering=False, num_devices=1)
    arrays = {}

    def dram(name, a):
        a = np.ascontiguousarray(a)
        arrays[name] = a
        return nc.dram_tensor(name, a.shape, mybir.dt.from_np(a.dtype), kind="ExternalInput").ap()

    I = {k: np.asarray(v) for k, v in inputs.items()}
    attn_w, attn_b, router_w, experts = [], [], [], []
    for l in range(2):
        ws = [I[f"L{l}_xattn_W{c}"] for c in "qkvo"]
        attn_w.append([dram(f"w{c}{l}", w.T if l else w) for c, w in zip("qkvo", ws)])
        bs = [I[f"L{l}_xattn_b{c}"] for c in "qkvo"]
        attn_b.append([dram(f"b{c}{l}", b.reshape(2, 128).T if c in "qk" else b) for c, b in zip("qkvo", bs)])
    router_w = [dram("router0", I["L0_ffn_router_w"]), dram("router1", I["L1_ffn_router_w"].T)]
    experts = [[dram("gate0", I["L0_ffn_w_gate"]), dram("up0", I["L0_ffn_w_up"]), dram("down0", I["L0_ffn_w_down"])],
               [dram("w1", I["L1_ffn_w1_all"]), dram("w2", I["L1_ffn_w2_all"])]]
    x = dram("x", I["x"])
    ctx_rows = dram("ctx", I["ctx_1024"])
    mask = dram("mask", I["mask_Bx1x1xS2_ff0"].reshape(8, 120))
    out = nc.dram_tensor("out", x.shape, F32, kind="ExternalOutput").ap()
    flamingo_kernel(nc, x, ctx_rows, mask, dram("g_xattn", I["g_xattn"]), dram("g_ffn", I["g_ffn"]),
                    attn_w, attn_b, router_w, experts, out)
    r = run_bass_kernel_spmd(nc, [arrays], core_ids=[0])
    return r.results[0]["out"]
```

```python
from contextlib import ExitStack

import concourse.bass as bass
from concourse import mybir

F32 = mybir.dt.float32
BF16 = mybir.dt.bfloat16
I32 = mybir.dt.int32
U32 = mybir.dt.uint32
ALU = mybir.AluOpType
ACT = mybir.ActivationFunctionType
X = mybir.AxisListType.X

P = 128
NEG = -1000000000.0


def need(eng, sem, value):
    if not isinstance(value, int) or value > 0:
        eng.wait_ge(sem, value)


def apart(eng, passed, *waits):
    for sem, v in waits:
        need(eng, sem, v)
    if any(not isinstance(v, int) for _, v in waits):
        eng.sem_inc(passed, 1)


def flamingo_kernel(nc, x, ctx_rows, mask, g_xattn, g_ffn, attn_w, attn_b, router_w, experts, out):
    NB, S, D = x.shape
    K = ctx_rows.shape[1]
    H = 16
    DH = D // H
    HP = P // DH
    KT = D // P
    NT = NB * S // P
    QT = S // P
    NE = router_w[0].shape[1]
    TOPK = 2
    CH = 4 * K
    HID = [experts[0][0].shape[2], experts[1][0].shape[2]]
    KD = [-(-h // P) for h in HID]
    MAX_BLOCKS = (NT * P * TOPK + NE * (P - 1)) // P
    REGION = NT * P + P
    UPW = [2 * HID[0], HID[1]]
    EW = [KT * UPW[l] + KD[l] * D for l in range(2)]
    U3 = 3
    assert MAX_BLOCKS % U3 == 0 and QT == 2 and KT == 2

    xs_dram = nc.dram_tensor("xs_dram", [NE * REGION, D], F32, kind="Internal").ap()
    ys_dram = nc.dram_tensor("ys_dram", [MAX_BLOCKS * P, D], F32, kind="Internal").ap()

    es = ExitStack()
    with es:
        def sb(name, shape, dt=F32):
            return es.enter_context(nc.sbuf_tensor(name, shape, dt))

        def sem(name):
            return es.enter_context(nc.semaphore(name))

        x_sb = sb("x_sb", [P, NT, D])
        w_all = sb("w_all", [P, NE * EW[0]])
        w_att = sb("w_att", [P, 4, KT, D])
        wr = sb("wr", [P, 2, KT, NE])
        bq = sb("bq", [P, 2, KT])
        bq4 = sb("bq4", [P, 2, KT])
        bk = sb("bk", [P, 2, KT])
        bv = sb("bv", [P, 2, D])
        bo = sb("bo", [P, 2, D])
        gates = sb("gates", [P, 4])
        tg = sb("tg", [P, 4])
        mask3 = sb("mask3", [P, NB, K], BF16)
        ctx_sb = sb("ctx_sb", [P, D])
        ctxT = sb("ctxT", [P, KT, K])
        kT = sb("kT", [P, KT, K])
        v_tmp = sb("v_tmp", [P, D])
        v_pad = sb("v_pad", [P, H, 2 * DH])
        xn1 = sb("xn1", [P, QT, D])
        xn1T = sb("xn1T", [P, KT, S])
        qT = sb("qT", [P, KT, S])
        pT = sb("pT", [P, 2, 4 * P])
        rT = sb("rT", [P, KT, P])
        rsum = sb("rsum", [P, QT, H])
        rinv = sb("rinv", [P, QT, H])
        rinv16 = sb("rinv16", [P, H, DH])
        cT = sb("cT", [P, KT, P])
        xn2 = sb("xn2", [P, QT, D])
        kept = sb("kept", [P, QT, D])
        share = sb("share", [P, 3968])
        s_sb = share[:, 0:2 * HP * K].rearrange("p (h n) -> p h n", h=2)
        kbd = share[:, 2 * HP * K:4 * HP * K].rearrange("p (m h k) -> p m h k", m=2, h=HP)
        xg = share[:, 0:768].rearrange("p (u d) -> p u d", u=U3)
        xgT = share[:, 768:1024].rearrange("p (k n) -> p k n", k=KT)
        act_sb = share[:, 1024:1712]
        h_sb = share[:, 1712:2400]
        hT = share[:, 2400:3168].rearrange("p (c n) -> p c n", c=6)
        y_sb = share[:, 3168:3936].rearrange("p (u d) -> p u d", u=U3)
        zrow = y_sb[:, 1, :]
        p_buf = w_all[:, (NE - 1) * EW[0]:(NE - 1) * EW[0] + 2 * H * K].rearrange("p (q n) -> p q n", q=2)
        yg = w_all[:, NE * EW[1]:NE * EW[1] + NB * QT * TOPK * D].rearrange("p (b t k d) -> p b t k d", b=NB, t=QT, k=TOPK)
        mask_bc = share[:, 0:NB * K].rearrange("p (b k) -> p b k", b=NB)
        mask_hi = share[:, NB * K:NB * K + NB * K // 2].bitcast(BF16).rearrange("p (b k) -> p b k", b=NB)
        spare = (NE - 1) * EW[0] + 2 * H * K
        xn2T = w_all[:, spare:spare + D].rearrange("p (k n) -> p k n", k=KT)
        assert 2 * H * K + D <= EW[0]
        mx = sb("mx", [P, 2, HP])
        st1 = sb("st1", [P, QT, 6])
        mv1 = sb("mv1", [P, QT, 2])
        ve1 = sb("ve1", [P, QT])
        rstd1 = sb("rstd1", [P, QT])
        st2 = sb("st2", [P, QT, 6])
        mv2 = sb("mv2", [P, QT, 2])
        ve2 = sb("ve2", [P, QT])
        rstd2 = sb("rstd2", [P, QT])
        jc, be, sbx = (share[:, 2048 + n * MAX_BLOCKS:2048 + (n + 1) * MAX_BLOCKS] for n in range(3))
        logits = share[:, 3840:3856].rearrange("p (t e) -> p t e", t=2)
        topnow = share[:, 3856:3872].rearrange("p (t e) -> p t e", t=2)
        idx8 = share[:, 3872:3888].bitcast(U32).rearrange("p (t e) -> p t e", t=2)
        rk = share[:, 3888:3904].rearrange("p (t e) -> p t e", t=2)
        prod = share[:, 3904:3936].rearrange("p (t k e) -> p t k e", t=2, k=TOPK)
        idxf = share[:, 3936:3940].rearrange("p (t k) -> p t k", t=2)
        top8 = sb("top8", [P, NT, 8])
        onehot = sb("onehot", [P, NT, TOPK, NE])
        maskb = sb("maskb", [P, 2, NE], BF16)
        cumb = sb("cumb", [P, NE], BF16)
        slotf = sb("slotf", [P, NT, TOPK])
        slot_now = sb("slot_now", [P, 2, TOPK], I32)
        cnt = sb("cnt", [P, NE])
        pad_i = sb("pad_i", [P, NE], I32)
        cmpb = pT[:, :, :].rearrange("p a b -> p (a b)")[:, 0:MAX_BLOCKS * NE]
        nb = sb("nb", [P, NE])
        sbk = sb("sbk", [P, NE])
        tot1 = sb("tot1", [P, 1])
        xrow_i = sb("xrow_i", [P, MAX_BLOCKS], I32)
        woff_i = sb("woff_i", [P, MAX_BLOCKS], I32)
        yoff = sb("yoff", [P, NE])
        yslot = sb("yslot", [P, NT, TOPK])
        yslot_i = sb("yslot_i", [P, NT, TOPK], I32)
        ynow = sb("ynow", [P, 2, TOPK], I32)
        zsum = sb("zsum", [P, NT])
        wcomb = sb("wcomb", [P, NT, TOPK])
        ident = sb("ident", [P, P])
        hmask = sb("hmask", [P, HP])
        tri = sb("tri", [P, P], BF16)
        ones = sb("ones", [P, P], BF16)
        iota8 = sb("iota8", [P, NE])
        eR = sb("eR", [P, NE])
        thr = sb("thr", [P, NT])
        jrow = sb("jrow", [P, MAX_BLOCKS])
        lower = sb("lower", [P, NE, NE])
        mhalf = sb("mhalf", [P, QT])
        ps = es.enter_context(nc.psum_tensor("ps", [P, 8, 512], F32))

        L_x = [sem(f"x_loaded{i}") for i in range(4)]
        L_w = sem("attn_w_loaded")
        L_small = sem("small_loaded")
        L_ctx = sem("ctx_loaded")
        L_exp = sem("experts_loaded")
        L_xg = [sem(f"block_loaded{u}") for u in range(U3)]
        D_y = [sem(f"block_stored{u}") for u in range(U3)]
        D_sc = sem("tokens_scattered")
        D_pad = sem("pads_scattered")
        D_ga = sem("results_gathered")
        D_gl = [sem(f"last_results_gathered{b}") for b in range(NB)]
        D_out = [sem(f"out_stored{i}") for i in range(2)]
        C_g = sem("consts_pool")
        C_v = sem("consts_vector")
        C_a = sem("gates_ready")
        p_k, p_xnT, p_q, p_v, p_ctx = (sem(n) for n in ("k_psum", "xn1T_psum", "q_psum", "v_psum", "ctxT_psum"))
        p_s, p_t, p_pv, p_o = (sem(n) for n in ("scores_psum", "probsT_psum", "ctx_chunk_psum", "o_psum"))
        p_x2, p_lg, p_rk = (sem(n) for n in ("xn2T_psum", "logits_psum", "rank_psum"))
        a_k, a_xnT, a_q, a_ctx = (sem(n) for n in ("k_sb_ready", "xn1T_ready", "q_ready", "ctxT_ready"))
        a_t, a_exp, a_rt, a_x2, a_lg = (sem(n) for n in ("probsT_ready", "exp_ready", "rinvT_ready", "xn2T_ready", "logits_ready"))
        d_v, d_max, d_sub, d_c = (sem(n) for n in ("v_ready", "max_ready", "shifted_ready", "cT_ready"))
        d_o, d_st2, d_mv2, d_xn2 = (sem(n) for n in ("residual_ready", "stats2_ready", "meanvar2_ready", "xn2_ready"))
        d_st1, d_mv1, d_xn1 = (sem(n) for n in ("stats1_ready", "meanvar1_ready", "xn1_ready"))
        d_r1, d_mask, d_rk, d_slot, d_cum = (sem(n) for n in ("route_step", "mask_ready", "rank_read", "slots_ready", "cum_ready"))
        d_r2 = sem("route2_step")
        d_keep = sem("batch_kept")
        d_f = sem("final_route_step")
        d_sum, d_ri, a_re, p_rt = (sem(n) for n in ("sums_ready", "rinv_ready", "rinv_spread", "rinvT_psum"))
        d_m = sem("mask_split_step")
        d_tm = sem("top_max_ready")
        d_comb, d_c1, d_yn = (sem(n) for n in ("combined", "combine_step", "gather_index_ready"))
        g_kbd, g_ve2, g_rs2, g_ve1, g_rs1, g_vp = (sem(n) for n in (
            "kbd_ready", "vareps2", "rstd2_ready", "vareps1", "rstd1_ready", "vpad_ready"))
        f_cnt = sem("count_psum")
        f_exp = sem("top_exp_ready")
        b_x, b_up, b_h, b_hT, b_y = (sem(n) for n in ("blkT_psum", "up_psum", "h_used", "hT_psum", "y_psum"))
        e_x, e_act, e_hT, e_hTv, e_y, e_h = (sem(n) for n in ("blkT_ready", "act_ready", "hT_ready_a", "hT_ready_v", "y_ready", "h_ready"))
        g_z = sem("zeros_ready")
        g_bias = sem("bias_added")
        d_yi = sem("last_indices_ready")
        g_passed, d_passed = sem("pool_passed"), sem("vector_passed")

        block = es.enter_context(nc.Block())

        NSMALL = 2 * 5 + 3

        def run_steps(eng, l, step):
            step(-1, False, True, True, False)
            step(0, True, True, True, False)
            step(1, True, True, True, True)
            with eng.Fori(2, NB - 2) as b:
                step(b, True, True, True, True)
            step(NB - 2, True, True, False, True)
            step(NB - 1, True, False, False, True)
            step(NB, False, False, False, True)

        def run_blocks(eng, l, step):
            for j in range(U3 + 1):
                step(j, j % U3, (j - 1) // U3, j == 0, False)
            with eng.Fori(1, (MAX_BLOCKS - U3) // U3) as i:
                for u in range(U3):
                    step(U3 * i + (1 + u), (1 + u) % U3, i, False, False)
            for j in (MAX_BLOCKS - 2, MAX_BLOCKS - 1):
                step(j, j % U3, (j - 1) // U3, False, j == MAX_BLOCKS - 1)

        UP = [[(0, 0, 344), (1, HID[0], 344), (2, 344, 344), (3, HID[0] + 344, 344)], [(0, 0, HID[1])]]
        DOWN = [[(c, min(P, HID[l] - c * P)) for c in range(KD[l])] for l in range(2)]

        def load_experts(eng, l, es_):
            base = [w_all[:, e * EW[l]:(e + 1) * EW[l]] for e in range(NE)]
            for e in es_:
                ups, down = experts[l][:-1], experts[l][-1]
                for i, w in enumerate(ups):
                    dst = base[e][:, 0:KT * UPW[l]].rearrange("p (k n) -> p k n", k=KT)
                    eng.dma_start(dst[:, :, i * HID[l]:(i + 1) * HID[l]],
                                w[e, :, :].rearrange("(k p) n -> p k n", p=P)).then_inc(L_exp, 16)
                full = HID[l] // P
                dst = base[e][:, KT * UPW[l]:].rearrange("p (c n) -> p c n", c=KD[l])
                eng.dma_start(dst[:, 0:full, :],
                            down[e, 0:full * P, :].rearrange("(c p) n -> p c n", p=P)).then_inc(L_exp, 16)
                if HID[l] % P:
                    eng.dma_start(dst[0:HID[l] % P, full, :], down[e, full * P:, :]).then_inc(L_exp, 16)

        @block.sync
        def _(sp):
            xv = x.rearrange("b (t p) d -> p (b t) d", p=P)

            def load_ctx(l, b):
                sp.dma_start(ctx_sb[0:K, :], ctx_rows[b % NB if isinstance(b, int) else b, :, :]).then_inc(L_ctx, 16)

            def load_att(l):
                for i in (1, 0, 2, 3):
                    sp.dma_start(w_att[:, i, :, :], attn_w[l][i].rearrange("(k p) n -> p k n", p=P)).then_inc(L_w, 16)

            sp.dma_start(x_sb[:, 0:2, :], xv[:, 0:2, :]).then_inc(L_x[0], 16)
            sp.dma_start(ctx_sb[0:K, :], ctx_rows[0, :, :]).then_inc(L_ctx, 16)
            load_att(0)
            for l in range(2):
                q_b, k_b, v_b, o_b = attn_b[l]
                sp.dma_start(bq[:, l, :], q_b).then_inc(L_small, 16)
                sp.dma_start(bk[:, l, :], k_b).then_inc(L_small, 16)
                sp.dma_start(bv[:, l, :], v_b.unsqueeze(0).to_broadcast([P, D])).then_inc(L_small, 16)
                sp.dma_start(bo[:, l, :], o_b.unsqueeze(0).to_broadcast([P, D])).then_inc(L_small, 16)
                sp.dma_start(wr[:, l, :, :], router_w[l].rearrange("(k p) n -> p k n", p=P)).then_inc(L_small, 16)
            sp.dma_start(mask_bc, mask.unsqueeze(0).to_broadcast([P, NB, K])).then_inc(L_small, 16)
            sp.dma_start(gates[:, 0:2], g_xattn.unsqueeze(0).to_broadcast([P, 2])).then_inc(L_small, 16)
            sp.dma_start(gates[:, 2:4], g_ffn.unsqueeze(0).to_broadcast([P, 2])).then_inc(L_small, 16)
            for i, (a, z) in enumerate(((2, 4), (4, 8), (8, 16))):
                sp.dma_start(x_sb[:, a:z, :], xv[:, a:z, :]).then_inc(L_x[i + 1], 16)

            for l in range(2):
                if l == 1:
                    sp.wait_ge(b_y, MAX_BLOCKS)
                    load_experts(sp, 1, range(NE))
                with sp.Fori(1, NB) as b:
                    sp.wait_ge(p_ctx, NB * l + b)
                    sp.dma_start(ctx_sb[0:K, :], ctx_rows[bass.ds(b, 1), :, :].rearrange("b k d -> (b k) d")).then_inc(L_ctx, 16)
                sp.wait_ge(p_ctx, NB * (l + 1))
                if l == 0:
                    sp.dma_start(ctx_sb[0:K, :], ctx_rows[0, :, :]).then_inc(L_ctx, 16)
                    sp.wait_ge(p_o, NT)
                    load_att(1)
                sp.wait_ge(d_f, 2 + 22 * l)
                sp.wait_ge(g_z, l + 1)
                for e in range(NE):
                    row = sp.value_load(pad_i[0:1, e:e + 1], min_val=0, max_val=NE * REGION - P)
                    sp.dma_start(xs_dram[bass.ds(row, P), :], zrow).then_inc(D_pad, 16)
                sp.wait_ge(D_sc, 16 * TOPK * NT * (l + 1))
                sp.wait_ge(D_pad, 16 * NE * (l + 1))
                sp.wait_ge(d_f, 16 + 22 * l)

                def load_block(j, u):
                    J = MAX_BLOCKS * l + j
                    if not (isinstance(j, int) and j < U3):
                        sp.wait_ge(b_x, J - U3 + 1)
                    row = sp.value_load(xrow_i[0:1, bass.ds(j, 1)], min_val=0, max_val=NE * REGION - P)
                    sp.dma_start(xg[:, u, :], xs_dram[bass.ds(row, P), :]).then_inc(L_xg[u], 16)

                for j in range(U3):
                    load_block(j, j)
                with sp.Fori(1, MAX_BLOCKS // U3) as i:
                    for u in range(U3):
                        load_block(U3 * i + u, u)
            ov = out.rearrange("b (t p) d -> p b t d", p=P)
            for b in range(NB):
                sp.wait_ge(d_comb, NT + 2 * (b + 1))
                sp.dma_start(ov[:, b, :, :], x_sb[:, 2 * b:2 * b + 2, :]).then_inc(D_out[b % 2], 16)
            sp.wait_ge(D_out[0], 16 * NB // 2)
            sp.wait_ge(D_out[1], 16 * NB // 2)

        @block.gpsimd
        def _(g):
            g.memset(ident[:], 0.0).then_inc(C_g, 1)
            g.memset(hmask[:], 1.0).then_inc(C_g, 1)
            g.memset(tri[:], 1.0).then_inc(C_g, 1)
            g.memset(ones[:], 1.0).then_inc(C_g, 1)
            g.memset(lower[:], 1.0).then_inc(C_g, 1)
            g.memset(mhalf[:], -0.5).then_inc(C_g, 1)
            g.wait_ge(C_g, 6)
            g.affine_select(out=ident[:], in_=ident[:], compare_op=ALU.not_equal, fill=1.0, base=0,
                            pattern=[[-1, P]], channel_multiplier=1).then_inc(C_g, 1)
            g.affine_select(out=hmask[:], in_=hmask[:], compare_op=ALU.is_ge, fill=0.0, base=0,
                            pattern=[[-DH, HP]], channel_multiplier=1).then_inc(C_g, 1)
            g.wait_ge(C_g, 8)
            g.affine_select(out=hmask[:], in_=hmask[:], compare_op=ALU.is_ge, fill=0.0, base=DH - 1,
                            pattern=[[DH, HP]], channel_multiplier=-1).then_inc(C_g, 1)
            g.affine_select(out=tri[:], in_=tri[:], compare_op=ALU.is_ge, fill=0.0, base=-1,
                            pattern=[[1, P]], channel_multiplier=-1).then_inc(C_g, 1)
            g.affine_select(out=lower[:], in_=lower[:], compare_op=ALU.is_ge, fill=0.0, base=-1,
                            pattern=[[1, NE], [-1, NE]], channel_multiplier=0).then_inc(C_g, 1)

            def ramp(t, n, step, base, per):
                return g.iota(t, pattern=[[step, n]], base=base, channel_multiplier=per,
                              allow_small_or_imprecise_dtypes=True)
            ramp(iota8[:], NE, 1, 0, 0)
            ramp(eR[:], NE, REGION, 0, 0)
            ramp(thr[:], NT, P, 0, 0).then_inc(C_g, 1)
            ramp(jrow[:], MAX_BLOCKS, 1, 0, 0).then_inc(C_g, 1)
            g.memset(v_pad[:], 0.0).then_inc(C_g, 1)

            def rstd(mv, ve, out_, ready, s_ve, v_ve, s_out):
                g.tensor_scalar(ve, mv, 1e-5, None, ALU.add).then_inc(s_ve, 1)
                g.wait_ge(s_ve, v_ve)
                g.tensor_tensor(out_, ve, ready, ALU.pow).then_inc(s_out, 1)

            for l in range(2):
                def ln1_rstd(B):
                    apart(g, g_passed, (d_mv1, 2 * B + 2))
                    rstd(mv1[:, :, 1], ve1[:], rstd1[:], mhalf[:], g_ve1, B + 1, g_rs1)

                def add_bias(B, b):
                    g.wait_ge(d_xn1, B + 1)
                    xb = x_sb[:, bass.ds(2 * b, 2), :]
                    g.tensor_tensor(xb, xb, bo[:, l, :].unsqueeze(1).to_broadcast([P, QT, D]), ALU.add).then_inc(g_bias, 1)

                def gather(B):
                    apart(g, g_passed, (d_yn, B + 1))
                    for t in range(2):
                        for k in range(TOPK):
                            g.indirect_dma_start(yg[:, 0, t, k, :], None, ys_dram,
                                                 bass.IndirectOffsetOnAxis(ap=ynow[:, t, k:k + 1], axis=0)
                                                 ).then_inc(D_ga, 16)

                def ln2_rstd(U, qt):
                    apart(g, g_passed, (d_mv2, U + 1))
                    rstd(mv2[:, qt, 1:2], ve2[:, qt:qt + 1], rstd2[:, qt:qt + 1], mhalf[:, 0:1], g_ve2, U + 1, g_rs2)

                if l == 1:
                    for u in range(U3):
                        g.wait_ge(D_y[u], 16 * MAX_BLOCKS // U3)
                    gather(0)
                def keys(B, cur):
                    g.wait_ge(a_k, B + 1)
                    if cur:
                        g.wait_ge(p_s, 4 * B)
                    g.tensor_tensor(kbd, kT[:, :, :].unsqueeze(2).to_broadcast([P, KT, HP, K]),
                                    hmask[:, :].unsqueeze(1).unsqueeze(3).to_broadcast([P, KT, HP, K]),
                                    ALU.mult).then_inc(g_kbd, 1)

                keys(NB * l, False)
                ln1_rstd(NB * l)
                add_bias(NB * l, 0)

                def step(b, cur, nxt, nn, prev):
                    B = NB * l + b
                    if nxt and cur:
                        keys(B + 1, cur)
                    if nn and l == 1:
                        gather(b + 2)
                    if cur:
                        ln2_rstd(2 * B, 0)
                    if nn:
                        ln1_rstd(B + 2)
                    if prev and not cur:
                        g.wait_ge(p_s, 4 * NB * (l + 1))
                        g.memset(zrow, 0.0).then_inc(g_z, 1)
                    if prev:
                        apart(g, g_passed, (d_keep, B), (d_slot, B))
                        for t in range(2):
                            for k in range(TOPK):
                                g.indirect_dma_start(xs_dram, bass.IndirectOffsetOnAxis(ap=slot_now[:, t, k:k + 1], axis=0),
                                                     kept[:, t, :], None).then_inc(D_sc, 16)
                    if nxt:
                        apart(g, g_passed, (d_v, B + 2), (p_pv, 8 * B + 8 if cur else 0))
                        for s in range(2):
                            i = g.tensor_copy(v_pad[0:K, s::2, s * DH:(s + 1) * DH],
                                              v_tmp[0:K, :].rearrange("p (g s d) -> p s g d", s=2, d=DH)[:, s, :, :])
                        i.then_inc(g_vp, 1)
                    if nn:
                        add_bias(B + 2, b + 2)
                    if cur:
                        ln2_rstd(2 * B + 1, 1)
                run_steps(g, l, step)

                def store(j, u):
                    g.wait_ge(e_y, MAX_BLOCKS * l + j + 1)
                    g.dma_start(ys_dram[bass.ds(j * P, P), :], y_sb[:, u, :]).then_inc(D_y[u], 16)
                with g.Fori(0, MAX_BLOCKS // U3) as i:
                    for u in range(U3):
                        store(U3 * i + u, u)

            for u in range(U3):
                g.wait_ge(D_y[u], 2 * 16 * MAX_BLOCKS // U3)
            g.wait_ge(d_yi, 1)
            for b in range(NB):
                for t in range(2):
                    for k in range(TOPK):
                        g.indirect_dma_start(yg[:, b, t, k, :], None, ys_dram,
                                             bass.IndirectOffsetOnAxis(ap=yslot_i[:, 2 * b + t, k:k + 1], axis=0)
                                             ).then_inc(D_gl[b], 16)

        @block.scalar
        def _(a):
            a.wait_ge(L_small, 16 * NSMALL)
            a.activation(tg[:, :], gates[:, :], ACT.Tanh).then_inc(C_a, 1)
            a.mul(bq4[:, :, :], bq[:, :, :], 0.25).then_inc(C_a, 1)
            a.wait_ge(C_a, 2)
            a.wait_ge(L_w, 64)
            a.wait_ge(L_x[0], 16)
            load_experts(a, 0, range(NE - 1))

            for l in range(2):
                def ctx_evac(B):
                    a.wait_ge(p_ctx, B + 1)
                    if not (isinstance(B, int) and B == 0):
                        a.wait_ge(p_v, B)
                    a.copy(ctxT[:, :, :], ps[:, 7, 0:KT * K].rearrange("p (k n) -> p k n", k=KT)).then_inc(a_ctx, 1)

                def t_evac(U, c):
                    a.wait_ge(p_t, 4 * U + c + 1)
                    need(a, p_pv, 4 * U + c - 1)
                    a.copy(pT[0:K, c % 2, :], ps[0:K, 4 + c % 2, :]).then_inc(a_t, 1)

                def exp(U, qt, h):
                    a.wait_ge(d_sub, 2 * U + h + 1)
                    need(a, p_t, 4 * U - 4)
                    a.activation(p_buf[:, qt, h * HP * K:(h + 1) * HP * K], s_sb[:, h, :], ACT.Exp).then_inc(a_exp, 1)

                def x2_evac(U):
                    a.wait_ge(p_x2, U + 1)
                    need(a, p_lg, U)
                    a.copy(xn2T[:, :, :], ps[:, 7, 0:KT * P].rearrange("p (k n) -> p k n", k=KT)).then_inc(a_x2, 1)

                def lg_evac(U, B, qt):
                    a.wait_ge(p_lg, U + 1)
                    need(a, d_mask, B)
                    a.copy(logits[:, qt, :], ps[:, 7, 0:NE]).then_inc(a_lg, 1)

                def spread(U, qt):
                    a.wait_ge(d_ri, 2 * U + 2)
                    need(a, p_rt, U)
                    a.copy(rinv16[:, :, :], rinv[:, qt, :].unsqueeze(2).to_broadcast([P, H, DH])).then_inc(a_re, 1)

                def rt_evac(U):
                    a.wait_ge(p_rt, U + 1)
                    need(a, d_c, U)
                    a.copy(rT[:, :, :], ps[:, 6, KT * P:2 * KT * P].rearrange("p (k q) -> p k q", k=KT)).then_inc(a_rt, 1)

                ctx_evac(NB * l)

                def step(b, cur, nxt, nn, prev):
                    B = NB * l + b
                    U = 2 * B
                    if cur:
                        t_evac(U, 0)
                        t_evac(U, 1)
                    if nxt:
                        a.wait_ge(p_k, B + 2)
                        need(a, g_kbd, B + 1)
                        for m in range(KT):
                            i = a.activation(kT[:, m, :], ps[:, 7, m * K:(m + 1) * K], ACT.Identity, bias=bk[:, l, m:m + 1])
                        i.then_inc(a_k, 1)
                    if nn and not cur:
                        ctx_evac(B + 2)
                    if cur:
                        t_evac(U, 2)
                        spread(U, 0)
                    if nxt:
                        a.wait_ge(p_xnT, B + 2)
                        need(a, p_q, B + 1)
                        a.copy(xn1T[:, :, :], ps[:, 7, :].rearrange("p (k n) -> p k n", k=KT)).then_inc(a_xnT, 1)
                    if cur:
                        t_evac(U, 3)
                        exp(U + 1, 1, 1)
                    if nxt:
                        a.wait_ge(p_q, B + 2)
                        need(a, p_s, 4 * B + 4)
                        for m in range(KT):
                            i = a.activation(qT[:, m, :], ps[:, 7, m * S:(m + 1) * S], ACT.Identity,
                                             bias=bq4[:, l, m:m + 1], scale=0.25)
                        i.then_inc(a_q, 1)
                    if cur:
                        rt_evac(U)
                    if prev:
                        x2_evac(U - 1)
                        lg_evac(U - 1, B - 1, 1)
                    if nxt:
                        exp(U + 2, 0, 0)
                    if cur:
                        t_evac(U + 1, 0)
                        t_evac(U + 1, 1)
                        spread(U + 1, 1)
                        t_evac(U + 1, 2)
                    if nn and cur:
                        ctx_evac(B + 2)
                    if cur:
                        t_evac(U + 1, 3)
                    if nxt:
                        exp(U + 2, 0, 1)
                    if cur:
                        rt_evac(U + 1)
                        x2_evac(U)
                        lg_evac(U, B, 0)
                    if nxt:
                        exp(U + 3, 1, 0)
                run_steps(a, l, step)

                if l == 0:
                    a.wait_ge(p_t, 4 * NT)
                    a.wait_ge(p_lg, NT)
                    load_experts(a, 0, [NE - 1])      
                a.wait_ge(d_f, 17 + 22 * l)
                a.activation(top8[:, :, :], top8[:, :, :], ACT.Exp).then_inc(f_exp, 1)

                def blk(j, u, i, first, last):
                    J = MAX_BLOCKS * l + j
                    nq = len(UP[l]) // 2 or 1
                    if l == 0:
                        for q in range(2):
                            a.wait_ge(b_up, 4 * j + 2 * q + 1)
                            need(a, e_h, 2 * j - 1 + q)
                            a.activation(act_sb[:, 344 * q:344 * q + 344], ps[:, 2 * q, 0:344], ACT.Silu).then_inc(e_act, 1)
                    else:
                        a.wait_ge(b_up, 4 * MAX_BLOCKS + j + 1)
                        a.wait_ge(e_h, 2 * MAX_BLOCKS + j)
                        a.activation(act_sb[:, 0:HID[1]], ps[:, 0, 0:HID[1]], ACT.Relu).then_inc(e_act, 1)
                    a.wait_ge(b_hT, 2 * j + 1 if l == 0 else 2 * MAX_BLOCKS + j + 1)
                    need(a, b_y, J)
                    n = min(4, KD[l])
                    a.copy(hT[:, 0:n, :], ps[:, 4, 0:n * P].rearrange("p (c n) -> p c n", c=n)).then_inc(e_hT, 1)
                run_blocks(a, l, blk)

        @block.vector
        def _(v):
            v.memset(cumb[:], 0.0).then_inc(C_v, 1)
            v.wait_ge(L_small, 16 * NSMALL)
            v.tensor_scalar(mask_bc, mask_bc, NEG, None, ALU.mult).then_inc(C_v, 1)
            v.memset(mask3[:], 0.0).then_inc(C_v, 1)
            v.wait_ge(C_a, 2)
            for l in range(2):
                v.tensor_scalar(bo[:, l, :], bo[:, l, :], tg[:, l:l + 1], None, ALU.mult).then_inc(C_v, 1)
            v.wait_ge(C_v, 5)
            for part in range(3):
                v.tensor_copy(mask_hi, mask_bc).then_inc(d_m, 1)
                v.wait_ge(d_m, 3 * part + 1)
                v.tensor_copy(mask3[32 * part:32 * part + 1, :, :], mask_hi[32 * part:32 * part + 1, :, :]).then_inc(d_m, 1)
                v.tensor_tensor(mask_bc, mask_bc, mask_hi, ALU.subtract).then_inc(d_m, 1)
                v.wait_ge(d_m, 3 * part + 3)
            v.wait_ge(C_g, 14)

            for l in range(2):
                F = 22 * l

                def ln1_stats(B, b, loaded=None):
                    if loaded is not None:
                        v.wait_ge(loaded, 16)
                    for t in range(2):
                        v.bn_stats(st1[:, t, :], x_sb[:, 2 * b + t, :] if isinstance(b, int) else
                                   x_sb[:, bass.ds(2 * b + t, 1), :]).then_inc(d_st1, 1)
                    for t in range(2):
                        apart(v, d_passed, (d_st1, 2 * B + t + 1))
                        v.bn_aggr(mv1[:, t, :], st1[:, t, :]).then_inc(d_mv1, 1)

                def ln1_apply(B, b):
                    v.wait_ge(g_rs1, B + 1)
                    v.wait_ge(d_mv1, 2 * B + 2)
                    need(v, p_xnT, B)
                    for t in range(2):
                        i = v.tensor_scalar(xn1[:, t:t + 1, :], x_sb[:, bass.ds(2 * b + t, 1), :], mv1[:, t, 0:1],
                                            rstd1[:, t:t + 1], ALU.subtract, ALU.mult)
                    i.then_inc(d_xn1, 1)

                def combine(B, b, gathered, value, gb=0):
                    v.wait_ge(gathered, value)
                    for k in range(TOPK):
                        for t in range(2):
                            if k:
                                v.wait_ge(d_c1, 2 * B + t + 1)
                            xt = x_sb[:, bass.ds(2 * b + t, 1), :]
                            v.scalar_tensor_tensor(
                                out=xt, in0=yg[:, gb, t, k:k + 1, :], scalar=wcomb[:, bass.ds(2 * b + t, 1), k:k + 1].rearrange("p a b -> p (a b)"),
                                in1=xt, op0=ALU.mult, op1=ALU.add).then_inc(d_comb if k else d_c1, 1)

                def next_index(B, b):
                    apart(v, d_passed, (D_ga, 64 * B))
                    v.tensor_copy(ynow[:, :, :], yslot[:, bass.ds(2 * b, 2), :]).then_inc(d_yn, 1)

                def shift(U, h):
                    v.wait_ge(p_s, 2 * U + h + 1)
                    sps = ps[:, 2 * h:2 * h + 2, 0:CH].rearrange("p c (h k) -> p c h k", h=4)
                    s4 = s_sb[:, h, :].rearrange("p (c h k) -> p c h k", c=2, h=4)
                    m4 = mx[:, h, :].rearrange("p (c h) -> p c h", c=2)
                    need(v, a_exp, 2 * U + h - 1)
                    v.tensor_reduce(m4, sps, X, ALU.max).then_inc(d_max, 1)
                    v.wait_ge(d_max, 2 * U + h + 1)
                    v.tensor_tensor(s4, sps, m4.unsqueeze(3).to_broadcast([P, 2, 4, K]),
                                    ALU.subtract).then_inc(d_sub, 1)

                def totals(U, qt, h):
                    v.wait_ge(a_exp, 2 * U + h + 1)
                    hs = slice(h * HP, (h + 1) * HP)
                    v.tensor_reduce(rsum[:, qt, hs], p_buf[:, qt, h * HP * K:(h + 1) * HP * K]
                                    .rearrange("p (h k) -> p h k", h=HP), X, ALU.add).then_inc(d_sum, 1)
                    v.wait_ge(d_sum, 2 * U + h + 1)
                    need(v, a_re, U - 1)
                    v.reciprocal(rinv[:, qt, hs], rsum[:, qt, hs]).then_inc(d_ri, 1)

                def divide(U):
                    v.wait_ge(p_pv, 4 * U + 4)
                    v.wait_ge(a_rt, U + 1)
                    need(v, p_o, U)
                    v.tensor_tensor(cT[:, :, :], ps[:, 6, 0:KT * P].rearrange("p (k q) -> p k q", k=KT), rT[:, :, :],
                                    ALU.mult).then_inc(d_c, 1)

                def residual(U, T, B, qt):
                    v.wait_ge(p_o, U + 1)
                    v.wait_ge(g_bias, B + 1)
                    xt = x_sb[:, bass.ds(T, 1), :]
                    v.scalar_tensor_tensor(out=xt, in0=ps[:, 7, 0:D].unsqueeze(1), scalar=tg[:, l:l + 1], in1=xt,
                                           op0=ALU.mult, op1=ALU.add).then_inc(d_o, 1)
                    apart(v, d_passed, (d_o, U + 1))
                    v.bn_stats(st2[:, qt, :], xt).then_inc(d_st2, 1)
                    apart(v, d_passed, (d_st2, U + 1))
                    v.bn_aggr(mv2[:, qt, :], st2[:, qt, :]).then_inc(d_mv2, 1)

                def keep(B):
                    need(v, D_sc, 64 * B)
                    v.wait_ge(d_xn2, 2 * B + 2)
                    v.tensor_copy(kept[:, :, :], xn2[:, :, :]).then_inc(d_keep, 1)

                def ln2_apply(U, T, B, qt):
                    v.wait_ge(g_rs2, U + 1)
                    v.wait_ge(d_mv2, U + 1)
                    if qt == 0:
                        need(v, d_keep, B)
                    need(v, p_x2, U - 1)
                    v.tensor_scalar(xn2[:, qt:qt + 1, :], x_sb[:, bass.ds(T, 1), :], mv2[:, qt, 0:1], rstd2[:, qt:qt + 1],
                                    ALU.subtract, ALU.mult).then_inc(d_xn2, 1)

                def route1(B, b):
                    apart(v, d_passed, (a_lg, 2 * B + 2))
                    for t in range(2):
                        v.max(topnow[:, t, :], logits[:, t, :]).then_inc(d_r1, 1)
                    for t in range(2):
                        apart(v, d_passed, (d_r1, 7 * B + t + 1))
                        v.max_index(idx8[:, t, :], topnow[:, t, :], logits[:, t, :]).then_inc(d_r1, 1)
                    v.tensor_copy(top8[:, bass.ds(2 * b, 2), :], topnow[:, :, :]).then_inc(d_r1, 1)
                    v.wait_ge(d_r1, 7 * B + 5)
                    v.tensor_copy(idxf[:, :, :], idx8[:, :, 0:TOPK]).then_inc(d_r1, 1)
                    v.wait_ge(d_r1, 7 * B + 6)
                    oh = onehot[:, bass.ds(2 * b, 2), :, :]
                    v.tensor_tensor(oh, iota8[:, :].unsqueeze(1).unsqueeze(1).to_broadcast([P, 2, TOPK, NE]),
                                    idxf[:, :, :].unsqueeze(3).to_broadcast([P, 2, TOPK, NE]), ALU.is_equal).then_inc(d_r1, 1)
                    v.wait_ge(d_r1, 7 * B + 7)
                    need(v, p_rk, B)
                    need(v, d_cum, 2 * B)
                    v.tensor_tensor(maskb[:, :, :], oh[:, :, 0, :], oh[:, :, 1, :], ALU.add).then_inc(d_mask, 1)

                def route2(B, b):
                    v.wait_ge(p_rk, B + 1)
                    v.tensor_tensor(rk[:, :, :], ps[:, 7, 0:2 * NE].rearrange("p (t e) -> p t e", t=2),
                                    eR[:, :].unsqueeze(1).to_broadcast([P, 2, NE]), ALU.add).then_inc(d_rk, 1)
                    v.wait_ge(d_rk, B + 1)
                    v.tensor_tensor(prod[:, :, :, :], onehot[:, bass.ds(2 * b, 2), :, :],
                                    rk[:, :, :].unsqueeze(2).to_broadcast([P, 2, TOPK, NE]), ALU.mult).then_inc(d_r2, 1)
                    v.tensor_tensor(cumb[:, :], cumb[:, :], maskb[:, 0, :], ALU.add).then_inc(d_cum, 1)
                    v.wait_ge(d_r2, 2 * B + 1)
                    v.tensor_reduce(slotf[:, bass.ds(2 * b, 2), :], prod[:, :, :, :], X, ALU.add).then_inc(d_r2, 1)
                    v.wait_ge(d_cum, 2 * B + 1)
                    v.tensor_tensor(cumb[:, :], cumb[:, :], maskb[:, 1, :], ALU.add).then_inc(d_cum, 1)
                    apart(v, d_passed, (d_r2, 2 * B + 2), (D_sc, 64 * B))
                    v.tensor_copy(slot_now[:, :, :], slotf[:, bass.ds(2 * b, 2), :]).then_inc(d_slot, 1)

                def value_bias(B):
                    v.wait_ge(p_v, B + 1)
                    need(v, g_vp, B)
                    v.tensor_tensor(v_tmp[0:K, :], ps[0:K, 7, 0:D], bv[0:K, l, :], ALU.add).then_inc(d_v, 1)

                if l == 1:
                    next_index(0, 0)
                    combine(0, 0, D_ga, 64)
                    v.wait_ge(d_comb, 2)
                ln1_stats(NB * l, 0, L_x[0] if l == 0 else None)
                ln1_apply(NB * l, 0)

                def step(b, cur, nxt, nn, prev):
                    B = NB * l + b
                    U = 2 * B
                    if nn and l == 1:
                        next_index(b + 2, b + 2)
                    if cur:
                        totals(U + 1, 1, 0)
                        totals(U + 1, 1, 1)
                    if prev:
                        keep(B - 1)
                    if cur:
                        divide(U)
                    if nxt and not cur:
                        value_bias(B + 1)
                    if nxt:
                        shift(U + 2, 0)
                    if nxt and cur:
                        value_bias(B + 1)
                    if prev:
                        route1(B - 1, b - 1)
                    if cur:
                        residual(U, 2 * b, B, 0)
                    if nxt:
                        shift(U + 2, 1)
                    if cur:
                        ln2_apply(U, 2 * b, B, 0)
                    if nn:
                        if l == 1:
                            combine(b + 2, b + 2, D_ga, 64 * (b + 3))
                            apart(v, d_passed, (d_comb, 2 * (b + 2) + 2))
                        if l == 0 and not cur:
                            v.wait_ge(L_x[1], 16)
                        if l == 0 and cur and not prev:
                            v.wait_ge(L_x[2], 16)
                            v.wait_ge(L_x[3], 16)
                        ln1_stats(B + 2, b + 2)
                    if prev:
                        route2(B - 1, b - 1)
                    if nn:
                        ln1_apply(B + 2, b + 2)
                    if cur:
                        divide(U + 1)
                    if nxt:
                        shift(U + 3, 0)
                        totals(U + 2, 0, 0)
                        totals(U + 2, 0, 1)
                    if cur:
                        residual(U + 1, 2 * b + 1, B, 1)
                    if nxt:
                        shift(U + 3, 1)
                    if cur:
                        ln2_apply(U + 1, 2 * b + 1, B, 1)
                run_steps(v, l, step)

                bc = lambda t, n: t.unsqueeze(1).to_broadcast([P, n, NE])
                v.wait_ge(d_r1, 7 * NB * (l + 1))
                v.tensor_copy(zsum[:, :], top8[:, :, 0]).then_inc(d_tm, 1)
                v.wait_ge(f_cnt, l + 1)
                v.tensor_copy(cnt[:, :], ps[:, 7, 0:NE]).then_inc(d_f, 1)
                v.wait_ge(d_f, F + 1)
                v.tensor_tensor(pad_i[:, :], cnt[:, :], eR[:, :], ALU.add).then_inc(d_f, 1)
                c16 = cmpb[:, 0:NE * NT].rearrange("p (e t) -> p e t", e=NE)
                v.tensor_tensor(c16, cnt[:, :].unsqueeze(2).to_broadcast([P, NE, NT]),
                                thr[:, :].unsqueeze(1).to_broadcast([P, NE, NT]), ALU.is_gt).then_inc(d_f, 1)
                v.wait_ge(d_f, F + 3)
                v.tensor_reduce(nb[:, :], c16, X, ALU.add).then_inc(d_f, 1)
                v.wait_ge(d_f, F + 4)
                c8 = cmpb[:, 0:NE * NE].rearrange("p (e f) -> p e f", e=NE)
                v.tensor_tensor(c8, lower[:, :, :], bc(nb[:, :], NE), ALU.mult).then_inc(d_f, 1)
                v.wait_ge(d_f, F + 5)
                v.tensor_reduce(sbk[:, :], c8, X, ALU.add).then_inc(d_f, 1)
                v.wait_ge(d_f, F + 6)
                v.tensor_scalar(tot1[:, :], nb[:, NE - 1:NE], sbk[:, NE - 1:NE], -1.0, ALU.add, ALU.add).then_inc(d_f, 1)
                v.wait_ge(d_f, F + 7)
                v.tensor_scalar(jc[:, :], jrow[:, :], tot1[:, 0:1], None, ALU.min).then_inc(d_f, 1)
                v.wait_ge(d_f, F + 8)
                cj = cmpb[:, :].rearrange("p (j e) -> p j e", e=NE)
                v.tensor_tensor(cj, jc[:, :].unsqueeze(2).to_broadcast([P, MAX_BLOCKS, NE]),
                                bc(sbk[:, :], MAX_BLOCKS), ALU.is_ge).then_inc(d_f, 1)
                v.wait_ge(d_f, F + 9)
                v.tensor_reduce(be[:, :], cj, X, ALU.add).then_inc(d_f, 1)
                v.wait_ge(d_f, F + 10)
                v.tensor_tensor(cj, cj, bc(sbk[:, :], MAX_BLOCKS), ALU.mult).then_inc(d_f, 1)
                v.wait_ge(d_f, F + 11)
                v.tensor_reduce(sbx[:, :], cj, X, ALU.max).then_inc(d_f, 1)
                v.wait_ge(d_f, F + 12)
                v.tensor_tensor(jc[:, :], jc[:, :], sbx[:, :], ALU.subtract).then_inc(d_f, 1)
                v.wait_ge(d_f, F + 13)
                v.tensor_scalar(jc[:, :], jc[:, :], float(P), -float(REGION), ALU.mult, ALU.add).then_inc(d_f, 1)
                v.wait_ge(d_f, F + 14)
                v.scalar_tensor_tensor(out=xrow_i[:, :], in0=be[:, :], scalar=float(REGION), in1=jc[:, :],
                                       op0=ALU.mult, op1=ALU.add).then_inc(d_f, 1)
                v.tensor_scalar(woff_i[:, :], be[:, :], float(EW[l]), -float(EW[l]), ALU.mult, ALU.add).then_inc(d_f, 1)
                v.wait_ge(d_tm, l + 1)
                v.tensor_tensor(top8[:, :, :], top8[:, :, :], zsum[:, :].unsqueeze(2).to_broadcast([P, NT, 8]),
                                ALU.subtract).then_inc(d_f, 1)
                v.scalar_tensor_tensor(out=yoff[:, :], in0=sbk[:, :], scalar=float(P), in1=eR[:, :],
                                       op0=ALU.mult, op1=ALU.subtract).then_inc(d_f, 1)
                v.wait_ge(d_f, F + 18)
                c32 = cmpb[:, 0:NT * TOPK * NE].rearrange("p (n e) -> p n e", e=NE)
                v.tensor_tensor(c32, onehot[:, :, :, :].rearrange("p t k e -> p (t k) e"), bc(yoff[:, :], NT * TOPK),
                                ALU.mult).then_inc(d_f, 1)
                v.wait_ge(d_f, F + 19)
                v.tensor_reduce(yslot[:, :, :].rearrange("p t k -> p (t k)"), c32, X, ALU.add).then_inc(d_f, 1)
                v.wait_ge(d_f, F + 20)
                v.tensor_tensor(yslot[:, :, :], yslot[:, :, :], slotf[:, :, :], ALU.add).then_inc(d_f, 1)
                v.memset(cumb[:], 0.0).then_inc(d_f, 1)
                if l == 1:
                    v.wait_ge(d_f, F + 21)
                    v.tensor_copy(yslot_i[:, :, :], yslot[:, :, :]).then_inc(d_yi, 1)

                def blk(j, u, i, first, last):
                    J = MAX_BLOCKS * l + j
                    if first:
                        x_evac(J, j)
                    if l == 0:
                        for q in range(2):
                            v.wait_ge(e_act, 2 * j + q + 1)
                            v.wait_ge(b_up, 4 * j + 2 * q + 2)
                            need(v, b_hT, 2 * j)
                            v.tensor_tensor(h_sb[:, 344 * q:344 * q + 344], act_sb[:, 344 * q:344 * q + 344],
                                            ps[:, 2 * q + 1, 0:344], ALU.mult).then_inc(e_h, 1)
                    else:
                        v.wait_ge(e_act, 2 * MAX_BLOCKS + j + 1)
                        v.wait_ge(b_hT, 2 * MAX_BLOCKS + j)
                        v.tensor_tensor(h_sb[:, 0:HID[1]], act_sb[:, 0:HID[1]], act_sb[:, 0:HID[1]], ALU.mult).then_inc(e_h, 1)
                    if not last:
                        x_evac(J + 1, j + 1)
                    if not first:
                        y_evac(J - 1, (u - 1) % U3, i)
                    if l == 0:
                        v.wait_ge(b_hT, 2 * j + 2)
                        need(v, b_y, j)
                        v.tensor_copy(hT[:, 4, :], ps[:, 5, 0:P])
                        r = DOWN[0][5][1]
                        v.tensor_copy(hT[0:r, 5, :], ps[0:r, 5, P:2 * P]).then_inc(e_hTv, 1)
                    if last:
                        y_evac(J, u, i)

                def x_evac(J, j):
                    v.wait_ge(b_x, J + 1)
                    need(v, b_up, 4 * j if l == 0 else 4 * MAX_BLOCKS + j)
                    v.tensor_copy(xgT[:, :, :], ps[:, 7, 0:KT * P].rearrange("p (k n) -> p k n", k=KT)).then_inc(e_x, 1)

                def y_evac(J, u, i):
                    v.wait_ge(b_y, J + 1)
                    need(v, D_y[u], 16 * i + 16 * (MAX_BLOCKS // U3) * l)
                    v.tensor_copy(y_sb[:, u, :], ps[:, 6, 0:D]).then_inc(e_y, 1)

                v.wait_ge(f_exp, l + 1)
                e01 = top8[:, :, 0:TOPK]
                v.tensor_reduce(zsum[:, :], top8[:, :, :], X, ALU.add).then_inc(C_v, 1)
                v.tensor_tensor(wcomb[:, :, 0], top8[:, :, 0], top8[:, :, 1], ALU.add).then_inc(C_v, 1)
                v.wait_ge(C_v, 5 + 6 * l + 2)
                v.scalar_tensor_tensor(out=zsum[:, :], in0=zsum[:, :], scalar=1e-6 if l == 0 else 0.0, in1=wcomb[:, :, 0],
                                       op0=ALU.mult, op1=ALU.add).then_inc(C_v, 1)
                v.wait_ge(C_v, 5 + 6 * l + 3)
                v.reciprocal(zsum[:, :], zsum[:, :]).then_inc(C_v, 1)
                v.wait_ge(C_v, 5 + 6 * l + 4)
                v.tensor_scalar(zsum[:, :], zsum[:, :], tg[:, 2 + l:3 + l], None, ALU.mult).then_inc(C_v, 1)
                v.wait_ge(C_v, 5 + 6 * l + 5)
                v.tensor_tensor(wcomb[:, :, :], e01, zsum[:, :].unsqueeze(2).to_broadcast([P, NT, TOPK]), ALU.mult).then_inc(C_v, 1)
                v.wait_ge(C_v, 5 + 6 * l + 6)

                run_blocks(v, l, blk)

            for b in range(NB):
                combine(b + NB, b, D_gl[b], 64, b)

        @block.tensor
        def _(t):
            t.wait_ge(C_g, 14)

            for l in range(2):
                def ctx_t(B):
                    t.wait_ge(L_ctx, 16 * (B + 1))
                    for k in range(KT):
                        i = t.transpose(ps[:, 7, k * K:(k + 1) * K], ctx_sb[0:K, k * P:(k + 1) * P], ident[0:K, 0:K])
                    i.then_inc(p_ctx, 1)

                def k_proj(B):
                    t.wait_ge(a_ctx, B + 1)
                    need(t, d_o, 2 * B - 2)
                    for m in range(KT):
                        for k in range(KT):
                            i = t.matmul(ps[:, 7, m * K:(m + 1) * K], w_att[:, 1, k, m * P:(m + 1) * P], ctxT[:, k, :],
                                         start=(k == 0), stop=(k == KT - 1))
                    i.then_inc(p_k, 1)

                def x_t(B):
                    t.wait_ge(d_xn1, B + 1)
                    t.wait_ge(a_k, B + 1)
                    for k in range(KT):
                        for q in range(QT):
                            i = t.transpose(ps[:, 7, k * S + q * P:k * S + (q + 1) * P], xn1[:, q, k * P:(k + 1) * P], ident[:, :])
                    i.then_inc(p_xnT, 1)

                def q_proj(B):
                    t.wait_ge(a_xnT, B + 1)
                    for m in range(KT):
                        for k in range(KT):
                            i = t.matmul(ps[:, 7, m * S:(m + 1) * S], w_att[:, 0, k, m * P:(m + 1) * P], xn1T[:, k, :],
                                         start=(k == 0), stop=(k == KT - 1))
                    i.then_inc(p_q, 1)

                def v_proj(B):
                    for k in range(KT):
                        i = t.matmul(ps[0:K, 7, 0:D], ctxT[:, k, :], w_att[:, 2, k, :], start=(k == 0), stop=(k == KT - 1))
                    i.then_inc(p_v, 1)

                def score(b, U, qt, c):
                    h = c // 2
                    if c % 2 == 0:
                        need(t, d_sub, 2 * U + h - 1)
                    if l == 0:
                        t.matmul(ps[:, c, 0:CH].rearrange("p (h k) -> p h k", h=4), ones[0:96, :],
                                 mask3[0:96, bass.ds(b, 1), :].to_broadcast([96, 4, K]), start=True, stop=False)
                    i = t.matmul(ps[:, c, 0:CH], qT[:, h, qt * P:(qt + 1) * P],
                                 kbd[:, h, 4 * (c % 2):4 * (c % 2) + 4, :], start=(l == 1), stop=True)
                    if c % 2 == 1:
                        i.then_inc(p_s, 1)

                def probs_t(U, qt, c):
                    if c % 2 == 0:
                        t.wait_ge(a_exp, 2 * U + c // 2 + 1)
                    need(t, a_t, 4 * U + c - 1)
                    for h in range(4):
                        i = t.transpose(ps[0:K, 4 + c % 2, h * P:(h + 1) * P],
                                        p_buf[:, qt, (4 * c + h) * K:(4 * c + h + 1) * K], ident[:, :])
                    i.then_inc(p_t, 1)

                def values(U, B, c):
                    t.wait_ge(a_t, 4 * U + c + 1)
                    if c == 0:
                        t.wait_ge(g_vp, B + 1)
                        need(t, d_c, U)
                    for h4 in range(4):
                        h = 4 * c + h4
                        g4 = (h % HP) // 2
                        i = t.matmul(ps[32 * g4:32 * g4 + 32, 6, (h // HP) * P:(h // HP + 1) * P], v_pad[0:K, h, :],
                                     pT[0:K, c % 2, h4 * P:(h4 + 1) * P], start=(h % 2 == 0), stop=(h % 2 == 1))
                    i.then_inc(p_pv, 1)

                def rinv_t(U):
                    t.wait_ge(a_re, U + 1)
                    need(t, a_rt, U)
                    for k in range(KT):
                        i = t.transpose(ps[:, 6, (KT + k) * P:(KT + k + 1) * P],
                                        rinv16[:, k * HP:(k + 1) * HP, :].rearrange("p h d -> p (h d)"), ident[:, :])
                    i.then_inc(p_rt, 1)

                def out_proj(U):
                    t.wait_ge(d_c, U + 1)
                    for k in range(KT):
                        i = t.matmul(ps[:, 7, 0:D], cT[:, k, :], w_att[:, 3, k, :], start=(k == 0), stop=(k == KT - 1))
                    i.then_inc(p_o, 1)

                def x2_t(U, qt):
                    t.wait_ge(d_xn2, U + 1)
                    for k in range(KT):
                        i = t.transpose(ps[:, 7, k * P:(k + 1) * P], xn2[:, qt, k * P:(k + 1) * P], ident[:, :])
                    i.then_inc(p_x2, 1)

                def route(U):
                    t.wait_ge(a_x2, U + 1)
                    for k in range(KT):
                        i = t.matmul(ps[:, 7, 0:NE], xn2T[:, k, :], wr[:, l, k, :], start=(k == 0), stop=(k == KT - 1))
                    i.then_inc(p_lg, 1)

                def ranks(B):
                    t.wait_ge(d_mask, B + 1)
                    need(t, d_cum, 2 * B)
                    t.matmul(ps[:, 7, 0:NE], tri[:, :], maskb[:, 0, :], start=True, stop=False)
                    t.matmul(ps[:, 7, 0:NE], ones[:, :], cumb[:, :], start=False, stop=True)
                    t.matmul(ps[:, 7, NE:2 * NE], tri[:, :], maskb[:, 1, :], start=True, stop=False)
                    t.matmul(ps[:, 7, NE:2 * NE], ones[:, :], maskb[:, 0, :], start=False, stop=False)
                    t.matmul(ps[:, 7, NE:2 * NE], ones[:, :], cumb[:, :], start=False, stop=True).then_inc(p_rk, 1)

                if l == 1:
                    t.wait_ge(e_x, MAX_BLOCKS)
                    t.wait_ge(e_y, MAX_BLOCKS)
                t.wait_ge(L_w, 64 * (l + 1))
                t.wait_ge(d_m, 9)
                ctx_t(NB * l)

                def step(b, cur, nxt, nn, prev):
                    B = NB * l + b
                    U = 2 * B
                    if cur:
                        probs_t(U, 0, 0)
                        probs_t(U, 0, 1)
                        values(U, B, 0)
                    if nxt:
                        k_proj(B + 1)
                    if nxt and not cur:
                        t.wait_ge(a_k, B + 2)
                        v_proj(B + 1)
                        t.wait_ge(d_v, B + 2)
                        ctx_t(B + 2)
                        t.wait_ge(a_ctx, B + 3)
                    if cur:
                        probs_t(U, 0, 2)
                        values(U, B, 1)
                    if nxt:
                        x_t(B + 1)
                    if cur:
                        probs_t(U, 0, 3)
                        values(U, B, 2)
                    if nxt:
                        q_proj(B + 1)
                    if cur:
                        values(U, B, 3)
                        rinv_t(U)
                    if nxt:
                        t.wait_ge(a_q, B + 2)
                    if prev:
                        x2_t(U - 1, 1)
                    if nxt:
                        t.wait_ge(g_kbd, B + 2)
                        score(b + 1, U + 2, 0, 0)
                    if prev:
                        route(U - 1)
                    if nxt:
                        score(b + 1, U + 2, 0, 1)
                    if prev:
                        t.wait_ge(a_lg, U)
                    if nxt and cur:
                        v_proj(B + 1)
                    if nxt:
                        score(b + 1, U + 2, 0, 2)
                        score(b + 1, U + 2, 0, 3)
                        t.wait_ge(d_v, B + 2)
                    if cur:
                        out_proj(U)
                        probs_t(U + 1, 1, 0)
                        probs_t(U + 1, 1, 1)
                        values(U + 1, B, 0)
                        probs_t(U + 1, 1, 2)
                        t.wait_ge(d_o, U + 1)
                    if nn and cur:
                        ctx_t(B + 2)
                    if cur:
                        values(U + 1, B, 1)
                        probs_t(U + 1, 1, 3)
                        values(U + 1, B, 2)
                    if nn:
                        t.wait_ge(a_ctx, B + 3)
                    if prev:
                        ranks(B - 1)
                    if cur:
                        values(U + 1, B, 3)
                        rinv_t(U + 1)
                    if nxt:
                        score(b + 1, U + 3, 1, 0)
                        score(b + 1, U + 3, 1, 1)
                    if cur:
                        if prev:
                            t.wait_ge(d_rk, B)
                        x2_t(U, 0)
                    if nxt:
                        score(b + 1, U + 3, 1, 2)
                    if cur:
                        route(U)
                    if nxt:
                        score(b + 1, U + 3, 1, 3)
                    if cur:
                        t.wait_ge(a_lg, U + 1)
                        out_proj(U + 1)
                run_steps(t, l, step)

                t.wait_ge(d_cum, 2 * NB * (l + 1))
                t.wait_ge(d_rk, NB * (l + 1))
                t.matmul(ps[:, 7, 0:NE], ones[:, :], cumb[:, :], start=True, stop=True).then_inc(f_cnt, 1)
                t.wait_ge(d_f, 16 + 22 * l)
                t.wait_ge(L_exp, 16 * (4 * NE if l == 0 else 4 * NE + 2 * NE))

                def block_t(j, u, i):
                    J = MAX_BLOCKS * l + j
                    t.wait_ge(L_xg[u], 16 * i + (16 + 16 * (MAX_BLOCKS // U3) * l))
                    need(t, e_x, J)
                    for k in range(KT):
                        i = t.transpose(ps[:, 7, k * P:(k + 1) * P], xg[:, u, k * P:(k + 1) * P], ident[:, :])
                    i.then_inc(b_x, 1)

                def up(j):
                    J = MAX_BLOCKS * l + j
                    off = t.value_load(woff_i[0:1, bass.ds(j, 1)], min_val=0, max_val=(NE - 1) * EW[l])
                    t.wait_ge(e_x, J + 1)
                    for n, (bank, col, w) in enumerate(UP[l]):
                        if l == 0:
                            need(t, e_h, 2 * j - 1 + n // 2) if n % 2 else need(t, e_act, 2 * j - 1 + n // 2)
                        else:
                            t.wait_ge(e_act, 2 * MAX_BLOCKS + j)
                        for k in range(KT):
                            i = t.matmul(ps[:, bank, 0:w], xgT[:, k, :], w_all[:, bass.ds(off + (k * UPW[l] + col), w)],
                                         start=(k == 0), stop=(k == KT - 1))
                        i.then_inc(b_up, 1)

                def h_t(j):
                    if l == 0:
                        t.wait_ge(e_h, 2 * j + 2)
                        need(t, e_hT, j)
                    else:
                        t.wait_ge(e_h, 2 * MAX_BLOCKS + j + 1)
                        t.wait_ge(e_hT, MAX_BLOCKS + j)
                    for c, r in DOWN[l]:
                        if c == 4:
                            i.then_inc(b_hT, 1)
                            need(t, e_hTv, j)
                        i = t.transpose(ps[0:r, 4 + c // 4, (c % 4) * P:(c % 4 + 1) * P], h_sb[:, c * P:c * P + r], ident[:, :])
                    i.then_inc(b_hT, 1)

                def down(j):
                    J = MAX_BLOCKS * l + j
                    off = t.value_load(woff_i[0:1, bass.ds(j, 1)], min_val=0, max_val=(NE - 1) * EW[l])
                    t.wait_ge(e_hT, J + 1)
                    if l == 0:
                        t.wait_ge(e_hTv, j + 1)
                    need(t, e_y, J)
                    for c, r in DOWN[l]:
                        i = t.matmul(ps[:, 6, 0:D], hT[0:r, c, :], w_all[0:r, bass.ds(off + (KT * UPW[l] + c * D), D)],
                                     start=(c == 0), stop=(c == KD[l] - 1))
                    i.then_inc(b_y, 1)

                block_t(0, 0, 0)

                def blk(j, u, i, first, last):
                    up(j)
                    if not last:
                        block_t(j + 1, (u + 1) % U3, i if u == 1 else i + 1)
                    if not first:
                        down(j - 1)
                    h_t(j)
                    if last:
                        down(j)
                run_blocks(t, l, blk)


def kernel(**inputs):
    import numpy as np
    import concourse.bacc as bacc
    from concourse.bass_utils import run_bass_kernel_spmd

    nc = bacc.Bacc("TRN2", target_bir_lowering=False, num_devices=1)
    arrays = {}

    def dram(name, a):
        a = np.ascontiguousarray(a)
        arrays[name] = a
        return nc.dram_tensor(name, a.shape, mybir.dt.from_np(a.dtype), kind="ExternalInput").ap()

    I = {k: np.asarray(v) for k, v in inputs.items()}
    attn_w, attn_b, router_w, experts = [], [], [], []
    for l in range(2):
        ws = [I[f"L{l}_xattn_W{c}"] for c in "qkvo"]
        attn_w.append([dram(f"w{c}{l}", w.T if l else w) for c, w in zip("qkvo", ws)])
        bs = [I[f"L{l}_xattn_b{c}"] for c in "qkvo"]
        attn_b.append([dram(f"b{c}{l}", b.reshape(2, 128).T if c in "qk" else b) for c, b in zip("qkvo", bs)])
    router_w = [dram("router0", I["L0_ffn_router_w"]), dram("router1", I["L1_ffn_router_w"].T)]
    experts = [[dram("gate0", I["L0_ffn_w_gate"]), dram("up0", I["L0_ffn_w_up"]), dram("down0", I["L0_ffn_w_down"])],
               [dram("w1", I["L1_ffn_w1_all"]), dram("w2", I["L1_ffn_w2_all"])]]
    x = dram("x", I["x"])
    ctx_rows = dram("ctx", I["ctx_1024"])
    mask = dram("mask", I["mask_Bx1x1xS2_ff0"].reshape(8, 120))
    out = nc.dram_tensor("out", x.shape, F32, kind="ExternalOutput").ap()
    flamingo_kernel(nc, x, ctx_rows, mask, dram("g_xattn", I["g_xattn"]), dram("g_ffn", I["g_ffn"]),
                    attn_w, attn_b, router_w, experts, out)
    r = run_bass_kernel_spmd(nc, [arrays], core_ids=[0])
    return r.results[0]["out"]
```

```python
from contextlib import ExitStack

import concourse.bass as bass
from concourse import mybir

F32 = mybir.dt.float32
BF16 = mybir.dt.bfloat16
I32 = mybir.dt.int32
U32 = mybir.dt.uint32
ALU = mybir.AluOpType
ACT = mybir.ActivationFunctionType
X = mybir.AxisListType.X

P = 128
NEG = -1000000000.0


def need(eng, sem, value):
    if not isinstance(value, int) or value > 0:
        eng.wait_ge(sem, value)


def apart(eng, passed, *waits):
    for sem, v in waits:
        need(eng, sem, v)
    if any(not isinstance(v, int) for _, v in waits):
        eng.sem_inc(passed, 1)


def flamingo_kernel(nc, x, ctx_rows, mask, g_xattn, g_ffn, attn_w, attn_b, router_w, experts, out):
    NB, S, D = x.shape
    K = ctx_rows.shape[1]
    H = 16
    DH = D // H
    HP = P // DH
    KT = D // P
    NT = NB * S // P
    QT = S // P
    NE = router_w[0].shape[1]
    TOPK = 2
    CH = 4 * K
    HID = [experts[0][0].shape[2], experts[1][0].shape[2]]
    KD = [-(-h // P) for h in HID]
    MAX_BLOCKS = (NT * P * TOPK + NE * (P - 1)) // P
    REGION = NT * P + P
    UPW = [2 * HID[0], HID[1]]
    EW = [KT * UPW[l] + KD[l] * D for l in range(2)]
    U3 = 3
    assert MAX_BLOCKS % U3 == 0 and QT == 2 and KT == 2

    xs_dram = nc.dram_tensor("xs_dram", [NE * REGION, D], F32, kind="Internal").ap()
    ys_dram = nc.dram_tensor("ys_dram", [MAX_BLOCKS * P, D], F32, kind="Internal").ap()

    es = ExitStack()
    with es:
        def sb(name, shape, dt=F32):
            return es.enter_context(nc.sbuf_tensor(name, shape, dt))

        def sem(name):
            return es.enter_context(nc.semaphore(name))

        x_sb = sb("x_sb", [P, NT, D])
        w_all = sb("w_all", [P, NE * EW[0]])
        w_att = sb("w_att", [P, 4, KT, D])
        wr = sb("wr", [P, 2, KT, NE])
        bq = sb("bq", [P, 2, KT])
        bq4 = sb("bq4", [P, 2, KT])
        bk = sb("bk", [P, 2, KT])
        bv = sb("bv", [P, 2, D])
        bo = sb("bo", [P, 2, D])
        gates = sb("gates", [P, 4])
        tg = sb("tg", [P, 4])
        mask3 = sb("mask3", [P, NB, K], BF16)
        ctx_sb = sb("ctx_sb", [P, D])
        ctxT = sb("ctxT", [P, KT, K])
        kT = sb("kT", [P, KT, K])
        v_tmp = sb("v_tmp", [P, D])
        v_pad = sb("v_pad", [P, H, 2 * DH])
        xn1 = sb("xn1", [P, QT, D])
        xn1T = sb("xn1T", [P, KT, S])
        qT = sb("qT", [P, KT, S])
        pT = sb("pT", [P, 2, 4 * P])
        rT = sb("rT", [P, KT, P])
        rsum = sb("rsum", [P, QT, H])
        rinv = sb("rinv", [P, QT, H])
        rinv16 = sb("rinv16", [P, H, DH])
        cT = sb("cT", [P, KT, P])
        xn2 = sb("xn2", [P, QT, D])
        kept = sb("kept", [P, QT, D])
        share = sb("share", [P, 3968])
        s_sb = share[:, 0:2 * HP * K].rearrange("p (h n) -> p h n", h=2)
        kbd = share[:, 2 * HP * K:4 * HP * K].rearrange("p (m h k) -> p m h k", m=2, h=HP)
        xg = share[:, 0:768].rearrange("p (u d) -> p u d", u=U3)
        xgT = share[:, 768:1024].rearrange("p (k n) -> p k n", k=KT)
        act_sb = share[:, 1024:1712]
        h_sb = share[:, 1712:2400]
        hT = share[:, 2400:3168].rearrange("p (c n) -> p c n", c=6)
        y_sb = share[:, 3168:3936].rearrange("p (u d) -> p u d", u=U3)
        zrow = y_sb[:, 1, :]
        p_buf = w_all[:, (NE - 1) * EW[0]:(NE - 1) * EW[0] + 2 * H * K].rearrange("p (q n) -> p q n", q=2)
        yg = w_all[:, NE * EW[1]:NE * EW[1] + NB * QT * TOPK * D].rearrange("p (b t k d) -> p b t k d", b=NB, t=QT, k=TOPK)
        mask_bc = share[:, 0:NB * K].rearrange("p (b k) -> p b k", b=NB)
        mask_hi = share[:, NB * K:NB * K + NB * K // 2].bitcast(BF16).rearrange("p (b k) -> p b k", b=NB)
        spare = (NE - 1) * EW[0] + 2 * H * K
        xn2T = w_all[:, spare:spare + D].rearrange("p (k n) -> p k n", k=KT)
        assert 2 * H * K + D <= EW[0]
        mx = sb("mx", [P, 2, HP])
        st1 = sb("st1", [P, QT, 6])
        mv1 = sb("mv1", [P, QT, 2])
        ve1 = sb("ve1", [P, QT])
        rstd1 = sb("rstd1", [P, QT])
        st2 = sb("st2", [P, QT, 6])
        mv2 = sb("mv2", [P, QT, 2])
        ve2 = sb("ve2", [P, QT])
        rstd2 = sb("rstd2", [P, QT])
        jc, be, sbx = (share[:, 2048 + n * MAX_BLOCKS:2048 + (n + 1) * MAX_BLOCKS] for n in range(3))
        logits = share[:, 3840:3856].rearrange("p (t e) -> p t e", t=2)
        topnow = share[:, 3856:3872].rearrange("p (t e) -> p t e", t=2)
        idx8 = share[:, 3872:3888].bitcast(U32).rearrange("p (t e) -> p t e", t=2)
        rk = share[:, 3888:3904].rearrange("p (t e) -> p t e", t=2)
        prod = share[:, 3904:3936].rearrange("p (t k e) -> p t k e", t=2, k=TOPK)
        idxf = share[:, 3936:3940].rearrange("p (t k) -> p t k", t=2)
        top8 = sb("top8", [P, NT, 8])
        onehot = sb("onehot", [P, NT, TOPK, NE])
        maskb = sb("maskb", [P, 2, NE], BF16)
        cumb = sb("cumb", [P, NE], BF16)
        slotf = sb("slotf", [P, NT, TOPK])
        slot_now = sb("slot_now", [P, 2, TOPK], I32)
        cnt = sb("cnt", [P, NE])
        pad_i = sb("pad_i", [P, NE], I32)
        cmpb = pT[:, :, :].rearrange("p a b -> p (a b)")[:, 0:MAX_BLOCKS * NE]
        nb = sb("nb", [P, NE])
        sbk = sb("sbk", [P, NE])
        tot1 = sb("tot1", [P, 1])
        xrow_i = sb("xrow_i", [P, MAX_BLOCKS], I32)
        woff_i = sb("woff_i", [P, MAX_BLOCKS], I32)
        yoff = sb("yoff", [P, NE])
        yslot = sb("yslot", [P, NT, TOPK])
        yslot_i = sb("yslot_i", [P, NT, TOPK], I32)
        ynow = sb("ynow", [P, 2, TOPK], I32)
        zsum = sb("zsum", [P, NT])
        wcomb = sb("wcomb", [P, NT, TOPK])
        ident = sb("ident", [P, P])
        hmask = sb("hmask", [P, HP])
        tri = sb("tri", [P, P], BF16)
        ones = sb("ones", [P, P], BF16)
        iota8 = sb("iota8", [P, NE])
        eR = sb("eR", [P, NE])
        thr = sb("thr", [P, NT])
        jrow = sb("jrow", [P, MAX_BLOCKS])
        lower = sb("lower", [P, NE, NE])
        mhalf = sb("mhalf", [P, QT])
        ps = es.enter_context(nc.psum_tensor("ps", [P, 8, 512], F32))

        L_x = [sem(f"x_loaded{i}") for i in range(4)]
        L_w = sem("attn_w_loaded")
        L_qk = sem("first_biases_loaded")
        L_mask = sem("mask_loaded")
        L_gates = sem("gates_loaded")
        L_vr = sem("values_bias_and_router_loaded")
        L_small1 = sem("layer1_small_loaded")
        L_ctx = sem("ctx_loaded")
        L_exp = sem("experts_loaded")
        L_xg = [sem(f"block_loaded{u}") for u in range(U3)]
        D_y = [sem(f"block_stored{u}") for u in range(U3)]
        D_sc = sem("tokens_scattered")
        D_pad = sem("pads_scattered")
        D_ga = sem("results_gathered")
        D_gl = [sem(f"last_results_gathered{b}") for b in range(NB)]
        D_out = [sem(f"out_stored{i}") for i in range(2)]
        C_g = sem("consts_pool")
        C_v = sem("consts_vector")
        C_a = sem("gates_ready")
        C_q = sem("query_bias_ready")
        C_bo = sem("output_bias_ready")
        p_k, p_xnT, p_q, p_v, p_ctx = (sem(n) for n in ("k_psum", "xn1T_psum", "q_psum", "v_psum", "ctxT_psum"))
        p_s, p_t, p_pv, p_o = (sem(n) for n in ("scores_psum", "probsT_psum", "ctx_chunk_psum", "o_psum"))
        p_x2, p_lg, p_rk = (sem(n) for n in ("xn2T_psum", "logits_psum", "rank_psum"))
        a_k, a_xnT, a_q, a_ctx = (sem(n) for n in ("k_sb_ready", "xn1T_ready", "q_ready", "ctxT_ready"))
        a_t, a_exp, a_rt, a_x2, a_lg = (sem(n) for n in ("probsT_ready", "exp_ready", "rinvT_ready", "xn2T_ready", "logits_ready"))
        a_v, d_max, d_sub, d_c = (sem(n) for n in ("v_ready", "max_ready", "shifted_ready", "cT_ready"))
        d_o, d_st2, d_mv2, d_xn2 = (sem(n) for n in ("residual_ready", "stats2_ready", "meanvar2_ready", "xn2_ready"))
        d_st1, d_mv1, d_xn1 = (sem(n) for n in ("stats1_ready", "meanvar1_ready", "xn1_ready"))
        d_r1, d_mask, d_rk, d_slot, d_cum = (sem(n) for n in ("route_step", "mask_ready", "rank_read", "slots_ready", "cum_ready"))
        d_r2 = sem("route2_step")
        a_keep = sem("batch_kept")
        d_f = sem("final_route_step")
        d_sum, d_ri, a_re, p_rt = (sem(n) for n in ("sums_ready", "rinv_ready", "rinv_spread", "rinvT_psum"))
        d_m = sem("mask_split_step")
        d_tm = sem("top_max_ready")
        d_comb, d_c1, d_yn = (sem(n) for n in ("combined", "combine_step", "gather_index_ready"))
        g_kbd, g_ve2, g_rs2, g_ve1, g_rs1, g_vp = (sem(n) for n in (
            "kbd_ready", "vareps2", "rstd2_ready", "vareps1", "rstd1_ready", "vpad_ready"))
        f_cnt = sem("count_psum")
        f_exp = sem("top_exp_ready")
        b_x, b_up, b_hT, b_y = (sem(n) for n in ("blkT_psum", "up_psum", "hT_psum", "y_psum"))
        e_x, e_act, e_hT, e_hTv, e_y, e_h = (sem(n) for n in ("blkT_ready", "act_ready", "hT_ready_a", "hT_ready_v", "y_ready", "h_ready"))
        g_z = sem("zeros_ready")
        g_bias = sem("bias_added")
        d_yi = sem("last_indices_ready")
        g_passed, d_passed = sem("pool_passed"), sem("vector_passed")

        block = es.enter_context(nc.Block())

        def run_steps(eng, l, step):
            step(-1, False, True, True, False)
            step(0, True, True, True, False)
            step(1, True, True, True, True)
            with eng.Fori(2, NB - 2) as b:
                step(b, True, True, True, True)
            step(NB - 2, True, True, False, True)
            step(NB - 1, True, False, False, True)
            step(NB, False, False, False, True)

        def run_blocks(eng, l, step):
            for j in range(U3 + 1):
                step(j, j % U3, (j - 1) // U3, j == 0, False)
            with eng.Fori(1, (MAX_BLOCKS - U3) // U3) as i:
                for u in range(U3):
                    step(U3 * i + (1 + u), (1 + u) % U3, i, False, False)
            for j in (MAX_BLOCKS - 2, MAX_BLOCKS - 1):
                step(j, j % U3, (j - 1) // U3, False, j == MAX_BLOCKS - 1)

        UP = [[(0, 0, 344), (1, HID[0], 344), (2, 344, 344), (3, HID[0] + 344, 344)], [(0, 0, HID[1])]]
        DOWN = [[(c, min(P, HID[l] - c * P)) for c in range(KD[l])] for l in range(2)]

        def load_expert(eng, l, e):
            slot = w_all[:, bass.ds(e * EW[l], EW[l])]
            ups, down = experts[l][:-1], experts[l][-1]
            dst = slot[:, 0:KT * UPW[l]].rearrange("p (k n) -> p k n", k=KT)
            for i, w in enumerate(ups):
                eng.dma_start(dst[:, :, i * HID[l]:(i + 1) * HID[l]],
                              w[bass.ds(e, 1), :, :].rearrange("e (k p) n -> p (e k) n", p=P)).then_inc(L_exp, 16)
            full = HID[l] // P
            dst = slot[:, KT * UPW[l]:EW[l]].rearrange("p (c n) -> p c n", c=KD[l])
            eng.dma_start(dst[:, 0:full, :],
                          down[bass.ds(e, 1), 0:full * P, :].rearrange("e (c p) n -> p (e c) n", p=P)).then_inc(L_exp, 16)
            if HID[l] % P:
                eng.dma_start(dst[0:HID[l] % P, full, :],
                              down[bass.ds(e, 1), full * P:HID[l], :].rearrange("e p n -> p (e n)")).then_inc(L_exp, 16)

        @block.sync
        def _(sp):
            xv = x.rearrange("b (t p) d -> p (b t) d", p=P)

            def load_att(l):
                for i in (1, 0, 2, 3):
                    sp.dma_start(w_att[:, i, :, :], attn_w[l][i].rearrange("(k p) n -> p k n", p=P)).then_inc(L_w, 16)

            sp.dma_start(x_sb[:, 0:2, :], xv[:, 0:2, :]).then_inc(L_x[0], 16)
            sp.dma_start(ctx_sb[0:K, :], ctx_rows[0, :, :]).then_inc(L_ctx, 16)
            load_att(0)
            q_b, k_b, v_b, o_b = attn_b[0]
            sp.dma_start(bo[:, 0, :], o_b.unsqueeze(0).to_broadcast([P, D])).then_inc(L_gates, 16)
            sp.dma_start(bv[:, 0, :], v_b.unsqueeze(0).to_broadcast([P, D])).then_inc(L_vr, 16)
            sp.dma_start(wr[:, 0, :, :], router_w[0].rearrange("(k p) n -> p k n", p=P)).then_inc(L_vr, 16)
            for i, (a, z) in enumerate(((2, 4), (4, 8), (8, 16))):
                sp.dma_start(x_sb[:, a:z, :], xv[:, a:z, :]).then_inc(L_x[i + 1], 16)
            q_b, k_b, v_b, o_b = attn_b[1]
            sp.dma_start(bq[:, 1, :], q_b).then_inc(L_small1, 16)
            sp.dma_start(bk[:, 1, :], k_b).then_inc(L_small1, 16)
            sp.dma_start(bv[:, 1, :], v_b.unsqueeze(0).to_broadcast([P, D])).then_inc(L_small1, 16)
            sp.dma_start(bo[:, 1, :], o_b.unsqueeze(0).to_broadcast([P, D])).then_inc(L_small1, 16)
            sp.dma_start(wr[:, 1, :, :], router_w[1].rearrange("(k p) n -> p k n", p=P)).then_inc(L_small1, 16)

            for l in range(2):
                if l == 1:
                    sp.wait_ge(b_y, MAX_BLOCKS)
                    for e in range(NE):
                        load_expert(sp, 1, e)
                with sp.Fori(1, NB) as b:
                    sp.wait_ge(p_ctx, NB * l + b)
                    sp.dma_start(ctx_sb[0:K, :], ctx_rows[bass.ds(b, 1), :, :].rearrange("b k d -> (b k) d")).then_inc(L_ctx, 16)
                    if l == 0:
                        load_expert(sp, 0, b - 1)
                sp.wait_ge(p_ctx, NB * (l + 1))
                if l == 0:
                    sp.dma_start(ctx_sb[0:K, :], ctx_rows[0, :, :]).then_inc(L_ctx, 16)
                    sp.wait_ge(p_o, NT)
                    load_att(1)
                sp.wait_ge(d_f, 2 + 22 * l)
                sp.wait_ge(g_z, l + 1)
                for e in range(NE):
                    row = sp.value_load(pad_i[0:1, e:e + 1], min_val=0, max_val=NE * REGION - P)
                    sp.dma_start(xs_dram[bass.ds(row, P), :], zrow).then_inc(D_pad, 16)
                sp.wait_ge(D_sc, 16 * TOPK * NT * (l + 1))
                sp.wait_ge(D_pad, 16 * NE * (l + 1))
                sp.wait_ge(d_f, 16 + 22 * l)

                def load_block(j, u):
                    J = MAX_BLOCKS * l + j
                    if not (isinstance(j, int) and j < U3):
                        sp.wait_ge(b_x, J - U3 + 1)
                    row = sp.value_load(xrow_i[0:1, bass.ds(j, 1)], min_val=0, max_val=NE * REGION - P)
                    sp.dma_start(xg[:, u, :], xs_dram[bass.ds(row, P), :]).then_inc(L_xg[u], 16)

                def store_block(j, u):
                    sp.wait_ge(e_y, MAX_BLOCKS * l + j + 1)
                    sp.dma_start(ys_dram[bass.ds(j * P, P), :], y_sb[:, u, :]).then_inc(D_y[u], 16)

                for j in range(2 * U3):
                    load_block(j, j % U3)
                with sp.Fori(2, MAX_BLOCKS // U3) as i:
                    for u in range(U3):
                        load_block(U3 * i + u, u)
                        store_block(U3 * i + (u - 2 * U3), u)
                for j in range(MAX_BLOCKS - 2 * U3, MAX_BLOCKS):
                    store_block(j, j % U3)
            ov = out.rearrange("b (t p) d -> p b t d", p=P)
            for b in range(NB):
                sp.wait_ge(d_comb, NT + 2 * (b + 1))
                sp.dma_start(ov[:, b, :, :], x_sb[:, 2 * b:2 * b + 2, :]).then_inc(D_out[b % 2], 16)
            sp.wait_ge(D_out[0], 16 * NB // 2)
            sp.wait_ge(D_out[1], 16 * NB // 2)

        @block.gpsimd
        def _(g):
            g.memset(ident[:], 0.0).then_inc(C_g, 1)
            g.memset(hmask[:], 1.0).then_inc(C_g, 1)
            g.memset(tri[:], 1.0).then_inc(C_g, 1)
            g.memset(ones[:], 1.0).then_inc(C_g, 1)
            g.memset(lower[:], 1.0).then_inc(C_g, 1)
            g.memset(mhalf[:], -0.5).then_inc(C_g, 1)
            g.wait_ge(C_g, 6)
            g.affine_select(out=ident[:], in_=ident[:], compare_op=ALU.not_equal, fill=1.0, base=0,
                            pattern=[[-1, P]], channel_multiplier=1).then_inc(C_g, 1)
            g.affine_select(out=hmask[:], in_=hmask[:], compare_op=ALU.is_ge, fill=0.0, base=0,
                            pattern=[[-DH, HP]], channel_multiplier=1).then_inc(C_g, 1)
            g.wait_ge(C_g, 8)
            g.affine_select(out=hmask[:], in_=hmask[:], compare_op=ALU.is_ge, fill=0.0, base=DH - 1,
                            pattern=[[DH, HP]], channel_multiplier=-1).then_inc(C_g, 1)
            g.affine_select(out=tri[:], in_=tri[:], compare_op=ALU.is_ge, fill=0.0, base=-1,
                            pattern=[[1, P]], channel_multiplier=-1).then_inc(C_g, 1)
            g.affine_select(out=lower[:], in_=lower[:], compare_op=ALU.is_ge, fill=0.0, base=-1,
                            pattern=[[1, NE], [-1, NE]], channel_multiplier=0).then_inc(C_g, 1)

            def ramp(t, n, step, base, per):
                return g.iota(t, pattern=[[step, n]], base=base, channel_multiplier=per,
                              allow_small_or_imprecise_dtypes=True)
            ramp(iota8[:], NE, 1, 0, 0)
            ramp(eR[:], NE, REGION, 0, 0)
            ramp(thr[:], NT, P, 0, 0).then_inc(C_g, 1)
            ramp(jrow[:], MAX_BLOCKS, 1, 0, 0).then_inc(C_g, 1)
            g.memset(v_pad[:], 0.0).then_inc(C_g, 1)

            def rstd(mv, ve, out_, ready, s_ve, v_ve, s_out):
                g.tensor_scalar(ve, mv, 1e-5, None, ALU.add).then_inc(s_ve, 1)
                g.wait_ge(s_ve, v_ve)
                g.tensor_tensor(out_, ve, ready, ALU.pow).then_inc(s_out, 1)

            for l in range(2):
                def ln1_rstd(B):
                    apart(g, g_passed, (d_mv1, 2 * B + 2))
                    rstd(mv1[:, :, 1], ve1[:], rstd1[:], mhalf[:], g_ve1, B + 1, g_rs1)

                def add_bias(B, b):
                    g.wait_ge(d_xn1, B + 1)
                    g.wait_ge(C_bo, l + 1)
                    xb = x_sb[:, bass.ds(2 * b, 2), :]
                    g.tensor_tensor(xb, xb, bo[:, l, :].unsqueeze(1).to_broadcast([P, QT, D]), ALU.add).then_inc(g_bias, 1)

                def gather(B):
                    apart(g, g_passed, (d_yn, B + 1))
                    for t in range(2):
                        for k in range(TOPK):
                            g.indirect_dma_start(yg[:, 0, t, k, :], None, ys_dram,
                                                 bass.IndirectOffsetOnAxis(ap=ynow[:, t, k:k + 1], axis=0)
                                                 ).then_inc(D_ga, 16)

                def ln2_rstd(U, qt):
                    apart(g, g_passed, (d_mv2, U + 1))
                    rstd(mv2[:, qt, 1:2], ve2[:, qt:qt + 1], rstd2[:, qt:qt + 1], mhalf[:, 0:1], g_ve2, U + 1, g_rs2)

                if l == 1:
                    for u in range(U3):
                        g.wait_ge(D_y[u], 16 * MAX_BLOCKS // U3)
                    gather(0)
                def keys(B, cur):
                    g.wait_ge(a_k, B + 1)
                    if cur:
                        g.wait_ge(p_s, 4 * B)
                    g.tensor_tensor(kbd, kT[:, :, :].unsqueeze(2).to_broadcast([P, KT, HP, K]),
                                    hmask[:, :].unsqueeze(1).unsqueeze(3).to_broadcast([P, KT, HP, K]),
                                    ALU.mult).then_inc(g_kbd, 1)

                if l == 1:
                    keys(NB * l, False)
                ln1_rstd(NB * l)
                if l == 0:
                    keys(NB * l, False)
                add_bias(NB * l, 0)

                def step(b, cur, nxt, nn, prev):
                    B = NB * l + b
                    if nxt and cur:
                        keys(B + 1, cur)
                    if nn and l == 1:
                        gather(b + 2)
                    if cur:
                        ln2_rstd(2 * B, 0)
                    if nxt:
                        g.wait_ge(a_v, B + 2)
                        g.wait_ge(*((L_vr, 32) if l == 0 else (L_small1, 80)))
                        if cur:
                            g.wait_ge(p_pv, 8 * B + 8)
                        for s in range(2):
                            heads = lambda t: t.rearrange("p (g s d) -> p s g d", s=2, d=DH)[:, s, :, :]
                            i = g.tensor_tensor(v_pad[0:K, s::2, s * DH:(s + 1) * DH], heads(v_tmp[0:K, :]),
                                                heads(bv[0:K, l, :]), ALU.add)
                        i.then_inc(g_vp, 1)
                    if nn:
                        ln1_rstd(B + 2)
                    if prev and not cur:
                        g.wait_ge(p_s, 4 * NB * (l + 1))
                        g.memset(zrow, 0.0).then_inc(g_z, 1)
                    if prev:
                        apart(g, g_passed, (a_keep, (NB - 1) * l + b if cur else 0), (d_slot, B))
                        rows = kept if cur else xn2
                        for t in range(2):
                            for k in range(TOPK):
                                g.indirect_dma_start(xs_dram, bass.IndirectOffsetOnAxis(ap=slot_now[:, t, k:k + 1], axis=0),
                                                     rows[:, t, :], None).then_inc(D_sc, 16)
                    if nn:
                        add_bias(B + 2, b + 2)
                    if cur:
                        ln2_rstd(2 * B + 1, 1)
                run_steps(g, l, step)
            for u in range(U3):
                g.wait_ge(D_y[u], 2 * 16 * MAX_BLOCKS // U3)
            g.wait_ge(d_yi, 1)
            for b in range(NB):
                for t in range(2):
                    for k in range(TOPK):
                        g.indirect_dma_start(yg[:, b, t, k, :], None, ys_dram,
                                             bass.IndirectOffsetOnAxis(ap=yslot_i[:, 2 * b + t, k:k + 1], axis=0)
                                             ).then_inc(D_gl[b], 16)

        @block.scalar
        def _(a):
            q_b, k_b, v_b, o_b = attn_b[0]
            a.dma_start(bk[:, 0, :], k_b).then_inc(L_qk, 16)
            a.dma_start(bq[:, 0, :], q_b).then_inc(L_qk, 16)
            a.dma_start(mask_bc, mask.unsqueeze(0).to_broadcast([P, NB, K])).then_inc(L_mask, 16)
            a.dma_start(gates[:, 0:2], g_xattn.unsqueeze(0).to_broadcast([P, 2])).then_inc(L_gates, 16)
            a.dma_start(gates[:, 2:4], g_ffn.unsqueeze(0).to_broadcast([P, 2])).then_inc(L_gates, 16)
            for l in range(2):
                def ctx_evac(B):
                    a.wait_ge(p_ctx, B + 1)
                    if not (isinstance(B, int) and B == 0):
                        a.wait_ge(p_v, B)
                    a.copy(ctxT[:, :, :], ps[:, 7, 0:KT * K].rearrange("p (k n) -> p k n", k=KT)).then_inc(a_ctx, 1)

                def t_evac(U, c):
                    a.wait_ge(p_t, 4 * U + c + 1)
                    need(a, p_pv, 4 * U + c - 1)
                    a.copy(pT[0:K, c % 2, :], ps[0:K, 4 + c % 2, :]).then_inc(a_t, 1)

                def exp(U, qt, h):
                    a.wait_ge(d_sub, 2 * U + h + 1)
                    need(a, p_t, 4 * U - 4)
                    a.activation(p_buf[:, qt, h * HP * K:(h + 1) * HP * K], s_sb[:, h, :], ACT.Exp).then_inc(a_exp, 1)

                def x2_evac(U):
                    a.wait_ge(p_x2, U + 1)
                    need(a, p_lg, U)
                    a.copy(xn2T[:, :, :], ps[:, 7, 0:KT * P].rearrange("p (k n) -> p k n", k=KT)).then_inc(a_x2, 1)

                def lg_evac(U, B, qt):
                    a.wait_ge(p_lg, U + 1)
                    need(a, d_mask, B)
                    a.copy(logits[:, qt, :], ps[:, 7, 0:NE]).then_inc(a_lg, 1)

                def spread(U, qt):
                    a.wait_ge(d_ri, U + 1)
                    need(a, p_rt, U)
                    a.copy(rinv16[:, :, :], rinv[:, qt, :].unsqueeze(2).to_broadcast([P, H, DH])).then_inc(a_re, 1)

                def keep(B):
                    need(a, D_sc, 64 * B)
                    a.wait_ge(d_xn2, 2 * B + 2)
                    a.copy(kept[:, :, :], xn2[:, :, :]).then_inc(a_keep, 1)

                def v_evac(B):
                    a.wait_ge(p_v, B + 1)
                    need(a, g_vp, B)
                    a.copy(v_tmp[0:K, :], ps[0:K, 7, 0:D]).then_inc(a_v, 1)

                def rt_evac(U):
                    a.wait_ge(p_rt, U + 1)
                    need(a, d_c, U)
                    a.copy(rT[:, :, :], ps[:, 6, KT * P:2 * KT * P].rearrange("p (k q) -> p k q", k=KT)).then_inc(a_rt, 1)

                a.wait_ge(*((L_qk, 32) if l == 0 else (L_small1, 80)))
                a.mul(bq4[:, l, :], bq[:, l, :], 0.25).then_inc(C_q, 1)
                ctx_evac(NB * l)
                if l == 0:
                    a.wait_ge(L_gates, 48)
                    a.activation(tg[:, :], gates[:, :], ACT.Tanh).then_inc(C_a, 1)

                def step(b, cur, nxt, nn, prev):
                    B = NB * l + b
                    U = 2 * B
                    if cur:
                        t_evac(U, 0)
                        t_evac(U, 1)
                        exp(U + 1, 1, 0)
                    if nxt:
                        a.wait_ge(p_k, B + 2)
                        need(a, g_kbd, B + 1)
                        for m in range(KT):
                            i = a.activation(kT[:, m, :], ps[:, 7, m * K:(m + 1) * K], ACT.Identity, bias=bk[:, l, m:m + 1])
                        i.then_inc(a_k, 1)
                    if nxt and not cur:
                        v_evac(B + 1)
                        ctx_evac(B + 2)
                    if cur:
                        t_evac(U, 2)
                    if nxt:
                        a.wait_ge(p_xnT, B + 2)
                        need(a, p_q, B + 1)
                        a.copy(xn1T[:, :, :], ps[:, 7, :].rearrange("p (k n) -> p k n", k=KT)).then_inc(a_xnT, 1)
                    if cur:
                        t_evac(U, 3)
                        spread(U, 0)
                        exp(U + 1, 1, 1)
                    if nxt:
                        a.wait_ge(p_q, B + 2)
                        need(a, p_s, 4 * B + 4)
                        a.wait_ge(C_q, l + 1)
                        for m in range(KT):
                            i = a.activation(qT[:, m, :], ps[:, 7, m * S:(m + 1) * S], ACT.Identity,
                                             bias=bq4[:, l, m:m + 1], scale=0.25)
                        i.then_inc(a_q, 1)
                    if cur:
                        rt_evac(U)
                    if prev and cur:
                        keep(B - 1)
                    if cur and not nxt:
                        t_evac(U + 1, 0)
                        t_evac(U + 1, 1)
                    if prev:
                        x2_evac(U - 1)
                    if cur and not nxt:
                        t_evac(U + 1, 2)
                    if prev:
                        lg_evac(U - 1, B - 1, 1)
                    if nxt and cur:
                        v_evac(B + 1)
                    if nxt:
                        exp(U + 2, 0, 0)
                    if cur and nxt:
                        t_evac(U + 1, 0)
                        t_evac(U + 1, 1)
                        t_evac(U + 1, 2)
                    if nn and cur:
                        ctx_evac(B + 2)
                    if cur:
                        t_evac(U + 1, 3)
                        spread(U + 1, 1)
                    if nxt:
                        exp(U + 2, 0, 1)
                    if cur:
                        rt_evac(U + 1)
                        x2_evac(U)
                        lg_evac(U, B, 0)
                run_steps(a, l, step)

                if l == 0:
                    a.wait_ge(p_t, 4 * NT)
                    a.wait_ge(p_lg, NT)
                    load_expert(a, 0, NE - 1)      
                a.wait_ge(d_f, 17 + 22 * l)
                a.activation(top8[:, :, :], top8[:, :, :], ACT.Exp).then_inc(f_exp, 1)

                def blk(j, u, i, first, last):
                    J = MAX_BLOCKS * l + j
                    nq = len(UP[l]) // 2 or 1
                    if l == 0:
                        for q in range(2):
                            a.wait_ge(b_up, 4 * j + 2 * q + 1)
                            need(a, e_h, 2 * j - 1 + q)
                            a.activation(act_sb[:, 344 * q:344 * q + 344], ps[:, 2 * q, 0:344], ACT.Silu).then_inc(e_act, 1)
                    else:
                        a.wait_ge(b_up, 4 * MAX_BLOCKS + j + 1)
                        a.wait_ge(e_h, 2 * MAX_BLOCKS + j)
                        a.activation(act_sb[:, 0:HID[1]], ps[:, 0, 0:HID[1]], ACT.Relu).then_inc(e_act, 1)
                    a.wait_ge(b_hT, 2 * j + 1 if l == 0 else 2 * MAX_BLOCKS + j + 1)
                    need(a, b_y, J)
                    n = min(4, KD[l])
                    a.copy(hT[:, 0:n, :], ps[:, 4, 0:n * P].rearrange("p (c n) -> p c n", c=n)).then_inc(e_hT, 1)
                run_blocks(a, l, blk)

        @block.vector
        def _(v):
            def split_mask():
                for part in range(3):
                    v.tensor_copy(mask_hi, mask_bc).then_inc(d_m, 1)
                    v.wait_ge(d_m, 3 * part + 1)
                    v.tensor_copy(mask3[32 * part:32 * part + 1, :, :], mask_hi[32 * part:32 * part + 1, :, :]).then_inc(d_m, 1)
                    v.tensor_tensor(mask_bc, mask_bc, mask_hi, ALU.subtract).then_inc(d_m, 1)
                    v.wait_ge(d_m, 3 * part + 3)

            v.memset(cumb[:], 0.0).then_inc(C_v, 1)
            v.memset(mask3[:], 0.0).then_inc(C_v, 1)
            v.wait_ge(C_g, 14)

            for l in range(2):
                F = 22 * l

                def ln1_stats(B, b, loaded=None):
                    if loaded is not None:
                        v.wait_ge(loaded, 16)
                    for t in range(2):
                        v.bn_stats(st1[:, t, :], x_sb[:, 2 * b + t, :] if isinstance(b, int) else
                                   x_sb[:, bass.ds(2 * b + t, 1), :]).then_inc(d_st1, 1)
                    for t in range(2):
                        apart(v, d_passed, (d_st1, 2 * B + t + 1))
                        v.bn_aggr(mv1[:, t, :], st1[:, t, :]).then_inc(d_mv1, 1)

                def ln1_apply(B, b):
                    v.wait_ge(g_rs1, B + 1)
                    v.wait_ge(d_mv1, 2 * B + 2)
                    need(v, p_xnT, B)
                    for t in range(2):
                        i = v.tensor_scalar(xn1[:, t:t + 1, :], x_sb[:, bass.ds(2 * b + t, 1), :], mv1[:, t, 0:1],
                                            rstd1[:, t:t + 1], ALU.subtract, ALU.mult)
                    i.then_inc(d_xn1, 1)

                def combine(B, b, gathered, value, gb=0):
                    v.wait_ge(gathered, value)
                    for k in range(TOPK):
                        for t in range(2):
                            if k:
                                v.wait_ge(d_c1, 2 * B + t + 1)
                            xt = x_sb[:, bass.ds(2 * b + t, 1), :]
                            v.scalar_tensor_tensor(
                                out=xt, in0=yg[:, gb, t, k:k + 1, :], scalar=wcomb[:, bass.ds(2 * b + t, 1), k:k + 1].rearrange("p a b -> p (a b)"),
                                in1=xt, op0=ALU.mult, op1=ALU.add).then_inc(d_comb if k else d_c1, 1)

                def next_index(B, b):
                    apart(v, d_passed, (D_ga, 64 * B))
                    v.tensor_copy(ynow[:, :, :], yslot[:, bass.ds(2 * b, 2), :]).then_inc(d_yn, 1)

                def shift(U, h):
                    v.wait_ge(p_s, 2 * U + h + 1)
                    sps = ps[:, 2 * h:2 * h + 2, 0:CH].rearrange("p c (h k) -> p c h k", h=4)
                    s4 = s_sb[:, h, :].rearrange("p (c h k) -> p c h k", c=2, h=4)
                    m4 = mx[:, h, :].rearrange("p (c h) -> p c h", c=2)
                    need(v, a_exp, 2 * U + h - 1)
                    v.tensor_reduce(m4, sps, X, ALU.max).then_inc(d_max, 1)
                    v.wait_ge(d_max, 2 * U + h + 1)
                    v.tensor_tensor(s4, sps, m4.unsqueeze(3).to_broadcast([P, 2, 4, K]),
                                    ALU.subtract).then_inc(d_sub, 1)

                def totals(U, qt):
                    v.wait_ge(a_exp, 2 * U + 2)
                    v.tensor_reduce(rsum[:, qt, :], p_buf[:, qt, :].rearrange("p (h k) -> p h k", h=H), X,
                                    ALU.add).then_inc(d_sum, 1)
                    v.wait_ge(d_sum, U + 1)
                    need(v, a_re, U - 1)
                    v.reciprocal(rinv[:, qt, :], rsum[:, qt, :]).then_inc(d_ri, 1)

                def divide(U):
                    v.wait_ge(p_pv, 4 * U + 4)
                    v.wait_ge(a_rt, U + 1)
                    need(v, p_o, U)
                    v.tensor_tensor(cT[:, :, :], ps[:, 6, 0:KT * P].rearrange("p (k q) -> p k q", k=KT), rT[:, :, :],
                                    ALU.mult).then_inc(d_c, 1)

                def residual(U, T, B, qt):
                    v.wait_ge(p_o, U + 1)
                    v.wait_ge(g_bias, B + 1)
                    xt = x_sb[:, bass.ds(T, 1), :]
                    v.scalar_tensor_tensor(out=xt, in0=ps[:, 7, 0:D].unsqueeze(1), scalar=tg[:, l:l + 1], in1=xt,
                                           op0=ALU.mult, op1=ALU.add).then_inc(d_o, 1)
                    apart(v, d_passed, (d_o, U + 1))
                    v.bn_stats(st2[:, qt, :], xt).then_inc(d_st2, 1)
                    apart(v, d_passed, (d_st2, U + 1))
                    v.bn_aggr(mv2[:, qt, :], st2[:, qt, :]).then_inc(d_mv2, 1)

                def ln2_apply(U, T, B, qt):
                    v.wait_ge(g_rs2, U + 1)
                    v.wait_ge(d_mv2, U + 1)
                    if qt == 0:
                        need(v, a_keep, B - l)
                    need(v, p_x2, U - 1)
                    v.tensor_scalar(xn2[:, qt:qt + 1, :], x_sb[:, bass.ds(T, 1), :], mv2[:, qt, 0:1], rstd2[:, qt:qt + 1],
                                    ALU.subtract, ALU.mult).then_inc(d_xn2, 1)

                def route1(B, b):
                    apart(v, d_passed, (a_lg, 2 * B + 2))
                    for t in range(2):
                        v.max(topnow[:, t, :], logits[:, t, :]).then_inc(d_r1, 1)
                    for t in range(2):
                        apart(v, d_passed, (d_r1, 7 * B + t + 1))
                        v.max_index(idx8[:, t, :], topnow[:, t, :], logits[:, t, :]).then_inc(d_r1, 1)
                    v.tensor_copy(top8[:, bass.ds(2 * b, 2), :], topnow[:, :, :]).then_inc(d_r1, 1)
                    v.wait_ge(d_r1, 7 * B + 5)
                    v.tensor_copy(idxf[:, :, :], idx8[:, :, 0:TOPK]).then_inc(d_r1, 1)
                    v.wait_ge(d_r1, 7 * B + 6)
                    oh = onehot[:, bass.ds(2 * b, 2), :, :]
                    v.tensor_tensor(oh, iota8[:, :].unsqueeze(1).unsqueeze(1).to_broadcast([P, 2, TOPK, NE]),
                                    idxf[:, :, :].unsqueeze(3).to_broadcast([P, 2, TOPK, NE]), ALU.is_equal).then_inc(d_r1, 1)
                    v.wait_ge(d_r1, 7 * B + 7)
                    need(v, p_rk, B)
                    need(v, d_cum, 2 * B)
                    v.tensor_tensor(maskb[:, :, :], oh[:, :, 0, :], oh[:, :, 1, :], ALU.add).then_inc(d_mask, 1)

                def route2(B, b):
                    v.wait_ge(p_rk, B + 1)
                    v.tensor_tensor(rk[:, :, :], ps[:, 7, 0:2 * NE].rearrange("p (t e) -> p t e", t=2),
                                    eR[:, :].unsqueeze(1).to_broadcast([P, 2, NE]), ALU.add).then_inc(d_rk, 1)
                    v.wait_ge(d_rk, B + 1)
                    v.tensor_tensor(prod[:, :, :, :], onehot[:, bass.ds(2 * b, 2), :, :],
                                    rk[:, :, :].unsqueeze(2).to_broadcast([P, 2, TOPK, NE]), ALU.mult).then_inc(d_r2, 1)
                    v.tensor_tensor(cumb[:, :], cumb[:, :], maskb[:, 0, :], ALU.add).then_inc(d_cum, 1)
                    v.wait_ge(d_r2, 2 * B + 1)
                    v.tensor_reduce(slotf[:, bass.ds(2 * b, 2), :], prod[:, :, :, :], X, ALU.add).then_inc(d_r2, 1)
                    v.wait_ge(d_cum, 2 * B + 1)
                    v.tensor_tensor(cumb[:, :], cumb[:, :], maskb[:, 1, :], ALU.add).then_inc(d_cum, 1)
                    apart(v, d_passed, (d_r2, 2 * B + 2), (D_sc, 64 * B))
                    v.tensor_copy(slot_now[:, :, :], slotf[:, bass.ds(2 * b, 2), :]).then_inc(d_slot, 1)

                if l == 1:
                    next_index(0, 0)
                    combine(0, 0, D_ga, 64)
                    v.wait_ge(d_comb, 2)
                ln1_stats(NB * l, 0, L_x[0] if l == 0 else None)
                if l == 0:
                    v.wait_ge(L_mask, 16)
                    v.tensor_scalar(mask_bc, mask_bc, NEG, None, ALU.mult).then_inc(C_v, 1)
                    v.wait_ge(C_v, 3)
                ln1_apply(NB * l, 0)
                v.wait_ge(C_a, 1)
                if l == 1:
                    v.wait_ge(L_small1, 80)
                v.tensor_scalar(bo[:, l, :], bo[:, l, :], tg[:, l:l + 1], None, ALU.mult).then_inc(C_bo, 1)
                if l == 0:
                    split_mask()

                def step(b, cur, nxt, nn, prev):
                    B = NB * l + b
                    U = 2 * B
                    if nn and l == 1:
                        next_index(b + 2, b + 2)
                    if cur:
                        divide(U)
                        totals(U + 1, 1)
                    if nxt:
                        shift(U + 2, 0)
                    if prev:
                        route1(B - 1, b - 1)
                    if cur:
                        residual(U, 2 * b, B, 0)
                    if nxt:
                        shift(U + 2, 1)
                    if cur:
                        ln2_apply(U, 2 * b, B, 0)
                    if prev:
                        route2(B - 1, b - 1)
                    if cur:
                        divide(U + 1)
                    if nn:
                        if l == 1:
                            combine(b + 2, b + 2, D_ga, 64 * (b + 3))
                            apart(v, d_passed, (d_comb, 2 * (b + 2) + 2))
                        if l == 0 and not cur:
                            v.wait_ge(L_x[1], 16)
                        if l == 0 and cur and not prev:
                            v.wait_ge(L_x[2], 16)
                            v.wait_ge(L_x[3], 16)
                        ln1_stats(B + 2, b + 2)
                    if nxt:
                        shift(U + 3, 0)
                    if nn:
                        ln1_apply(B + 2, b + 2)
                    if cur:
                        residual(U + 1, 2 * b + 1, B, 1)
                    if nxt:
                        totals(U + 2, 0)
                        shift(U + 3, 1)
                    if cur:
                        ln2_apply(U + 1, 2 * b + 1, B, 1)
                run_steps(v, l, step)

                bc = lambda t, n: t.unsqueeze(1).to_broadcast([P, n, NE])
                v.wait_ge(d_r1, 7 * NB * (l + 1))
                v.tensor_copy(zsum[:, :], top8[:, :, 0]).then_inc(d_tm, 1)
                v.wait_ge(f_cnt, l + 1)
                v.tensor_copy(cnt[:, :], ps[:, 7, 0:NE]).then_inc(d_f, 1)
                v.wait_ge(d_f, F + 1)
                v.tensor_tensor(pad_i[:, :], cnt[:, :], eR[:, :], ALU.add).then_inc(d_f, 1)
                c16 = cmpb[:, 0:NE * NT].rearrange("p (e t) -> p e t", e=NE)
                v.tensor_tensor(c16, cnt[:, :].unsqueeze(2).to_broadcast([P, NE, NT]),
                                thr[:, :].unsqueeze(1).to_broadcast([P, NE, NT]), ALU.is_gt).then_inc(d_f, 1)
                v.wait_ge(d_f, F + 3)
                v.tensor_reduce(nb[:, :], c16, X, ALU.add).then_inc(d_f, 1)
                v.wait_ge(d_f, F + 4)
                c8 = cmpb[:, 0:NE * NE].rearrange("p (e f) -> p e f", e=NE)
                v.tensor_tensor(c8, lower[:, :, :], bc(nb[:, :], NE), ALU.mult).then_inc(d_f, 1)
                v.wait_ge(d_f, F + 5)
                v.tensor_reduce(sbk[:, :], c8, X, ALU.add).then_inc(d_f, 1)
                v.wait_ge(d_f, F + 6)
                v.tensor_scalar(tot1[:, :], nb[:, NE - 1:NE], sbk[:, NE - 1:NE], -1.0, ALU.add, ALU.add).then_inc(d_f, 1)
                v.wait_ge(d_f, F + 7)
                v.tensor_scalar(jc[:, :], jrow[:, :], tot1[:, 0:1], None, ALU.min).then_inc(d_f, 1)
                v.wait_ge(d_f, F + 8)
                cj = cmpb[:, :].rearrange("p (j e) -> p j e", e=NE)
                v.tensor_tensor(cj, jc[:, :].unsqueeze(2).to_broadcast([P, MAX_BLOCKS, NE]),
                                bc(sbk[:, :], MAX_BLOCKS), ALU.is_ge).then_inc(d_f, 1)
                v.wait_ge(d_f, F + 9)
                v.tensor_reduce(be[:, :], cj, X, ALU.add).then_inc(d_f, 1)
                v.wait_ge(d_f, F + 10)
                v.tensor_tensor(cj, cj, bc(sbk[:, :], MAX_BLOCKS), ALU.mult).then_inc(d_f, 1)
                v.wait_ge(d_f, F + 11)
                v.tensor_reduce(sbx[:, :], cj, X, ALU.max).then_inc(d_f, 1)
                v.wait_ge(d_f, F + 12)
                v.tensor_tensor(jc[:, :], jc[:, :], sbx[:, :], ALU.subtract).then_inc(d_f, 1)
                v.wait_ge(d_f, F + 13)
                v.tensor_scalar(jc[:, :], jc[:, :], float(P), -float(REGION), ALU.mult, ALU.add).then_inc(d_f, 1)
                v.wait_ge(d_f, F + 14)
                v.scalar_tensor_tensor(out=xrow_i[:, :], in0=be[:, :], scalar=float(REGION), in1=jc[:, :],
                                       op0=ALU.mult, op1=ALU.add).then_inc(d_f, 1)
                v.tensor_scalar(woff_i[:, :], be[:, :], float(EW[l]), -float(EW[l]), ALU.mult, ALU.add).then_inc(d_f, 1)
                v.wait_ge(d_tm, l + 1)
                v.tensor_tensor(top8[:, :, :], top8[:, :, :], zsum[:, :].unsqueeze(2).to_broadcast([P, NT, 8]),
                                ALU.subtract).then_inc(d_f, 1)
                v.scalar_tensor_tensor(out=yoff[:, :], in0=sbk[:, :], scalar=float(P), in1=eR[:, :],
                                       op0=ALU.mult, op1=ALU.subtract).then_inc(d_f, 1)
                v.wait_ge(d_f, F + 18)
                c32 = cmpb[:, 0:NT * TOPK * NE].rearrange("p (n e) -> p n e", e=NE)
                v.tensor_tensor(c32, onehot[:, :, :, :].rearrange("p t k e -> p (t k) e"), bc(yoff[:, :], NT * TOPK),
                                ALU.mult).then_inc(d_f, 1)
                v.wait_ge(d_f, F + 19)
                v.tensor_reduce(yslot[:, :, :].rearrange("p t k -> p (t k)"), c32, X, ALU.add).then_inc(d_f, 1)
                v.wait_ge(d_f, F + 20)
                v.tensor_tensor(yslot[:, :, :], yslot[:, :, :], slotf[:, :, :], ALU.add).then_inc(d_f, 1)
                v.memset(cumb[:], 0.0).then_inc(d_f, 1)
                if l == 1:
                    v.wait_ge(d_f, F + 21)
                    v.tensor_copy(yslot_i[:, :, :], yslot[:, :, :]).then_inc(d_yi, 1)

                def blk(j, u, i, first, last):
                    J = MAX_BLOCKS * l + j
                    if first:
                        x_evac(J, j)
                    if l == 0:
                        for q in range(2):
                            v.wait_ge(e_act, 2 * j + q + 1)
                            v.wait_ge(b_up, 4 * j + 2 * q + 2)
                            need(v, b_hT, 2 * j)
                            v.tensor_tensor(h_sb[:, 344 * q:344 * q + 344], act_sb[:, 344 * q:344 * q + 344],
                                            ps[:, 2 * q + 1, 0:344], ALU.mult).then_inc(e_h, 1)
                    else:
                        v.wait_ge(e_act, 2 * MAX_BLOCKS + j + 1)
                        v.wait_ge(b_hT, 2 * MAX_BLOCKS + j)
                        v.tensor_tensor(h_sb[:, 0:HID[1]], act_sb[:, 0:HID[1]], act_sb[:, 0:HID[1]], ALU.mult).then_inc(e_h, 1)
                    if not last:
                        x_evac(J + 1, j + 1)
                    if not first:
                        y_evac(J - 1, (u - 1) % U3, i)
                    if l == 0:
                        v.wait_ge(b_hT, 2 * j + 2)
                        need(v, b_y, j)
                        v.tensor_copy(hT[:, 4, :], ps[:, 5, 0:P])
                        r = DOWN[0][5][1]
                        v.tensor_copy(hT[0:r, 5, :], ps[0:r, 5, P:2 * P]).then_inc(e_hTv, 1)
                    if last:
                        y_evac(J, u, i)

                def x_evac(J, j):
                    v.wait_ge(b_x, J + 1)
                    need(v, b_up, 4 * j if l == 0 else 4 * MAX_BLOCKS + j)
                    v.tensor_copy(xgT[:, :, :], ps[:, 7, 0:KT * P].rearrange("p (k n) -> p k n", k=KT)).then_inc(e_x, 1)

                def y_evac(J, u, i):
                    v.wait_ge(b_y, J + 1)
                    need(v, D_y[u], 16 * i + 16 * (MAX_BLOCKS // U3) * l)
                    v.tensor_copy(y_sb[:, u, :], ps[:, 6, 0:D]).then_inc(e_y, 1)

                v.wait_ge(f_exp, l + 1)
                e01 = top8[:, :, 0:TOPK]
                v.tensor_reduce(zsum[:, :], top8[:, :, :], X, ALU.add).then_inc(C_v, 1)
                v.tensor_tensor(wcomb[:, :, 0], top8[:, :, 0], top8[:, :, 1], ALU.add).then_inc(C_v, 1)
                v.wait_ge(C_v, 3 + 6 * l + 2)
                v.scalar_tensor_tensor(out=zsum[:, :], in0=zsum[:, :], scalar=1e-6 if l == 0 else 0.0, in1=wcomb[:, :, 0],
                                       op0=ALU.mult, op1=ALU.add).then_inc(C_v, 1)
                v.wait_ge(C_v, 3 + 6 * l + 3)
                v.reciprocal(zsum[:, :], zsum[:, :]).then_inc(C_v, 1)
                v.wait_ge(C_v, 3 + 6 * l + 4)
                v.tensor_scalar(zsum[:, :], zsum[:, :], tg[:, 2 + l:3 + l], None, ALU.mult).then_inc(C_v, 1)
                v.wait_ge(C_v, 3 + 6 * l + 5)
                v.tensor_tensor(wcomb[:, :, :], e01, zsum[:, :].unsqueeze(2).to_broadcast([P, NT, TOPK]), ALU.mult).then_inc(C_v, 1)
                v.wait_ge(C_v, 3 + 6 * l + 6)

                run_blocks(v, l, blk)

            for b in range(NB):
                combine(b + NB, b, D_gl[b], 64, b)

        @block.tensor
        def _(t):
            t.wait_ge(C_g, 14)

            for l in range(2):
                def ctx_t(B):
                    t.wait_ge(L_ctx, 16 * (B + 1))
                    for k in range(KT):
                        i = t.transpose(ps[:, 7, k * K:(k + 1) * K], ctx_sb[0:K, k * P:(k + 1) * P], ident[0:K, 0:K])
                    i.then_inc(p_ctx, 1)

                def k_proj(B):
                    t.wait_ge(a_ctx, B + 1)
                    need(t, d_o, 2 * B - 2)
                    for m in range(KT):
                        for k in range(KT):
                            i = t.matmul(ps[:, 7, m * K:(m + 1) * K], w_att[:, 1, k, m * P:(m + 1) * P], ctxT[:, k, :],
                                         start=(k == 0), stop=(k == KT - 1))
                    i.then_inc(p_k, 1)

                def x_t(B):
                    t.wait_ge(d_xn1, B + 1)
                    t.wait_ge(a_k, B + 1)
                    for k in range(KT):
                        for q in range(QT):
                            i = t.transpose(ps[:, 7, k * S + q * P:k * S + (q + 1) * P], xn1[:, q, k * P:(k + 1) * P], ident[:, :])
                    i.then_inc(p_xnT, 1)

                def q_proj(B):
                    t.wait_ge(a_xnT, B + 1)
                    for m in range(KT):
                        for k in range(KT):
                            i = t.matmul(ps[:, 7, m * S:(m + 1) * S], w_att[:, 0, k, m * P:(m + 1) * P], xn1T[:, k, :],
                                         start=(k == 0), stop=(k == KT - 1))
                    i.then_inc(p_q, 1)

                def v_proj(B):
                    for k in range(KT):
                        i = t.matmul(ps[0:K, 7, 0:D], ctxT[:, k, :], w_att[:, 2, k, :], start=(k == 0), stop=(k == KT - 1))
                    i.then_inc(p_v, 1)

                def score(b, U, qt, c):
                    h = c // 2
                    if c % 2 == 0:
                        need(t, d_sub, 2 * U + h - 1)
                    if l == 0:
                        t.matmul(ps[:, c, 0:CH].rearrange("p (h k) -> p h k", h=4), ones[0:96, :],
                                 mask3[0:96, bass.ds(b, 1), :].to_broadcast([96, 4, K]), start=True, stop=False)
                    i = t.matmul(ps[:, c, 0:CH], qT[:, h, qt * P:(qt + 1) * P],
                                 kbd[:, h, 4 * (c % 2):4 * (c % 2) + 4, :], start=(l == 1), stop=True)
                    if c % 2 == 1:
                        i.then_inc(p_s, 1)

                def probs_t(U, qt, c):
                    if c % 2 == 0:
                        t.wait_ge(a_exp, 2 * U + c // 2 + 1)
                    need(t, a_t, 4 * U + c - 1)
                    for h in range(4):
                        i = t.transpose(ps[0:K, 4 + c % 2, h * P:(h + 1) * P],
                                        p_buf[:, qt, (4 * c + h) * K:(4 * c + h + 1) * K], ident[:, :])
                    i.then_inc(p_t, 1)

                def values(U, B, c):
                    t.wait_ge(a_t, 4 * U + c + 1)
                    if c == 0:
                        t.wait_ge(g_vp, B + 1)
                        need(t, d_c, U)
                    for h4 in range(4):
                        h = 4 * c + h4
                        g4 = (h % HP) // 2
                        i = t.matmul(ps[32 * g4:32 * g4 + 32, 6, (h // HP) * P:(h // HP + 1) * P], v_pad[0:K, h, :],
                                     pT[0:K, c % 2, h4 * P:(h4 + 1) * P], start=(h % 2 == 0), stop=(h % 2 == 1))
                    i.then_inc(p_pv, 1)

                def rinv_t(U):
                    t.wait_ge(a_re, U + 1)
                    need(t, a_rt, U)
                    for k in range(KT):
                        i = t.transpose(ps[:, 6, (KT + k) * P:(KT + k + 1) * P],
                                        rinv16[:, k * HP:(k + 1) * HP, :].rearrange("p h d -> p (h d)"), ident[:, :])
                    i.then_inc(p_rt, 1)

                def out_proj(U):
                    t.wait_ge(d_c, U + 1)
                    for k in range(KT):
                        i = t.matmul(ps[:, 7, 0:D], cT[:, k, :], w_att[:, 3, k, :], start=(k == 0), stop=(k == KT - 1))
                    i.then_inc(p_o, 1)

                def x2_t(U, qt):
                    t.wait_ge(d_xn2, U + 1)
                    for k in range(KT):
                        i = t.transpose(ps[:, 7, k * P:(k + 1) * P], xn2[:, qt, k * P:(k + 1) * P], ident[:, :])
                    i.then_inc(p_x2, 1)

                def route(U):
                    t.wait_ge(a_x2, U + 1)
                    for k in range(KT):
                        i = t.matmul(ps[:, 7, 0:NE], xn2T[:, k, :], wr[:, l, k, :], start=(k == 0), stop=(k == KT - 1))
                    i.then_inc(p_lg, 1)

                def ranks(B):
                    t.wait_ge(d_mask, B + 1)
                    need(t, d_cum, 2 * B)
                    t.matmul(ps[:, 7, 0:NE], tri[:, :], maskb[:, 0, :], start=True, stop=False)
                    t.matmul(ps[:, 7, 0:NE], ones[:, :], cumb[:, :], start=False, stop=True)
                    t.matmul(ps[:, 7, NE:2 * NE], tri[:, :], maskb[:, 1, :], start=True, stop=False)
                    t.matmul(ps[:, 7, NE:2 * NE], ones[:, :], maskb[:, 0, :], start=False, stop=False)
                    t.matmul(ps[:, 7, NE:2 * NE], ones[:, :], cumb[:, :], start=False, stop=True).then_inc(p_rk, 1)

                if l == 1:
                    t.wait_ge(e_x, MAX_BLOCKS)
                    t.wait_ge(e_y, MAX_BLOCKS)
                t.wait_ge(L_w, 64 * (l + 1))
                t.wait_ge(*((L_vr, 32) if l == 0 else (L_small1, 80)))
                ctx_t(NB * l)

                def step(b, cur, nxt, nn, prev):
                    B = NB * l + b
                    U = 2 * B
                    if cur:
                        probs_t(U, 0, 0)
                        probs_t(U, 0, 1)
                        values(U, B, 0)
                    if nxt:
                        k_proj(B + 1)
                    if nxt and not cur:
                        t.wait_ge(a_k, B + 2)
                        v_proj(B + 1)
                        t.wait_ge(a_v, B + 2)
                        ctx_t(B + 2)
                        t.wait_ge(a_ctx, B + 3)
                    if cur:
                        probs_t(U, 0, 2)
                        values(U, B, 1)
                    if nxt:
                        x_t(B + 1)
                    if cur:
                        probs_t(U, 0, 3)
                        values(U, B, 2)
                    if nxt:
                        q_proj(B + 1)
                    if cur:
                        values(U, B, 3)
                        rinv_t(U)
                    if cur and not nxt:
                        probs_t(U + 1, 1, 0)
                        probs_t(U + 1, 1, 1)
                        x2_t(U - 1, 1)
                        values(U + 1, B, 0)
                        probs_t(U + 1, 1, 2)
                        route(U - 1)
                        values(U + 1, B, 1)
                        t.wait_ge(a_lg, U)
                        out_proj(U)
                        probs_t(U + 1, 1, 3)
                        values(U + 1, B, 2)
                        t.wait_ge(d_o, U + 1)
                        ranks(B - 1)
                        values(U + 1, B, 3)
                        rinv_t(U + 1)
                        t.wait_ge(d_rk, B)
                        x2_t(U, 0)
                        t.wait_ge(a_x2, U + 1)
                        out_proj(U + 1)
                        t.wait_ge(d_o, U + 2)
                        route(U)
                        return
                    if nxt:
                        t.wait_ge(a_q, B + 2)
                    if prev:
                        if not cur:
                            t.wait_ge(a_lg, U - 1)
                        x2_t(U - 1, 1)
                    if nxt:
                        t.wait_ge(g_kbd, B + 2)
                        if l == 0 and not cur:
                            t.wait_ge(d_m, 9)
                        score(b + 1, U + 2, 0, 0)
                    if prev:
                        route(U - 1)
                    if nxt:
                        score(b + 1, U + 2, 0, 1)
                    if prev:
                        t.wait_ge(a_lg, U)
                    if nxt and cur:
                        v_proj(B + 1)
                    if nxt:
                        score(b + 1, U + 2, 0, 2)
                        score(b + 1, U + 2, 0, 3)
                        t.wait_ge(a_v, B + 2)
                    if cur:
                        out_proj(U)
                        probs_t(U + 1, 1, 0)
                        probs_t(U + 1, 1, 1)
                        values(U + 1, B, 0)
                        probs_t(U + 1, 1, 2)
                        t.wait_ge(d_o, U + 1)
                    if nn and cur:
                        ctx_t(B + 2)
                    if cur:
                        values(U + 1, B, 1)
                        probs_t(U + 1, 1, 3)
                        values(U + 1, B, 2)
                    if nn:
                        t.wait_ge(a_ctx, B + 3)
                    if prev:
                        ranks(B - 1)
                    if cur:
                        values(U + 1, B, 3)
                        rinv_t(U + 1)
                    if nxt:
                        score(b + 1, U + 3, 1, 0)
                        score(b + 1, U + 3, 1, 1)
                    if cur:
                        if prev:
                            t.wait_ge(d_rk, B)
                        x2_t(U, 0)
                    if nxt:
                        score(b + 1, U + 3, 1, 2)
                    if cur:
                        route(U)
                    if nxt:
                        score(b + 1, U + 3, 1, 3)
                    if cur:
                        t.wait_ge(a_lg, U + 1)
                        out_proj(U + 1)
                run_steps(t, l, step)

                t.wait_ge(d_cum, 2 * NB * (l + 1))
                t.wait_ge(d_rk, NB * (l + 1))
                t.matmul(ps[:, 7, 0:NE], ones[:, :], cumb[:, :], start=True, stop=True).then_inc(f_cnt, 1)
                t.wait_ge(d_f, 16 + 22 * l)
                t.wait_ge(L_exp, 16 * (4 * NE if l == 0 else 4 * NE + 2 * NE))

                def block_t(j, u, i):
                    J = MAX_BLOCKS * l + j
                    t.wait_ge(L_xg[u], 16 * i + (16 + 16 * (MAX_BLOCKS // U3) * l))
                    need(t, e_x, J)
                    for k in range(KT):
                        i = t.transpose(ps[:, 7, k * P:(k + 1) * P], xg[:, u, k * P:(k + 1) * P], ident[:, :])
                    i.then_inc(b_x, 1)

                def up(j, off):
                    J = MAX_BLOCKS * l + j
                    t.wait_ge(e_x, J + 1)
                    for n, (bank, col, w) in enumerate(UP[l]):
                        if l == 0:
                            need(t, e_h, 2 * j - 1 + n // 2) if n % 2 else need(t, e_act, 2 * j - 1 + n // 2)
                        else:
                            t.wait_ge(e_act, 2 * MAX_BLOCKS + j)
                        for k in range(KT):
                            i = t.matmul(ps[:, bank, 0:w], xgT[:, k, :], w_all[:, bass.ds(off + (k * UPW[l] + col), w)],
                                         start=(k == 0), stop=(k == KT - 1))
                        i.then_inc(b_up, 1)

                def h_t(j):
                    if l == 0:
                        t.wait_ge(e_h, 2 * j + 2)
                        need(t, e_hT, j)
                    else:
                        t.wait_ge(e_h, 2 * MAX_BLOCKS + j + 1)
                        t.wait_ge(e_hT, MAX_BLOCKS + j)
                    for c, r in DOWN[l]:
                        if c == 4:
                            i.then_inc(b_hT, 1)
                            need(t, e_hTv, j)
                        i = t.transpose(ps[0:r, 4 + c // 4, (c % 4) * P:(c % 4 + 1) * P], h_sb[:, c * P:c * P + r], ident[:, :])
                    i.then_inc(b_hT, 1)

                def down(j, off):
                    J = MAX_BLOCKS * l + j
                    t.wait_ge(e_hT, J + 1)
                    if l == 0:
                        t.wait_ge(e_hTv, j + 1)
                    need(t, e_y, J)
                    for c, r in DOWN[l]:
                        i = t.matmul(ps[:, 6, 0:D], hT[0:r, c, :], w_all[0:r, bass.ds(off + (KT * UPW[l] + c * D), D)],
                                     start=(c == 0), stop=(c == KD[l] - 1))
                    i.then_inc(b_y, 1)

                block_t(0, 0, 0)

                def weights(j):
                    return t.value_load(woff_i[0:1, bass.ds(j, 1)], min_val=0, max_val=(NE - 1) * EW[l])

                off, off_before = None, None

                def blk(j, u, i, first, last):
                    nonlocal off, off_before
                    off_before = off
                    off = weights(j)
                    if not first:
                        h_t(j - 1)
                    up(j, off)
                    if u == 1:
                        off_before = weights(j - 1)
                    if not last:
                        block_t(j + 1, (u + 1) % U3, i if u == 1 else i + 1)
                    if not first:
                        down(j - 1, off_before)
                    if last:
                        h_t(j)
                        down(j, off)
                run_blocks(t, l, blk)


def kernel(**inputs):
    import numpy as np
    import concourse.bacc as bacc
    from concourse.bass_utils import run_bass_kernel_spmd

    nc = bacc.Bacc("TRN2", target_bir_lowering=False, num_devices=1)
    arrays = {}

    def dram(name, a):
        a = np.ascontiguousarray(a)
        arrays[name] = a
        return nc.dram_tensor(name, a.shape, mybir.dt.from_np(a.dtype), kind="ExternalInput").ap()

    I = {k: np.asarray(v) for k, v in inputs.items()}
    attn_w, attn_b, router_w, experts = [], [], [], []
    for l in range(2):
        ws = [I[f"L{l}_xattn_W{c}"] for c in "qkvo"]
        attn_w.append([dram(f"w{c}{l}", w.T if l else w) for c, w in zip("qkvo", ws)])
        bs = [I[f"L{l}_xattn_b{c}"] for c in "qkvo"]
        attn_b.append([dram(f"b{c}{l}", b.reshape(2, 128).T if c in "qk" else b) for c, b in zip("qkvo", bs)])
    router_w = [dram("router0", I["L0_ffn_router_w"]), dram("router1", I["L1_ffn_router_w"].T)]
    experts = [[dram("gate0", I["L0_ffn_w_gate"]), dram("up0", I["L0_ffn_w_up"]), dram("down0", I["L0_ffn_w_down"])],
               [dram("w1", I["L1_ffn_w1_all"]), dram("w2", I["L1_ffn_w2_all"])]]
    x = dram("x", I["x"])
    ctx_rows = dram("ctx", I["ctx_1024"])
    mask = dram("mask", I["mask_Bx1x1xS2_ff0"].reshape(8, 120))
    out = nc.dram_tensor("out", x.shape, F32, kind="ExternalOutput").ap()
    flamingo_kernel(nc, x, ctx_rows, mask, dram("g_xattn", I["g_xattn"]), dram("g_ffn", I["g_ffn"]),
                    attn_w, attn_b, router_w, experts, out)
    r = run_bass_kernel_spmd(nc, [arrays], core_ids=[0])
    return r.results[0]["out"]
```
